# Optimizing a Trainium2 kernel written in Bass

```python
import numpy as np
import jax
import jax.numpy as jnp

def _softmax(x, axis=-1):
    return jax.nn.softmax(x, axis=axis)

def _gelu(x):
    return jax.nn.gelu(x, approximate=True)

def _silu(x):
    return jax.nn.silu(x)

def _sigmoid(x):
    return jax.nn.sigmoid(x)

def _layernorm(x, axis=-1, eps=1e-05):
    m = jnp.mean(x, axis=axis, keepdims=True)
    v = jnp.var(x, axis=axis, keepdims=True)
    return (x - m) / jnp.sqrt(v + eps)

def _scatter_add(tgt, idx, src, axis=0):
    return tgt.at[idx].add(src)

def _segment_sum(src, seg, n):
    return jax.ops.segment_sum(src, seg, n)
kernel_name = 'mk_macaron_d2_jaxref_r8_a94db4'

def setup_inputs(seed: int=0):
    np.random.seed(seed)
    _w = jnp.asarray

    def _L0_attn_setup():
        import jax, jax.numpy as jnp
        import numpy as np
        D = 128
        H = 16
        HD = D // H
        SCALE = HD ** (-0.5)
        WIN = 32
        CBS = 32
        CSTRIDE = 32
        SBS = 64
        TOPK = 16
        B, S = (4, 256)

        def _sliding_attn(q, k, v):
            Sq, Kv = (q.shape[1], k.shape[1])
            scores = jnp.einsum('bqd,bkd->bqk', q, k) * SCALE
            i = jnp.arange(Sq)[:, None]
            j = jnp.arange(Kv)[None, :]
            mask = (j >= i - WIN) & (j < jnp.minimum(Sq, i + WIN + 1))
            scores = jnp.where(mask, scores, -1e+30)
            probs = jax.nn.softmax(scores, axis=-1)
            out = jnp.einsum('bqk,bkd->bqd', probs, v)
            return jnp.where(mask.any(-1)[None, :, None], out, 0.0)

        def _compress(t, w, b):
            Bt, St, Dt = t.shape
            nb = (St - CBS) // CSTRIDE + 1
            idx = jnp.arange(nb)[:, None] * CSTRIDE + jnp.arange(CBS)[None, :]
            blocks = t[:, idx, :].reshape(Bt, nb, CBS * Dt)
            return blocks @ w.T + b

        def _select(t, w, b):
            Bt, St, Dt = t.shape
            scores = (t @ w.T + b)[..., 0]
            nsb = St // SBS
            bscores = scores.reshape(Bt, nsb, SBS)
            _, tidx = jax.lax.top_k(bscores, TOPK)
            idx = (tidx + jnp.arange(nsb)[None, :, None] * SBS).reshape(Bt, nsb * TOPK)
            return jnp.take_along_axis(t, idx[..., None], axis=1)
        key = jax.random.key(seed)
        ks = jax.random.split(key, 8)
        init = lambda k, shape: jax.random.normal(k, shape, jnp.float32) * 0.02
        return {'x': jax.random.normal(ks[0], (B, S, D), jnp.float32), 'w_qkv': init(ks[1], (3 * D, D)), 'b_qkv': jnp.zeros((3 * D,), jnp.float32), 'w_comp': init(ks[2], (D, D * CBS)), 'b_comp': jnp.zeros((D,), jnp.float32), 'w_score': init(ks[3], (1, D)), 'b_score': jnp.zeros((1,), jnp.float32), 'w_gate': init(ks[4], (3, D)), 'b_gate': jnp.zeros((3,), jnp.float32), 'w_o': init(ks[5], (D, D)), 'b_o': jnp.zeros((D,), jnp.float32)}
    _L0_attn_in = _L0_attn_setup()

    def _L0_ffn_setup():
        import jax, jax.numpy as jnp
        import numpy as np
        IN_DIM, OUT_DIM, N_PROTO, RANK = (128, 128, 32, 16)
        key = jax.random.key(seed)
        ks = jax.random.split(key, 5)
        x = jax.random.normal(ks[0], (2, 512, IN_DIM), dtype=jnp.float32)
        prototypes = jax.random.normal(ks[1], (N_PROTO, IN_DIM), dtype=jnp.float32) * 0.02
        B = jax.random.normal(ks[2], (N_PROTO, RANK, IN_DIM), dtype=jnp.float32) * 0.02
        A = jax.random.normal(ks[3], (N_PROTO, OUT_DIM, RANK), dtype=jnp.float32) * 0.02
        bias = jnp.zeros((N_PROTO, OUT_DIM), dtype=jnp.float32)
        temp = jnp.asarray(1.0, dtype=jnp.float32)
        return {'x': x, 'prototypes': prototypes, 'B': B, 'A': A, 'bias': bias, 'temp': temp}
    _L0_ffn_in = _L0_ffn_setup()

    def _L1_attn_setup():
        import jax, jax.numpy as jnp
        import numpy as np
        import math
        D_MODEL, N_HEADS, D_K, D_C, D_HR = (128, 8, 128, 32, 32)
        B, S = (4, 256)
        key = jax.random.key(seed)
        ks = jax.random.split(key, 17)

        def lin(k, fan_in, fan_out):
            lim = 1.0 / math.sqrt(fan_in)
            kw, kb = jax.random.split(k)
            W = jax.random.uniform(kw, (fan_in, fan_out), jnp.float32, -lim, lim)
            b = jax.random.uniform(kb, (fan_out,), jnp.float32, -lim, lim)
            return (W, b)
        W_DQ, b_DQ = lin(ks[0], D_MODEL, D_C)
        W_UQ, b_UQ = lin(ks[1], D_C, N_HEADS * D_K)
        W_DKV, b_DKV = lin(ks[2], D_MODEL, D_C)
        W_UK, b_UK = lin(ks[3], D_C, N_HEADS * D_K)
        W_UV, b_UV = lin(ks[4], D_C, N_HEADS * D_K)
        W_QR, b_QR = lin(ks[5], D_C, N_HEADS * D_HR)
        W_KR, b_KR = lin(ks[6], D_MODEL, D_HR)
        W_O, b_O = lin(ks[7], N_HEADS * D_K, D_MODEL)
        h_t = jax.random.normal(ks[8], (B, S, D_MODEL), jnp.float32)
        return {'h_t': h_t, 'W_DQ': W_DQ, 'b_DQ': b_DQ, 'W_UQ': W_UQ, 'b_UQ': b_UQ, 'W_DKV': W_DKV, 'b_DKV': b_DKV, 'W_UK': W_UK, 'b_UK': b_UK, 'W_UV': W_UV, 'b_UV': b_UV, 'W_QR': W_QR, 'b_QR': b_QR, 'W_KR': W_KR, 'b_KR': b_KR, 'W_O': W_O, 'b_O': b_O}
    _L1_attn_in = _L1_attn_setup()

    def _L1_ffn_setup():
        import jax, jax.numpy as jnp
        import numpy as np
        B, T, D, E, F, K = (8, 256, 128, 8, 512, 2)
        key = jax.random.key(seed)
        ks = jax.random.split(key, 5)
        s = 1.0 / np.sqrt(D)
        return {'tokens': jax.random.normal(ks[0], (B, T, D), jnp.float32), 'gate_w': jax.random.normal(ks[1], (E, D), jnp.float32) * s, 'gate_b': jnp.zeros((E,), jnp.float32), 'w1': jax.random.normal(ks[2], (E, F, D), jnp.float32) * s, 'b1': jnp.zeros((E, F), jnp.float32), 'w2': jax.random.normal(ks[3], (E, D, F), jnp.float32) * (1.0 / np.sqrt(F)), 'b2': jnp.zeros((E, D), jnp.float32)}
    _L1_ffn_in = _L1_ffn_setup()
    _d = {'L0_attn_x': _L0_attn_in['x'], 'L0_attn_w_qkv': _L0_attn_in['w_qkv'], 'L0_attn_b_qkv': _L0_attn_in['b_qkv'], 'L0_attn_w_comp': _L0_attn_in['w_comp'], 'L0_attn_b_comp': _L0_attn_in['b_comp'], 'L0_attn_w_score': _L0_attn_in['w_score'], 'L0_attn_b_score': _L0_attn_in['b_score'], 'L0_attn_w_gate': _L0_attn_in['w_gate'], 'L0_attn_b_gate': _L0_attn_in['b_gate'], 'L0_attn_w_o': _L0_attn_in['w_o'], 'L0_attn_b_o': _L0_attn_in['b_o'], 'L0_ffn_prototypes': _L0_ffn_in['prototypes'], 'L0_ffn_B': _L0_ffn_in['B'], 'L0_ffn_A': _L0_ffn_in['A'], 'L0_ffn_bias': _L0_ffn_in['bias'], 'L0_ffn_temp': _L0_ffn_in['temp'], 'L1_attn_W_DQ': _L1_attn_in['W_DQ'], 'L1_attn_b_DQ': _L1_attn_in['b_DQ'], 'L1_attn_W_UQ': _L1_attn_in['W_UQ'], 'L1_attn_b_UQ': _L1_attn_in['b_UQ'], 'L1_attn_W_DKV': _L1_attn_in['W_DKV'], 'L1_attn_b_DKV': _L1_attn_in['b_DKV'], 'L1_attn_W_UK': _L1_attn_in['W_UK'], 'L1_attn_b_UK': _L1_attn_in['b_UK'], 'L1_attn_W_UV': _L1_attn_in['W_UV'], 'L1_attn_b_UV': _L1_attn_in['b_UV'], 'L1_attn_W_QR': _L1_attn_in['W_QR'], 'L1_attn_b_QR': _L1_attn_in['b_QR'], 'L1_attn_W_KR': _L1_attn_in['W_KR'], 'L1_attn_b_KR': _L1_attn_in['b_KR'], 'L1_attn_W_O': _L1_attn_in['W_O'], 'L1_attn_b_O': _L1_attn_in['b_O'], 'L1_ffn_gate_w': _L1_ffn_in['gate_w'], 'L1_ffn_gate_b': _L1_ffn_in['gate_b'], 'L1_ffn_w1': _L1_ffn_in['w1'], 'L1_ffn_b1': _L1_ffn_in['b1'], 'L1_ffn_w2': _L1_ffn_in['w2'], 'L1_ffn_b2': _L1_ffn_in['b2']}
    _x0 = _d['L0_attn_x']
    _d['L0_attn_x'] = jax.random.normal(jax.random.fold_in(jax.random.key(seed), 1), (8, 512, 128), dtype=_x0.dtype)
    del _x0
    return _d

def reference(L0_attn_x, L0_attn_w_qkv, L0_attn_b_qkv, L0_attn_w_comp, L0_attn_b_comp, L0_attn_w_score, L0_attn_b_score, L0_attn_w_gate, L0_attn_b_gate, L0_attn_w_o, L0_attn_b_o, L0_ffn_prototypes, L0_ffn_B, L0_ffn_A, L0_ffn_bias, L0_ffn_temp, L1_attn_W_DQ, L1_attn_b_DQ, L1_attn_W_UQ, L1_attn_b_UQ, L1_attn_W_DKV, L1_attn_b_DKV, L1_attn_W_UK, L1_attn_b_UK, L1_attn_W_UV, L1_attn_b_UV, L1_attn_W_QR, L1_attn_b_QR, L1_attn_W_KR, L1_attn_b_KR, L1_attn_W_O, L1_attn_b_O, L1_ffn_gate_w, L1_ffn_gate_b, L1_ffn_w1, L1_ffn_b1, L1_ffn_w2, L1_ffn_b2):

    def _L0_attn_ref(x, w_qkv, b_qkv, w_comp, b_comp, w_score, b_score, w_gate, b_gate, w_o, b_o):
        import jax, jax.numpy as jnp
        import numpy as np
        D = 128
        H = 16
        HD = D // H
        SCALE = HD ** (-0.5)
        WIN = 32
        CBS = 32
        CSTRIDE = 32
        SBS = 64
        TOPK = 16
        B, S = (4, 256)

        def _sliding_attn(q, k, v):
            Sq, Kv = (q.shape[1], k.shape[1])
            scores = jnp.einsum('bqd,bkd->bqk', q, k) * SCALE
            i = jnp.arange(Sq)[:, None]
            j = jnp.arange(Kv)[None, :]
            mask = (j >= i - WIN) & (j < jnp.minimum(Sq, i + WIN + 1))
            scores = jnp.where(mask, scores, -1e+30)
            probs = jax.nn.softmax(scores, axis=-1)
            out = jnp.einsum('bqk,bkd->bqd', probs, v)
            return jnp.where(mask.any(-1)[None, :, None], out, 0.0)

        def _compress(t, w, b):
            Bt, St, Dt = t.shape
            nb = (St - CBS) // CSTRIDE + 1
            idx = jnp.arange(nb)[:, None] * CSTRIDE + jnp.arange(CBS)[None, :]
            blocks = t[:, idx, :].reshape(Bt, nb, CBS * Dt)
            return blocks @ w.T + b

        def _select(t, w, b):
            Bt, St, Dt = t.shape
            scores = (t @ w.T + b)[..., 0]
            nsb = St // SBS
            bscores = scores.reshape(Bt, nsb, SBS)
            _, tidx = jax.lax.top_k(bscores, TOPK)
            idx = (tidx + jnp.arange(nsb)[None, :, None] * SBS).reshape(Bt, nsb * TOPK)
            return jnp.take_along_axis(t, idx[..., None], axis=1)
        Bx, Sx, _ = x.shape
        qkv = (x @ w_qkv.T + b_qkv).reshape(Bx, Sx, H, 3, HD)
        q = qkv[..., 0, :].reshape(Bx, Sx, D)
        k = qkv[..., 1, :].reshape(Bx, Sx, D)
        v = qkv[..., 2, :].reshape(Bx, Sx, D)
        ck = _compress(k, w_comp, b_comp)
        cv = _compress(v, w_comp, b_comp)
        sk = _select(k, w_score, b_score)
        sv = _select(v, w_score, b_score)
        o_comp = _sliding_attn(q, ck, cv)
        o_sel = _sliding_attn(q, sk, sv)
        o_win = _sliding_attn(q, k, v)
        gates = jax.nn.sigmoid(x @ w_gate.T + b_gate)
        combined = gates[..., 0:1] * o_comp + gates[..., 1:2] * o_sel + gates[..., 2:3] * o_win
        return combined @ w_o.T + b_o

    def _L0_ffn_ref(x, prototypes, B, A, bias, temp):
        import jax, jax.numpy as jnp
        import numpy as np
        IN_DIM, OUT_DIM, N_PROTO, RANK = (128, 128, 32, 16)
        lead = x.shape[:-1]
        xf = x.reshape(-1, IN_DIM)
        x2 = jnp.sum(xf * xf, axis=1, keepdims=True)
        p2 = jnp.sum(prototypes * prototypes, axis=1)
        d2 = x2 + p2[None, :] - 2.0 * (xf @ prototypes.T)
        dists = jnp.sqrt(jnp.maximum(d2, 0.0))
        t = jnp.maximum(jnp.abs(temp), 0.1)
        w = jax.nn.softmax(-dists / t, axis=1)
        topw, topi = jax.lax.top_k(w, 2)
        topw = topw / jnp.sum(topw, axis=1, keepdims=True)
        out = jnp.zeros((xf.shape[0], OUT_DIM), dtype=xf.dtype)
        for tslot in range(2):
            idx = topi[:, tslot]
            wt = topw[:, tslot:tslot + 1]
            h = jnp.einsum('nri,ni->nr', B[idx], xf)
            y = jnp.einsum('nor,nr->no', A[idx], h) + bias[idx]
            out = out + wt * y
        return out.reshape(*lead, OUT_DIM)

    def _L1_attn_ref(h_t, W_DQ, b_DQ, W_UQ, b_UQ, W_DKV, b_DKV, W_UK, b_UK, W_UV, b_UV, W_QR, b_QR, W_KR, b_KR, W_O, b_O):
        import jax, jax.numpy as jnp
        import numpy as np
        import math
        D_MODEL, N_HEADS, D_K, D_C, D_HR = (128, 8, 128, 32, 32)
        B, S = (4, 256)
        b, s, _ = h_t.shape
        c_q = h_t @ W_DQ + b_DQ
        c_kv = h_t @ W_DKV + b_DKV
        q_c = (c_q @ W_UQ + b_UQ).reshape(b, s, N_HEADS, D_K).transpose(0, 2, 1, 3)
        k_c = (c_kv @ W_UK + b_UK).reshape(b, s, N_HEADS, D_K).transpose(0, 2, 1, 3)
        v_c = (c_kv @ W_UV + b_UV).reshape(b, s, N_HEADS, D_K).transpose(0, 2, 1, 3)
        q_r = (c_q @ W_QR + b_QR).reshape(b, s, N_HEADS, D_HR).transpose(0, 2, 1, 3)
        k_r = (h_t @ W_KR + b_KR)[:, None, :, :]
        k_r = jnp.broadcast_to(k_r, (b, N_HEADS, s, D_HR))
        q = jnp.concatenate([q_c, q_r], axis=-1)
        k = jnp.concatenate([k_c, k_r], axis=-1)
        scale = 1.0 / math.sqrt(D_K + D_HR)
        scores = jnp.einsum('bhsd,bhtd->bhst', q, k) * scale
        attn = jax.nn.softmax(scores, axis=-1)
        o = jnp.einsum('bhst,bhtd->bhsd', attn, v_c)
        o = o.transpose(0, 2, 1, 3).reshape(b, s, N_HEADS * D_K)
        return o @ W_O + b_O

    def _L1_ffn_ref(tokens, gate_w, gate_b, w1, b1, w2, b2):
        import jax, jax.numpy as jnp
        import numpy as np
        B, T, D, E, F, K = (8, 256, 128, 8, 512, 2)
        logits = jnp.einsum('btd,ed->bte', tokens, gate_w) + gate_b
        weights, expert_ixs = jax.lax.top_k(logits, K)
        weights = jax.nn.softmax(weights, axis=1)
        onehot = jax.nn.one_hot(expert_ixs, E, dtype=weights.dtype)
        gate_per_expert = jnp.einsum('btk,btke->bte', weights, onehot)
        results = jnp.zeros_like(tokens)
        for e in range(E):
            h = jax.nn.relu(jnp.einsum('btd,fd->btf', tokens, w1[e]) + b1[e])
            y = jnp.einsum('btf,df->btd', h, w2[e]) + b2[e]
            results = results + gate_per_expert[..., e:e + 1] * y
        return results
    x = L0_attn_x
    x = x + 0.5 * _L0_ffn_ref(_layernorm(x, axis=-1), L0_ffn_prototypes, L0_ffn_B, L0_ffn_A, L0_ffn_bias, L0_ffn_temp)
    x = x + _L0_attn_ref(_layernorm(x, axis=-1), L0_attn_w_qkv, L0_attn_b_qkv, L0_attn_w_comp, L0_attn_b_comp, L0_attn_w_score, L0_attn_b_score, L0_attn_w_gate, L0_attn_b_gate, L0_attn_w_o, L0_attn_b_o)
    x = x + 0.5 * _L0_ffn_ref(_layernorm(x, axis=-1), L0_ffn_prototypes, L0_ffn_B, L0_ffn_A, L0_ffn_bias, L0_ffn_temp)
    x = x + 0.5 * _L1_ffn_ref(_layernorm(x, axis=-1), L1_ffn_gate_w, L1_ffn_gate_b, L1_ffn_w1, L1_ffn_b1, L1_ffn_w2, L1_ffn_b2)
    x = x + _L1_attn_ref(_layernorm(x, axis=-1), L1_attn_W_DQ, L1_attn_b_DQ, L1_attn_W_UQ, L1_attn_b_UQ, L1_attn_W_DKV, L1_attn_b_DKV, L1_attn_W_UK, L1_attn_b_UK, L1_attn_W_UV, L1_attn_b_UV, L1_attn_W_QR, L1_attn_b_QR, L1_attn_W_KR, L1_attn_b_KR, L1_attn_W_O, L1_attn_b_O)
    x = x + 0.5 * _L1_ffn_ref(_layernorm(x, axis=-1), L1_ffn_gate_w, L1_ffn_gate_b, L1_ffn_w1, L1_ffn_b1, L1_ffn_w2, L1_ffn_b2)
    return x

_drawn_inputs = setup_inputs


def setup_inputs(seed=0):
    import zlib

    import numpy as np

    out = dict(_drawn_inputs(seed))
    spreads = {'L0_attn_b_qkv': (0.0, 0.492),
     'L0_attn_b_comp': (0.0, 0.8),
     'L0_attn_b_gate': (0.0, 0.8),
     'L0_attn_b_o': (0.0, 0.1),
     'L0_ffn_bias': (0.0, 0.1),
     'L1_ffn_gate_b': (0.0, 0.8),
     'L1_ffn_b1': (0.0, 0.8),
     'L1_ffn_b2': (0.0, 2.0)}
    factors = {'L0_attn_w_qkv': 8.0,
     'L0_attn_w_comp': 8.0,
     'L0_attn_w_score': 8.0,
     'L0_attn_w_gate': 8.0,
     'L0_attn_w_o': 3.22,
     'L0_ffn_B': 4.46,
     'L0_ffn_A': 4.436,
     'L1_attn_W_DQ': 8.0,
     'L1_attn_b_DQ': 8.0,
     'L1_attn_W_UQ': 8.0,
     'L1_attn_b_UQ': 8.0,
     'L1_attn_b_DKV': 4.258,
     'L1_attn_W_UK': 8.0,
     'L1_attn_b_UK': 64.0,
     'L1_attn_W_QR': 8.0,
     'L1_attn_b_QR': 8.0,
     'L1_attn_W_KR': 8.0,
     'L1_attn_b_KR': 64.0,
     'L1_attn_b_O': 3.009,
     'L1_ffn_gate_w': 8.0,
     'L1_ffn_w1': 8.0,
     'L1_ffn_w2': 8.0}
    for name, (base, spread) in spreads.items():
        noise = np.random.default_rng([zlib.crc32(name.encode()), seed]).standard_normal(out[name].shape)
        drawn = base * np.exp(spread * noise) if base else spread * noise
        out[name] = jnp.asarray(drawn.astype(out[name].dtype))
    for name, factor in factors.items():
        out[name] = (out[name] * factor).astype(out[name].dtype)
    return out
```

```python
import concourse.bass as bass
from concourse import mybir
from contextlib import ExitStack
import numpy as np

F32 = mybir.dt.float32
U32 = mybir.dt.uint32
ALU = mybir.AluOpType
ACT = mybir.ActivationFunctionType
X = mybir.AxisListType.X

P = 128
NB, S, D = 8, 512, 128
T = S // P
EPS = 1e-5
NPROTO, RANK = 32, 16
PR = NPROTO * RANK // P
TINY = 2.0 ** -60
H0, HD0 = 16, 8
SCALE0 = HD0 ** -0.5
WIN = 32
CBS = 32
NCMP = S // CBS
SBS, TOPK = 64, 16
NSEL = S // SBS * TOPK
WK = P + 2 * WIN
PAD = WIN + S + (P - WIN)
SELT, CMPT = 2, 1
NSEG = T + SELT + CMPT
OSEL = T * WK
OCMP = OSEL + SELT * NSEL
NSC = OCMP + NCMP
NEG = -1e30
LOWEST = -3.4028234663852886e38
H1, DK, DC, DR = 8, 128, 32, 32
SCALE1 = (DK + DR) ** -0.5
KQ = DC + 1
KK = DC + DR + 1
E, F = 8, 512
FC = F // P

C_ID, C_MASK = 0, P
C_IOTA = C_MASK + NSC
C_PCOL = C_IOTA + NPROTO
C_VALID = C_PCOL + 1
C_DELTA = C_VALID + NSEG
C_HALF = C_DELTA + 2 * T * 2 * TOPK
C_ONES = C_HALF + 2 * TOPK
NCONST = C_ONES + P
DELTA_W = 2 * TOPK

ROWS = [("bv", D), ("bg", 3), ("bo", D), ("gb", E), ("bdkv", DC), ("bO", D), ("bs", 1), ("temp", 1)]
ROW_AT = {}
_at = 0
for _name, _n in ROWS:
    ROW_AT[_name] = _at
    _at += _n
NROWS = _at

COLS = [("bq", 1), ("bk", 1), ("bvc", 1), ("bcomp", 1), ("b1", E * FC), ("buv", H1), ("bkr", 1), ("bdq", 1), ("ws", 1)]
COL_AT = {}
_at = 0
for _name, _n in COLS:
    COL_AT[_name] = _at
    _at += _n
NCOLS = _at


def constants():
    c = np.zeros((P, NCONST), np.float32)
    c[:, C_ID:C_ID + P] = np.eye(P)
    mask = np.full((P, NSC), NEG, np.float32)
    for t in range(T):
        for p in range(P):
            i = t * P + p
            for w in range(WK):
                j = t * P - WIN + w
                if 0 <= j < S and i - WIN <= j < min(S, i + WIN + 1):
                    mask[p, t * WK + w] = 0
            if t < SELT:
                for j in range(NSEL):
                    if i - WIN <= j < min(S, i + WIN + 1):
                        mask[p, OSEL + t * NSEL + j] = 0
            if t < CMPT:
                for j in range(NCMP):
                    if i - WIN <= j < min(S, i + WIN + 1):
                        mask[p, OCMP + j] = 0
    c[:, C_MASK:C_MASK + NSC] = mask
    c[:, C_IOTA:C_IOTA + NPROTO] = np.arange(NPROTO)
    c[:, C_PCOL] = np.arange(P)
    c[:, C_VALID:C_VALID + T] = 1
    for t in range(SELT):
        c[:, C_VALID + T + t] = (mask[:, OSEL + t * NSEL:OSEL + (t + 1) * NSEL] == 0).any(1)
    c[:, C_VALID + T + SELT] = (mask[:, OCMP:] == 0).any(1)
    for j in range(2 * T):
        c[j, C_DELTA + j * DELTA_W:C_DELTA + (j + 1) * DELTA_W] = 1
    c[:, C_HALF + TOPK:C_HALF + 2 * TOPK] = SBS
    c[:, C_ONES:] = 1
    return c


def segment(i):
    if i < T:
        return i * WK, WK
    if i < T + SELT:
        return OSEL + (i - T) * NSEL, NSEL
    return OCMP, NCMP


def build(nc, dram, out):
    with ExitStack() as ctx:
        def sb(name, shape, dt=F32):
            return ctx.enter_context(nc.sbuf_tensor(name, shape, dt))

        def sem(name):
            return ctx.enter_context(nc.semaphore(name))

        const = sb("const", [P, NCONST])
        rows = sb("rows", [P, NROWS])
        cols = sb("cols", [P, NCOLS])
        proto = sb("proto", [P, NPROTO])
        pB = sb("pB", [P, NPROTO * RANK])
        pA = sb("pA", [P, PR, D])
        pbias = sb("pbias", [NPROTO, D])
        wqkv = sb("wqkv", [P, 3, D])
        wcomp = sb("wcomp", [P, CBS, D])
        wgate = sb("wgate", [P, 3])
        wo = sb("wo", [P, D])
        wdq = sb("wdq", [P, DC])
        wkvr = sb("wkvr", [P, DC + DR])
        uq = sb("uq", [P, H1, KQ])
        uk = sb("uk", [P, H1, KQ])
        uv = sb("uv", [P, H1, DC])
        wO = sb("wO", [P, H1, D])
        qr = sb("qr", [KQ, H1, DR])
        gatew = sb("gatew", [P, E])
        w1 = sb("w1", [P, E, F])
        w2 = sb("w2", [P, E, FC, D])
        b2 = sb("b2", [E, D])
        ws8 = sb("ws8", [P, 2 * T, 2 * T])
        protosq = sb("protosq", [P, NPROTO])
        p2b = sb("p2b", [P, NPROTO])
        ninvt = sb("ninvt", [P, 2])
        qk = sb("qk", [KQ, H1, KK])
        vo = sb("vo", [P, 2, D])
        buvb = sb("buvb", [P, H1, P])
        bOb = sb("bOb", [P, D])
        xin = sb("xin", [P, T, D])
        x = sb("x", [P, T, D])
        stats = sb("stats", [P, T, 6])
        mv = sb("mv", [P, T, 2])
        var = sb("var", [P, T])
        lnv = sb("lnv", [P, T])
        rstd0 = sb("rstd0", [P, T])
        nt = sb("nt", [P, T])
        rstd = sb("rstd", [P, T])
        xn = sb("xn", [P, T, D])
        xnT = sb("xnT", [P, PAD])
        sqjunk = sb("sqjunk", [P, D])
        x2 = sb("x2", [P, T])
        d2 = sb("d2", [P, T, NPROTO])
        lnd = sb("lnd", [P, T, NPROTO])
        root = sb("root", [P, T, NPROTO])
        quo = sb("quo", [P, T, NPROTO])
        low = sb("low", [P, T])
        prob = sb("prob", [P, T, NPROTO])
        top8 = sb("top8", [P, T, 8])
        idx8 = sb("idx8", [P, T, 8], U32)
        idxf = sb("idxf", [P, T, 2])
        den = sb("den", [P, T])
        rden = sb("rden", [P, T])
        wk = sb("wk", [P, T, 2])
        wa = sb("wa", [P, T, NPROTO])
        wb = sb("wb", [P, T, NPROTO])
        wsum = sb("wsum", [P, T, NPROTO])
        wT = sb("wT", [NPROTO, S])
        hw = sb("hw", [P, 2, NPROTO * RANK])
        hwT = sb("hwT", [P, 2, PR, P])
        qT = sb("qT", [P, S])
        kvT = sb("kvT", [P, 2, PAD])
        vs = sb("vs", [P, T + 1, D])
        gz = sb("gz", [P, T, 3])
        ge = sb("ge", [P, T, 3])
        gate = sb("gate", [P, T, 3])
        sc = sb("sc", [2 * T, P])
        sc2 = sb("sc2", [2 * T, P])
        sel8 = sb("sel8", [2 * T, 2, TOPK])
        seli = sb("seli", [2 * T, 2, TOPK], U32)
        self_ = sb("self", [2 * T, 2, TOPK])
        selx = sb("selx", [2 * T, 2 * T, DELTA_W])
        onehot = sb("onehot", [P, 2, T, DELTA_W])
        xsel = sb("xsel", [P, 2, NSEL])
        skT = sb("skT", [P, NSEL])
        sv = sb("sv", [P, D])
        ckv = sb("ckv", [P, 2, NCMP])
        cv = sb("cv", [NCMP, D])
        probs0 = sb("probs0", [P, NSC])
        nm0 = sb("nm0", [P, NSEG])
        sum0 = sb("sum0", [P, NSEG])
        rs0 = sb("rs0", [P, NSEG])
        coef = sb("coef", [P, NSEG])
        pTa = sb("pTa", [P, T, P])
        pTb = sb("pTb", [2 * WIN, T, P])
        pTs = sb("pTs", [P, SELT, P])
        pTc = sb("pTc", [NCMP, P])
        combT = sb("combT", [P, T, P])
        lg = sb("lg", [P, T, E])
        pm = sb("pm", [P, 2])
        gm = sb("gm", [2, 1])
        dg = sb("dg", [2, 2])
        nm1 = sb("nm1", [P, 2])
        ek = sb("ek", [P, 2, T])
        es = sb("es", [P, 2])
        rtot = sb("rtot", [P, 2])
        gk = sb("gk", [P, 2, T])
        ga = sb("ga", [P, T, E])
        gb = sb("gb", [P, T, E])
        g = sb("g", [P, T, E])
        gT = sb("gT", [E, S])
        hT = sb("hT", [P, 2, FC, S])
        cqT = sb("cqT", [KQ, S])
        kT = sb("kT", [KK, S])
        ckt = sb("ckt", [P, T, DC])
        QT = sb("QT", [KK, 2, S])
        nm = sb("nm", [P, H1, T])
        probs = sb("probs", [P, 2, T, S])
        rowsum = sb("rowsum", [P, H1, T])
        rrow = sb("rrow", [P, H1, T])
        PT = sb("PT", [P, T, S])
        on = sb("on", [P, T, H1, DC])
        oT = sb("oT", [P, 2, S])

        ps = ctx.enter_context(nc.psum_tensor("ps", [P, 8, S], F32))

        weights_in = sem("weights_in")
        x_in, x_out = sem("x_in"), sem("x_out")
        x_ready = sem("x_ready")
        zeroed = sem("zeroed")
        setup_v, setup_p, setup_own, setup_done = sem("setup_v"), sem("setup_p"), sem("setup_own"), sem("setup_done")
        v_chain, a_chain = sem("v_chain"), sem("a_chain")
        var_ready, rstd0_ready, xn_ready = sem("var_ready"), sem("rstd0_ready"), sem("xn_ready")
        xnT_psum, xnT_ready = sem("xnT_psum"), sem("xnT_ready")
        x2_ready, dot_psum, d2_ready, root_ready = sem("x2_ready"), sem("dot_psum"), sem("d2_ready"), sem("root_ready")
        gap_ready, prob_ready, w_ready, wT_psum, wT_ready = (sem("gap_ready"), sem("prob_ready"), sem("w_ready"),
                                                             sem("wT_psum"), sem("wT_ready"))
        h_psum, hw_ready, hwT_psum, hwT_ready, py_psum = (sem("h_psum"), sem("hw_ready"), sem("hwT_psum"),
                                                          sem("hwT_ready"), sem("py_psum"))
        qkv_psum, q_ready, kv_ready, vs_psum, vs_ready = (sem("qkv_psum"), sem("q_ready"), sem("kv_ready"),
                                                          sem("vs_psum"), sem("vs_ready"))
        gz_ready, ge_ready = sem("gz_ready"), sem("ge_ready")
        score_psum, selx_ready, sel_psum, onehot_ready = (sem("score_psum"), sem("selx_ready"), sem("sel_psum"),
                                                          sem("onehot_ready"))
        comp_psum, comp_ready, cv_psum, cv_ready = sem("comp_psum"), sem("comp_ready"), sem("cv_psum"), sem("cv_ready")
        xsel_psum, xsel_ready, skv_psum, skv_ready = (sem("xsel_psum"), sem("xsel_ready"), sem("skv_psum"),
                                                      sem("skv_ready"))
        win_psum, selcmp_psum, nm0_ready, exp0_ready = (sem("win_psum"), sem("selcmp_psum"), sem("nm0_ready"),
                                                        sem("exp0_ready"))
        probs0_ready, pT_psum, pT_ready, pTb_ready = (sem("probs0_ready"), sem("pT_psum"), sem("pT_ready"),
                                                      sem("pTb_ready"))
        comb_psum, comb_ready, o_psum = sem("comb_psum"), sem("comb_ready"), sem("o_psum")
        lg_psum, pm_ready, pm_psum, dg_ready, mx_psum, nm1_ready = (sem("lg_psum"), sem("pm_ready"), sem("pm_psum"),
                                                                    sem("dg_ready"), sem("mx_psum"), sem("nm1_ready"))
        es_ready, tot_psum, g_ready, gT_psum, gT_ready, b2_psum, b2_used = (
            sem("es_ready"), sem("tot_psum"), sem("g_ready"), sem("gT_psum"), sem("gT_ready"), sem("b2_psum"),
            sem("b2_used"))
        mh_psum, mh_ready, my_psum, my_used = sem("mh_psum"), sem("mh_ready"), sem("my_psum"), sem("my_used")
        cq_psum, cq_ready, kr_psum, kr_ready, ckt_psum, ckt_ready = (
            sem("cq_psum"), sem("cq_ready"), sem("kr_psum"), sem("kr_ready"), sem("ckt_psum"), sem("ckt_ready"))
        QT_psum, QT_ready, s_psum, nm_ready, p_ready = (sem("QT_psum"), sem("QT_ready"), sem("s_psum"),
                                                        sem("nm_ready"), sem("p_ready"))
        PT_psum, PT_ready, pv_psum, on_ready = sem("PT_psum"), sem("PT_ready"), sem("pv_psum"), sem("on_ready")
        oT_psum, oT_ready, mo_psum = sem("oT_psum"), sem("oT_ready"), sem("mo_psum")

        ident = const[:, C_ID:C_ID + P]
        ones = const[:, C_ONES:C_ONES + P]
        iota = const[:, C_IOTA:C_IOTA + NPROTO]

        def row(name):
            return rows[:, ROW_AT[name]:ROW_AT[name] + dict(ROWS)[name]]

        def col(name, k=0):
            return cols[:, COL_AT[name] + k:COL_AT[name] + k + 1]

        def over_tiles(ap, n):
            return ap.unsqueeze(1).to_broadcast([P, T, n])

        loads = [(const[:], dram["const"]), (proto[:], dram["proto"]), (pB[:], dram["pB"]), (pA[:], dram["pA"]),
                 (pbias[:], dram["pbias"]), (cols[:], dram["cols"]), (wqkv[:], dram["wqkv"]), (wgate[:], dram["wgate"]),
                 (wo[:], dram["wo"]), (wdq[:], dram["wdq"]), (wkvr[:], dram["wkvr"]), (uq[:], dram["uq"]),
                 (uk[:], dram["uk"]), (uv[:], dram["uv"]), (wO[:], dram["wO"]), (qr[:], dram["qr"]),
                 (gatew[:], dram["gatew"]), (b2[:], dram["b2"]), (wcomp[:], dram["wcomp"]), (w1[:], dram["w1"]),
                 (w2[:], dram["w2"])]
        NLOADS = len(loads) + 1

        xr = dram["x"].rearrange("b (t p) d -> b p t d", p=P)
        outr = out.rearrange("b (t p) d -> b p t d", p=P)

        block = ctx.enter_context(nc.Block())

        @block.sync
        def _(sp):
            sp.dma_start(xin[:], xr[0]).then_inc(x_in, 16)
            sp.dma_start(rows[:], dram["rows"].partition_broadcast(P)).then_inc(weights_in, 16)
            for dst, src in loads:
                sp.dma_start(dst, src).then_inc(weights_in, 16)
            with nc.sync.Fori(0, NB - 1) as b:
                sp.wait_ge(x_ready, 4 * b + 1)
                sp.dma_start(xin[:], xr[b + 1]).then_inc(x_in, 16)

        @block.gpsimd
        def _(pool):
            nc.gpsimd.memset(xnT[:], 0.0).then_inc(zeroed, 1)
            nc.gpsimd.memset(kvT[:], 0.0).then_inc(zeroed, 1)
            nc.gpsimd.memset(ws8[:], 0.0).then_inc(zeroed, 1)
            pool.wait_ge(zeroed, 3)
            nc.gpsimd.memset(cqT[DC:KQ], 1.0).then_inc(zeroed, 1)
            pool.wait_ge(zeroed, 4)
            nc.gpsimd.memset(kT[DC + DR:KK], 1.0).then_inc(zeroed, 1)
            with nc.gpsimd.Fori(0, NB) as b:
                pool.wait_ge(my_used, 2 * E * b + 2 * E)
                pool.dma_start(outr[b], x[:]).then_inc(x_out, 16)
            pool.wait_ge(x_out, 16 * NB)

        @block.tensor
        def _(pe):
            def mm(o, lhsT, rhs, start=True, stop=True):
                return pe.matmul(o, lhsT, rhs, start=start, stop=stop)

            def turn(o, in_):
                return pe.transpose(o, in_, const[0:in_.shape[0], C_ID:C_ID + in_.shape[0]])

            def setup():
                pe.wait_ge(weights_in, 16 * NLOADS)
                pe.wait_ge(setup_v, 1)
                mm(ps[:, 0, 0:NPROTO], ones, protosq[:]).then_inc(setup_p, 1)
                for h in range(H1):
                    m = mm(ps[0:KQ, 1, h * KQ:(h + 1) * KQ], uq[:, h, :], uk[:, h, :])
                m.then_inc(setup_p, 1)
                for h in range(H1):
                    a = DC * (h % 4)
                    m = mm(ps[a:a + DC, 2, (h // 4) * D:(h // 4 + 1) * D], uv[:, h, :], wO[:, h, :])
                m.then_inc(setup_p, 1)
                pe.wait_ge(setup_v, 2)
                for h in range(H1):
                    m = mm(ps[:, 3, 0:D], buvb[:, h, :], wO[:, h, :], h == 0, h == H1 - 1)
                m.then_inc(setup_p, 1)
                pe.wait_ge(setup_done, 1)

            def transpose_xn(b, s):
                pe.wait_ge(xn_ready, 6 * b + s + 1)
                for t in range(T):
                    m = turn(ps[:, 0, t * P:(t + 1) * P], xn[:, t, :])
                m.then_inc(xnT_psum, 1)
                pe.wait_ge(xnT_ready, 6 * b + s + 1)

            def xT(t):
                return xnT[:, WIN + t * P:WIN + (t + 1) * P]

            def proto_ffn(b, s, r):
                transpose_xn(b, s)
                for t in range(T):
                    m = mm(ps[:, 1, t * NPROTO:(t + 1) * NPROTO], xT(t), proto[:])
                m.then_inc(dot_psum, 1)
                for t in range(T):
                    mm(ps[:, 2 + t, :], xT(t), pB[:]).then_inc(h_psum, 1)
                pe.wait_ge(w_ready, 2 * b + r + 1)
                for t in range(T):
                    m = turn(ps[0:NPROTO, 7, t * P:(t + 1) * P], wsum[:, t, :])
                m.then_inc(wT_psum, 1)
                for t in range(T + 1):
                    if t < T:
                        pe.wait_ge(hw_ready, 8 * b + 4 * r + t + 1)
                        if t >= 2:
                            pe.wait_ge(hwT_ready, 8 * b + 4 * r + t - 1)
                        for c in range(PR):
                            m = turn(ps[:, t % 2, c * P:(c + 1) * P], hw[:, t % 2, c * P:(c + 1) * P])
                        m.then_inc(hwT_psum, 1)
                    if t == 0:
                        pe.wait_ge(wT_ready, 2 * b + r + 1)
                    if t >= 1:
                        u = t - 1
                        pe.wait_ge(hwT_ready, 8 * b + 4 * r + u + 1)
                        o = ps[:, 6, u * P:(u + 1) * P]
                        for c in range(PR):
                            mm(o, hwT[:, u % 2, c, :], pA[:, c, :], c == 0, False)
                        m = mm(o, wT[:, u * P:(u + 1) * P], pbias[:], False, True)
                m.then_inc(py_psum, 1)

            def nsa(b, s):
                transpose_xn(b, s)
                for j in range(3):
                    mm(ps[:, 1 + j, :], wqkv[:, j, :], xnT[:, WIN:WIN + S]).then_inc(qkv_psum, 1)
                for u in range(T + 1):
                    o = ps[:, 4, u * P:(u + 1) * P] if u < T else ps[:, 5, 0:P]
                    mm(o, xnT[:, u * P:(u + 1) * P], wqkv[:, 2, :])
                for t in range(T):
                    m = mm(ps[:, 5, P + 3 * t:P + 3 * t + 3], xT(t), wgate[:])
                m.then_inc(vs_psum, 1)
                pe.wait_ge(kv_ready, 2 * b + 2)
                for j in range(2 * T):
                    a = WIN + (j % T) * P
                    m = mm(ps[0:2 * T, 6, 0:P], ws8[:, j, :], kvT[:, j // T, a:a + P], j == 0, j == 2 * T - 1)
                m.then_inc(score_psum, 1)
                for c in range(CBS):
                    m = mm(ps[:, 7, 0:2 * NCMP], wcomp[:, c, :], kvT[:, :, WIN + c:WIN + S:CBS], c == 0, c == CBS - 1)
                m.then_inc(comp_psum, 1)
                pe.wait_ge(q_ready, b + 1)
                for t in range(T):
                    m = mm(ps[:, t // 2, (t % 2) * 256:(t % 2) * 256 + WK], qT[:, t * P:(t + 1) * P],
                           kvT[:, 0, t * P:t * P + WK])
                m.then_inc(win_psum, 1)
                pe.wait_ge(comp_ready, b + 1)
                turn(ps[0:NCMP, 2, 0:P], ckv[:, 1, :]).then_inc(cv_psum, 1)
                pe.wait_ge(selx_ready, b + 1)
                mm(ps[:, 6, 0:2 * T * DELTA_W], ones[0:2 * T, :], selx[:].rearrange("p a b -> p (a b)")).then_inc(sel_psum, 1)
                pe.wait_ge(onehot_ready, b + 1)
                for t in range(T):
                    o = ps[:, 7, 0:2 * NSEL].rearrange("p (k t j) -> p k t j", k=2, t=T)[:, :, t, :]
                    m = mm(o, xn[:, t, :], onehot[:, :, t, :])
                m.then_inc(xsel_psum, 1)
                pe.wait_ge(xsel_ready, b + 1)
                mm(ps[:, 6, 0:NSEL], wqkv[:, 1, :], xsel[:, 0, :])
                mm(ps[:, 6, P:2 * P], xsel[:, 1, :], wqkv[:, 2, :]).then_inc(skv_psum, 1)
                pe.wait_ge(skv_ready, b + 1)
                for t in range(SELT):
                    mm(ps[:, 7, t * NSEL:(t + 1) * NSEL], qT[:, t * P:(t + 1) * P], skT[:])
                mm(ps[:, 7, SELT * NSEL:SELT * NSEL + NCMP], qT[:, 0:P], ckv[:, 0, :]).then_inc(selcmp_psum, 1)
                pe.wait_ge(probs0_ready, b + 1)
                pe.wait_ge(cv_ready, b + 1)
                for t in range(T):
                    m = turn(ps[:, 2, t * P:(t + 1) * P], probs0[:, t * WK:t * WK + P])
                m.then_inc(pT_psum, 1)
                for t in range(T):
                    m = turn(ps[0:2 * WIN, 3, t * P:(t + 1) * P], probs0[:, t * WK + P:(t + 1) * WK])
                m.then_inc(pT_psum, 1)
                for t in range(SELT):
                    turn(ps[:, 4, t * P:(t + 1) * P], probs0[:, OSEL + t * NSEL:OSEL + (t + 1) * NSEL])
                turn(ps[0:NCMP, 4, SELT * P:(SELT + 1) * P], probs0[:, OCMP:OCMP + NCMP]).then_inc(pT_psum, 1)
                pe.wait_ge(pT_ready, 2 * b + 2)
                pe.wait_ge(pTb_ready, b + 1)
                for t in range(T):
                    o = ps[:, 5, t * P:(t + 1) * P]
                    mm(o, vs[:, t, :], pTa[:, t, :], True, False)
                    m = mm(o, vs[0:2 * WIN, t + 1, :], pTb[:, t, :], False, t >= SELT)
                    if t < SELT:
                        m = mm(o, sv[:], pTs[:, t, :], False, t >= CMPT)
                    if t < CMPT:
                        m = mm(o, cv[:], pTc[:], False, True)
                m.then_inc(comb_psum, 1)
                pe.wait_ge(comb_ready, b + 1)
                for t in range(T):
                    m = mm(ps[:, 6, t * P:(t + 1) * P], combT[:, t, :], wo[:])
                m.then_inc(o_psum, 1)

            def moe(b, s, r):
                HN = E * FC
                transpose_xn(b, s)
                for t in range(T):
                    m = mm(ps[:, 1, t * E:(t + 1) * E], xT(t), gatew[:])
                m.then_inc(lg_psum, 1)

                def hidden(e):
                    for c in range(FC):
                        n = e * FC + c
                        if n >= 3:
                            pe.wait_ge(mh_ready, 2 * HN * b + HN * r + n - 2)
                        mm(ps[:, 2 + n % 3, :], w1[:, e, c * P:(c + 1) * P], xnT[:, WIN:WIN + S]).then_inc(mh_psum, 1)

                def down(e):
                    pe.wait_ge(mh_ready, 2 * HN * b + HN * r + (e + 1) * FC)
                    if e >= 2:
                        pe.wait_ge(my_used, 2 * E * b + E * r + e - 1)
                    for t in range(T):
                        for c in range(FC):
                            m = mm(ps[:, 6 + e % 2, t * P:(t + 1) * P], hT[:, e % 2, c, t * P:(t + 1) * P],
                                   w2[:, e, c, :], c == 0, c == FC - 1)
                    m.then_inc(my_psum, 1)

                hidden(0)
                pe.wait_ge(pm_ready, 2 * b + r + 1)
                turn(ps[0:2, 1, 0:P], pm[:]).then_inc(pm_psum, 1)
                hidden(1)
                pe.wait_ge(dg_ready, 2 * b + r + 1)
                mm(ps[:, 1, 0:2], ones[0:2, :], dg[:]).then_inc(mx_psum, 1)
                down(0)
                pe.wait_ge(es_ready, 2 * b + r + 1)
                mm(ps[:, 1, 0:2], ones, es[:]).then_inc(tot_psum, 1)
                down(1)
                hidden(2)
                pe.wait_ge(g_ready, 2 * b + r + 1)
                for t in range(T):
                    m = turn(ps[0:E, 5, t * P:(t + 1) * P], g[:, t, :])
                m.then_inc(gT_psum, 1)
                hidden(3)
                pe.wait_ge(gT_ready, 2 * b + r + 1)
                for t in range(T):
                    m = mm(ps[:, 0, t * P:(t + 1) * P], gT[:, t * P:(t + 1) * P], b2[:])
                m.then_inc(b2_psum, 1)
                down(2)
                for e in range(4, E):
                    hidden(e)
                    down(e - 1)
                down(E - 1)

            def mla(b, s):
                transpose_xn(b, s)
                mm(ps[0:DC, 1, :], wdq[:], xnT[:, WIN:WIN + S]).then_inc(cq_psum, 1)
                mm(ps[0:DC + DR, 2, :], wkvr[:], xnT[:, WIN:WIN + S]).then_inc(kr_psum, 1)
                for t in range(T):
                    m = mm(ps[:, 3, t * DC:(t + 1) * DC], xT(t), wkvr[:, 0:DC])
                m.then_inc(ckt_psum, 1)

                def query(h):
                    if h == 0:
                        pe.wait_ge(cq_ready, b + 1)
                        pe.wait_ge(kr_ready, b + 1)
                    if h >= 2:
                        pe.wait_ge(QT_ready, H1 * b + h - 1)
                    mm(ps[0:KK, 1 + h % 2, :], qk[:, h, :], cqT[:]).then_inc(QT_psum, 1)

                def scores(h):
                    pe.wait_ge(QT_ready, H1 * b + h + 1)
                    if h == 0:
                        pe.wait_ge(ckt_ready, b + 1)
                    for t in range(T):
                        n = h * T + t
                        if n >= 2:
                            pe.wait_ge(p_ready, H1 * T * b + n - 1)
                        mm(ps[:, 3 + n % 2, :], QT[:, h % 2, t * P:(t + 1) * P], kT[:]).then_inc(s_psum, 1)

                def turn_probs(h):
                    pe.wait_ge(p_ready, H1 * T * b + (h + 1) * T)
                    for k in range(T):
                        n = h * T + k
                        if n >= 2:
                            pe.wait_ge(PT_ready, H1 * T * b + n - 1)
                        for t in range(T):
                            m = turn(ps[:, 5 + n % 2, t * P:(t + 1) * P], probs[:, h % 2, t, k * P:(k + 1) * P])
                        m.then_inc(PT_psum, 1)

                def values(h):
                    pe.wait_ge(PT_ready, H1 * T * b + (h + 1) * T)
                    for t in range(T):
                        a = (t % 2) * H1 * DC + h * DC
                        for k in range(T):
                            m = mm(ps[:, 7 * (1 - t // 2), a:a + DC], PT[:, k, t * P:(t + 1) * P], ckt[:, k, :],
                                   k == 0, k == T - 1)
                    m.then_inc(pv_psum, 1)

                query(0)
                scores(0)
                query(1)
                for h in range(H1):
                    if h + 1 < H1:
                        scores(h + 1)
                    if h + 2 < H1:
                        query(h + 2)
                    turn_probs(h)
                    values(h)
                pe.wait_ge(on_ready, b + 1)
                for c in range(2):
                    for t in range(T):
                        m = turn(ps[:, 5 + c, t * P:(t + 1) * P],
                                 on[:, t, 4 * c:4 * c + 4, :].rearrange("p h d -> p (h d)"))
                    m.then_inc(oT_psum, 1)
                pe.wait_ge(oT_ready, 2 * b + 2)
                for t in range(T):
                    for c in range(2):
                        m = mm(ps[:, 1, t * P:(t + 1) * P], oT[:, c, t * P:(t + 1) * P], vo[:, c, :], c == 0, c == 1)
                m.then_inc(mo_psum, 1)

            setup()
            with nc.tensor.Fori(0, NB) as b:
                proto_ffn(b, 0, 0)
                nsa(b, 1)
                proto_ffn(b, 2, 1)
                moe(b, 3, 0)
                mla(b, 4)
                moe(b, 5, 1)

        @block.scalar
        def _(act):
            nc.scalar.preload_act_table_set("natural_log_exp_and_others")
            chained = [0]

            def link(b, ins):
                chained[0] += 1
                ins.then_inc(a_chain, 1)
                act.wait_ge(a_chain, chained[0])

            def transpose_xn(b, s):
                act.wait_ge(var_ready, 6 * b + s + 1)
                link(b, nc.scalar.activation(lnv[:], var[:], ACT.Ln))
                nc.scalar.activation(rstd0[:], lnv[:], ACT.Exp, scale=-0.5).then_inc(rstd0_ready, 1)
                act.wait_ge(xnT_psum, 6 * b + s + 1)
                nc.scalar.copy(xnT[:, WIN:WIN + S], ps[:, 0, :]).then_inc(xnT_ready, 1)

            def proto_ffn(b, s, r):
                transpose_xn(b, s)
                for t in range(T):
                    i = nc.scalar.activation(sqjunk[:], xn[:, t, :], ACT.Square, accum_out=x2[:, t:t + 1])
                    if t < T - 1:
                        link(b, i)
                i.then_inc(x2_ready, 1)
                act.wait_ge(d2_ready, 2 * b + r + 1)
                link(b, nc.scalar.activation(lnd[:], d2[:], ACT.Ln))
                nc.scalar.activation(root[:], lnd[:], ACT.Exp, scale=0.5).then_inc(root_ready, 1)
                act.wait_ge(gap_ready, 2 * b + r + 1)
                nc.scalar.activation(prob[:], quo[:], ACT.Exp, scale=ninvt[:, 1:2]).then_inc(prob_ready, 1)
                act.wait_ge(wT_psum, 2 * b + r + 1)
                nc.scalar.copy(wT[:], ps[0:NPROTO, 7, :]).then_inc(wT_ready, 1)
                for t in range(T):
                    act.wait_ge(hwT_psum, 8 * b + 4 * r + t + 1)
                    nc.scalar.copy(hwT[:, t % 2].rearrange("p c j -> p (c j)"), ps[:, t % 2, :]).then_inc(hwT_ready, 1)

            def nsa(b, s):
                transpose_xn(b, s)
                for j, bias in ((0, col("bk")), (1, col("bvc"))):
                    act.wait_ge(qkv_psum, 3 * b + 2 + j)
                    nc.scalar.activation(kvT[:, j, WIN:WIN + S], ps[:, 2 + j, :], ACT.Identity, bias=bias).then_inc(kv_ready, 1)
                act.wait_ge(gz_ready, b + 1)
                nc.scalar.activation(ge[:], gz[:], ACT.Exp, scale=-1.0).then_inc(ge_ready, 1)
                act.wait_ge(comp_psum, b + 1)
                nc.scalar.activation(ckv[:].rearrange("p k n -> p (k n)"), ps[:, 7, 0:2 * NCMP], ACT.Identity,
                                     bias=col("bcomp")).then_inc(comp_ready, 1)
                act.wait_ge(cv_psum, b + 1)
                nc.scalar.copy(cv[:], ps[0:NCMP, 2, 0:P]).then_inc(cv_ready, 1)
                act.wait_ge(xsel_psum, b + 1)
                nc.scalar.copy(xsel[:].rearrange("p k n -> p (k n)"), ps[:, 7, 0:2 * NSEL]).then_inc(xsel_ready, 1)
                act.wait_ge(nm0_ready, b + 1)
                for i in range(NSEG):
                    a, n = segment(i)
                    e = nc.scalar.activation(probs0[:, a:a + n], probs0[:, a:a + n], ACT.Exp, bias=nm0[:, i:i + 1],
                                             accum_out=sum0[:, i:i + 1])
                e.then_inc(exp0_ready, 1)
                act.wait_ge(pT_psum, 3 * b + 1)
                nc.scalar.copy(pTa[:].rearrange("p t q -> p (t q)"), ps[:, 2, :]).then_inc(pT_ready, 1)
                act.wait_ge(pT_psum, 3 * b + 3)
                nc.scalar.copy(pTs[:].rearrange("p t q -> p (t q)"), ps[:, 4, 0:SELT * P])
                nc.scalar.copy(pTc[:], ps[0:NCMP, 4, SELT * P:(SELT + 1) * P]).then_inc(pT_ready, 1)
                act.wait_ge(comb_psum, b + 1)
                nc.scalar.copy(combT[:].rearrange("p t q -> p (t q)"), ps[:, 5, :]).then_inc(comb_ready, 1)

            def moe(b, s, r):
                HN = E * FC
                transpose_xn(b, s)

                def hidden(e):
                    for c in range(FC):
                        n = e * FC + c
                        act.wait_ge(mh_psum, 2 * HN * b + HN * r + n + 1)
                        if c == 0 and e >= 2:
                            act.wait_ge(my_psum, 2 * E * b + E * r + e - 1)
                        nc.scalar.activation(hT[:, e % 2, c, :], ps[:, 2 + n % 3, :], ACT.Relu,
                                             bias=col("b1", n)).then_inc(mh_ready, 1)

                hidden(0)
                hidden(1)
                act.wait_ge(nm1_ready, 2 * b + r + 1)
                for k in range(2):
                    i = nc.scalar.activation(ek[:, k, :], top8[:, :, k], ACT.Exp, bias=nm1[:, k:k + 1],
                                             accum_out=es[:, k:k + 1])
                i.then_inc(es_ready, 1)
                hidden(2)
                act.wait_ge(gT_psum, 2 * b + r + 1)
                nc.scalar.copy(gT[:], ps[0:E, 5, :]).then_inc(gT_ready, 1)
                for e in range(3, E):
                    hidden(e)

            def mla(b, s):
                transpose_xn(b, s)
                act.wait_ge(kr_psum, b + 1)
                nc.scalar.activation(kT[0:DC + DR, :], ps[0:DC + DR, 2, :], ACT.Identity,
                                     bias=cols[0:DC + DR, COL_AT["bkr"]:COL_AT["bkr"] + 1]).then_inc(kr_ready, 1)

                def query(h):
                    act.wait_ge(QT_psum, H1 * b + h + 1)
                    nc.scalar.copy(QT[:, h % 2, :], ps[0:KK, 1 + h % 2, :]).then_inc(QT_ready, 1)

                def soft(h):
                    for t in range(T):
                        n = h * T + t
                        act.wait_ge(nm_ready, H1 * T * b + n + 1)
                        if t == 0 and h >= 2:
                            act.wait_ge(PT_psum, H1 * T * b + (h - 1) * T)
                        nc.scalar.activation(probs[:, h % 2, t, :], ps[:, 3 + n % 2, :], ACT.Exp,
                                             bias=nm[:, h, t:t + 1], accum_out=rowsum[:, h, t:t + 1]).then_inc(p_ready, 1)

                query(0)
                soft(0)
                query(1)
                for h in range(H1):
                    if h + 1 < H1:
                        soft(h + 1)
                    if h + 2 < H1:
                        query(h + 2)
                for c in range(2):
                    act.wait_ge(oT_psum, 2 * b + c + 1)
                    nc.scalar.copy(oT[:, c, :], ps[:, 5 + c, :]).then_inc(oT_ready, 1)

            with nc.scalar.Fori(0, NB) as b:
                nc.scalar.sem_clear(a_chain)
                proto_ffn(b, 0, 0)
                nsa(b, 1)
                proto_ffn(b, 2, 1)
                moe(b, 3, 0)
                mla(b, 4)
                moe(b, 5, 1)

        @block.vector
        def _(dve):
            chained = [0]

            def link(b, ins):
                chained[0] += 1
                ins.then_inc(v_chain, 1)
                dve.wait_ge(v_chain, chained[0])

            def setup():
                dve.wait_ge(weights_in, 16 * NLOADS)
                dve.wait_ge(zeroed, 5)
                done = [0]

                def then(ins):
                    done[0] += 1
                    ins.then_inc(setup_own, 1)
                    dve.wait_ge(setup_own, done[0])

                nc.vector.tensor_tensor(protosq[:], proto[:], proto[:], ALU.mult).then_inc(setup_v, 1)
                nc.vector.tensor_copy(buvb[:], cols[:, COL_AT["buv"]:COL_AT["buv"] + H1].unsqueeze(2).to_broadcast([P, H1, P])
                                      ).then_inc(setup_v, 1)
                nc.vector.tensor_copy(ws8[:].rearrange("p a b -> p (a b)")[:, ::2 * T + 1],
                                      col("ws").to_broadcast([P, 2 * T]))
                then(nc.vector.tensor_scalar(ninvt[:, 0:1], row("temp"), -1.0, None, ALU.mult))
                then(nc.vector.tensor_tensor(ninvt[:, 0:1], ninvt[:, 0:1], row("temp"), ALU.max))
                then(nc.vector.tensor_scalar(ninvt[:, 0:1], ninvt[:, 0:1], 0.1, -2.0, ALU.max, ALU.mult))
                then(nc.vector.reciprocal(ninvt[:, 1:2], ninvt[:, 0:1]))
                dve.wait_ge(setup_p, 1)
                nc.vector.tensor_copy(p2b[:], ps[:, 0, 0:NPROTO])
                dve.wait_ge(setup_p, 2)
                o = ps[0:KQ, 1, 0:H1 * KQ].rearrange("p (h k) -> p h k", h=H1)
                nc.vector.tensor_scalar(qk[:, :, 0:DC], o[:, :, 0:DC], SCALE1, None, ALU.mult)
                nc.vector.tensor_scalar(qk[:, :, DC + DR:KK], o[:, :, DC:KQ], SCALE1, None, ALU.mult)
                nc.vector.tensor_scalar(qk[:, :, DC:DC + DR], qr[:], SCALE1, None, ALU.mult)
                dve.wait_ge(setup_p, 3)
                nc.vector.tensor_copy(vo[:].rearrange("p c d -> p (c d)"), ps[:, 2, 0:2 * D])
                dve.wait_ge(setup_p, 4)
                then(nc.vector.tensor_tensor(bOb[:], ps[:, 3, 0:D], row("bO"), ALU.add))
                nc.vector.memset(nt[:], 0.0).then_inc(setup_done, 1)

            def layernorm(b, s, src):
                for t in range(T):
                    i = nc.vector.bn_stats(stats[:, t, :], src[:, t, :])
                link(b, i)
                for t in range(T):
                    i = nc.vector.bn_aggr(mv[:, t, :], stats[:, t, :])
                link(b, i)
                nc.vector.tensor_scalar(var[:], mv[:, :, 1], EPS, None, ALU.add).then_inc(var_ready, 1)
                dve.wait_ge(rstd0_ready, 6 * b + s + 1)
                link(b, nc.vector.tensor_tensor(nt[:], rstd0[:], rstd0[:], ALU.mult))
                link(b, nc.vector.tensor_tensor(nt[:], nt[:], var[:], ALU.mult))
                link(b, nc.vector.tensor_scalar(nt[:], nt[:], -0.5, 1.5, ALU.mult, ALU.add))
                link(b, nc.vector.tensor_tensor(rstd[:], nt[:], rstd0[:], ALU.mult))
                for t in range(T):
                    i = nc.vector.tensor_scalar(xn[:, t, :], src[:, t, :], mv[:, t, 0:1], rstd[:, t:t + 1],
                                                ALU.subtract, ALU.mult)
                i.then_inc(xn_ready, 1)

            def two_hot(b, first, second, total, weight, n):
                for t in range(T):
                    nc.vector.tensor_scalar(first[:, t, :], iota[:, 0:n], idxf[:, t, 0:1], weight(t, 0),
                                            ALU.is_equal, ALU.mult)
                    i = nc.vector.tensor_scalar(second[:, t, :], iota[:, 0:n], idxf[:, t, 1:2], weight(t, 1),
                                                ALU.is_equal, ALU.mult)
                link(b, i)
                return nc.vector.tensor_tensor(total[:], first[:], second[:], ALU.add)

            def proto_ffn(b, s, r, src):
                layernorm(b, s, src)
                dve.wait_ge(dot_psum, 2 * b + r + 1)
                link(b, nc.vector.scalar_tensor_tensor(
                    out=d2[:], in0=ps[:, 1, 0:T * NPROTO].rearrange("p (t n) -> p t n", t=T), scalar=-2.0,
                    in1=over_tiles(p2b[:], NPROTO), op0=ALU.mult, op1=ALU.add))
                dve.wait_ge(x2_ready, 2 * b + r + 1)
                link(b, nc.vector.tensor_tensor(d2[:], d2[:], x2[:].unsqueeze(2).to_broadcast([P, T, NPROTO]), ALU.add))
                nc.vector.tensor_scalar(d2[:], d2[:], 0.0, TINY, ALU.max, ALU.max).then_inc(d2_ready, 1)
                dve.wait_ge(root_ready, 2 * b + r + 1)
                link(b, nc.vector.reciprocal(quo[:], root[:]))
                link(b, nc.vector.tensor_tensor(quo[:], quo[:], d2[:], ALU.mult))
                link(b, nc.vector.tensor_tensor(quo[:], quo[:], root[:], ALU.add))
                link(b, nc.vector.tensor_reduce(low[:], quo[:], X, ALU.min))
                nc.vector.tensor_tensor(quo[:], quo[:], low[:].unsqueeze(2).to_broadcast([P, T, NPROTO]),
                                        ALU.subtract).then_inc(gap_ready, 1)
                dve.wait_ge(prob_ready, 2 * b + r + 1)
                nc.vector.memset(wk[:], 0.0)
                for t in range(T):
                    i = nc.vector.max(top8[:, t, :], prob[:, t, :])
                link(b, i)
                for t in range(T):
                    nc.vector.max_index(idx8[:, t, :], top8[:, t, :], prob[:, t, :])
                link(b, nc.vector.tensor_tensor(den[:], top8[:, :, 0], top8[:, :, 1], ALU.add))
                nc.vector.tensor_copy(idxf[:], idx8[:, :, 0:2])
                link(b, nc.vector.reciprocal(rden[:], den[:]))
                link(b, nc.vector.scalar_tensor_tensor(out=wk[:], in0=top8[:, :, 0:2], scalar=0.5,
                                                       in1=rden[:].unsqueeze(2).to_broadcast([P, T, 2]),
                                                       op0=ALU.mult, op1=ALU.mult))
                two_hot(b, wa, wb, wsum, lambda t, k: wk[:, t, k:k + 1], NPROTO).then_inc(w_ready, 1)
                dve.wait_ge(w_ready, 2 * b + r + 1)
                for t in range(T):
                    dve.wait_ge(h_psum, 8 * b + 4 * r + t + 1)
                    if t >= 2:
                        dve.wait_ge(hwT_psum, 8 * b + 4 * r + t - 1)
                    nc.vector.tensor_tensor(hw[:, t % 2].rearrange("p (n j) -> p n j", j=RANK),
                                            ps[:, 2 + t, :].rearrange("p (n j) -> p n j", j=RANK),
                                            wsum[:, t, :].unsqueeze(2).to_broadcast([P, NPROTO, RANK]),
                                            ALU.mult).then_inc(hw_ready, 1)
                dve.wait_ge(py_psum, 2 * b + r + 1)
                if s == 0:
                    dve.wait_ge(x_out, 16 * b)
                nc.vector.tensor_tensor(x[:].rearrange("p t d -> p (t d)"), ps[:, 6, :],
                                        src[:].rearrange("p t d -> p (t d)"), ALU.add).then_inc(x_ready, 1)
                dve.wait_ge(x_ready, 4 * b + s + 1)

            def topk(b):
                link(b, nc.vector.tensor_scalar(sc[:], ps[0:2 * T, 6, 0:P], rows[0:2 * T, ROW_AT["bs"]:ROW_AT["bs"] + 1],
                                                None, ALU.add))
                blk = [slice(h * SBS, (h + 1) * SBS) for h in range(2)]
                for h in range(2):
                    i = nc.vector.max(sel8[:, h, 0:8], sc[:, blk[h]])
                link(b, i)
                for h in range(2):
                    nc.vector.max_index(seli[:, h, 0:8], sel8[:, h, 0:8], sc[:, blk[h]])
                    i = nc.vector.match_replace(sc2[:, blk[h]], sel8[:, h, 0:8], sc[:, blk[h]], LOWEST)
                link(b, i)
                for h in range(2):
                    i = nc.vector.max(sel8[:, h, 8:16], sc2[:, blk[h]])
                link(b, i)
                for h in range(2):
                    i = nc.vector.max_index(seli[:, h, 8:16], sel8[:, h, 8:16], sc2[:, blk[h]])
                link(b, i)
                link(b, nc.vector.tensor_copy(self_[:], seli[:]))
                link(b, nc.vector.tensor_tensor(self_[:].rearrange("p a b -> p (a b)"), self_[:].rearrange("p a b -> p (a b)"),
                                                const[0:2 * T, C_HALF:C_HALF + DELTA_W], ALU.add))
                nc.vector.tensor_tensor(
                    selx[:], self_[:].rearrange("p a b -> p (a b)").unsqueeze(1).to_broadcast([2 * T, 2 * T, DELTA_W]),
                    const[0:2 * T, C_DELTA:C_DELTA + 2 * T * DELTA_W].rearrange("p (a b) -> p a b", a=2 * T),
                    ALU.mult).then_inc(selx_ready, 1)

            def nsa(b, s):
                layernorm(b, s, x)
                dve.wait_ge(qkv_psum, 3 * b + 1)
                nc.vector.tensor_scalar(qT[:], ps[:, 1, :], col("bq"), None, ALU.add).then_inc(q_ready, 1)
                dve.wait_ge(vs_psum, b + 1)
                nc.vector.tensor_tensor(vs[:, 0:T, :], ps[:, 4, :].rearrange("p (t d) -> p t d", t=T),
                                        over_tiles(row("bv"), D), ALU.add)
                nc.vector.tensor_tensor(gz[:], ps[:, 5, P:P + 3 * T].rearrange("p (t n) -> p t n", t=T),
                                        over_tiles(row("bg"), 3), ALU.add).then_inc(gz_ready, 1)
                nc.vector.tensor_tensor(vs[:, T, :], ps[:, 5, 0:P], row("bv"), ALU.add).then_inc(vs_ready, 1)
                dve.wait_ge(score_psum, b + 1)
                topk(b)
                dve.wait_ge(ge_ready, b + 1)
                link(b, nc.vector.tensor_scalar(ge[:], ge[:], 1.0, None, ALU.add))
                link(b, nc.vector.reciprocal(gate[:], ge[:]))
                dve.wait_ge(win_psum, b + 1)
                for j in range(2):
                    a = 2 * j * WK
                    i = nc.vector.scalar_tensor_tensor(
                        out=probs0[:, a:a + 2 * WK].rearrange("p (t k) -> p t k", t=2),
                        in0=ps[:, j, :].rearrange("p (t k) -> p t k", t=2)[:, :, 0:WK], scalar=SCALE0,
                        in1=const[:, C_MASK + a:C_MASK + a + 2 * WK].rearrange("p (t k) -> p t k", t=2),
                        op0=ALU.mult, op1=ALU.add)
                link(b, i)
                nc.vector.tensor_reduce(nm0[:, 0:T], probs0[:, 0:T * WK].rearrange("p (t k) -> p t k", t=T), X, ALU.max,
                                        negate=True)
                dve.wait_ge(sel_psum, b + 1)
                nc.vector.tensor_scalar(onehot[:].rearrange("p k t j -> p (k t j)"), ps[:, 6, 0:2 * T * DELTA_W],
                                        const[:, C_PCOL:C_PCOL + 1], None, ALU.is_equal).then_inc(onehot_ready, 1)
                dve.wait_ge(skv_psum, b + 1)
                nc.vector.tensor_scalar(skT[:], ps[:, 6, 0:NSEL], col("bk"), None, ALU.add)
                nc.vector.tensor_tensor(sv[:], ps[:, 6, P:2 * P], row("bv"), ALU.add).then_inc(skv_ready, 1)
                dve.wait_ge(selcmp_psum, b + 1)
                link(b, nc.vector.scalar_tensor_tensor(
                    out=probs0[:, OSEL:NSC], in0=ps[:, 7, 0:NSC - OSEL], scalar=SCALE0,
                    in1=const[:, C_MASK + OSEL:C_MASK + NSC], op0=ALU.mult, op1=ALU.add))
                nc.vector.tensor_reduce(nm0[:, T:T + SELT], probs0[:, OSEL:OCMP].rearrange("p (t k) -> p t k", t=SELT),
                                        X, ALU.max, negate=True)
                nc.vector.tensor_reduce(nm0[:, T + SELT:NSEG], probs0[:, OCMP:NSC], X, ALU.max,
                                        negate=True).then_inc(nm0_ready, 1)
                dve.wait_ge(exp0_ready, b + 1)
                link(b, nc.vector.reciprocal(rs0[:], sum0[:]))
                nc.vector.tensor_tensor(coef[:, 0:T], rs0[:, 0:T], gate[:, :, 2], ALU.mult)
                nc.vector.tensor_tensor(coef[:, T:T + SELT], rs0[:, T:T + SELT], gate[:, 0:SELT, 1], ALU.mult)
                link(b, nc.vector.tensor_tensor(coef[:, T + SELT:NSEG], rs0[:, T + SELT:NSEG], gate[:, 0:CMPT, 0], ALU.mult))
                link(b, nc.vector.tensor_tensor(coef[:], coef[:], const[:, C_VALID:C_VALID + NSEG], ALU.mult))
                for k in range(NSEG):
                    a, n = segment(k)
                    i = nc.vector.tensor_scalar(probs0[:, a:a + n], probs0[:, a:a + n], coef[:, k:k + 1], None, ALU.mult)
                i.then_inc(probs0_ready, 1)
                dve.wait_ge(pT_psum, 3 * b + 2)
                nc.vector.tensor_copy(pTb[:].rearrange("p t q -> p (t q)"), ps[0:2 * WIN, 3, :]).then_inc(pTb_ready, 1)
                dve.wait_ge(o_psum, b + 1)
                link(b, nc.vector.tensor_tensor(x[:].rearrange("p t d -> p (t d)"), ps[:, 6, :],
                                                x[:].rearrange("p t d -> p (t d)"), ALU.add))
                nc.vector.tensor_tensor(x[:], x[:], over_tiles(row("bo"), D), ALU.add).then_inc(x_ready, 1)
                dve.wait_ge(x_ready, 4 * b + 2)

            def moe(b, s, r):
                layernorm(b, s, x)
                dve.wait_ge(lg_psum, 2 * b + r + 1)
                link(b, nc.vector.tensor_tensor(lg[:], ps[:, 1, 0:T * E].rearrange("p (t e) -> p t e", t=T),
                                                over_tiles(row("gb"), E), ALU.add))
                for t in range(T):
                    i = nc.vector.max(top8[:, t, :], lg[:, t, :])
                link(b, i)
                nc.vector.tensor_reduce(pm[:], top8[:, :, 0:2].rearrange("p t k -> p k t"), X, ALU.max).then_inc(pm_ready, 1)
                for t in range(T):
                    i = nc.vector.max_index(idx8[:, t, :], top8[:, t, :], lg[:, t, :])
                link(b, i)
                nc.vector.tensor_copy(idxf[:], idx8[:, :, 0:2])
                dve.wait_ge(pm_psum, 2 * b + r + 1)
                link(b, nc.vector.tensor_reduce(gm[:], ps[0:2, 1, 0:P], X, ALU.max))
                nc.vector.tensor_scalar(dg[:], const[0:2, C_ID:C_ID + 2], gm[:], None, ALU.mult).then_inc(dg_ready, 1)
                dve.wait_ge(mx_psum, 2 * b + r + 1)
                nc.vector.tensor_scalar(nm1[:], ps[:, 1, 0:2], -1.0, None, ALU.mult).then_inc(nm1_ready, 1)
                dve.wait_ge(tot_psum, 2 * b + r + 1)
                link(b, nc.vector.reciprocal(rtot[:], ps[:, 1, 0:2]))
                link(b, nc.vector.scalar_tensor_tensor(out=gk[:], in0=ek[:], scalar=0.5,
                                                       in1=rtot[:].unsqueeze(2).to_broadcast([P, 2, T]),
                                                       op0=ALU.mult, op1=ALU.mult))
                two_hot(b, ga, gb, g, lambda t, k: gk[:, k, t:t + 1], E).then_inc(g_ready, 1)
                dve.wait_ge(g_ready, 2 * b + r + 1)
                for e in range(E):
                    dve.wait_ge(my_psum, 2 * E * b + E * r + e + 1)
                    for t in range(T):
                        i = nc.vector.scalar_tensor_tensor(
                            out=x[:, t, :], in0=ps[:, 6 + e % 2, t * P:(t + 1) * P], scalar=g[:, t, e:e + 1],
                            in1=x[:, t, :], op0=ALU.mult, op1=ALU.add)
                    i.then_inc(my_used, 1)
                    if s < 5 or e < E - 1:
                        dve.wait_ge(my_used, 2 * E * b + E * r + e + 1)
                    if e == 2:
                        dve.wait_ge(b2_psum, 2 * b + r + 1)
                        link(b, nc.vector.tensor_tensor(x[:].rearrange("p t d -> p (t d)"), ps[:, 0, :],
                                                        x[:].rearrange("p t d -> p (t d)"), ALU.add))

            def mla(b, s):
                layernorm(b, s, x)
                dve.wait_ge(cq_psum, b + 1)
                nc.vector.tensor_scalar(cqT[0:DC, :], ps[0:DC, 1, :], cols[0:DC, COL_AT["bdq"]:COL_AT["bdq"] + 1], None,
                                        ALU.add).then_inc(cq_ready, 1)
                dve.wait_ge(ckt_psum, b + 1)
                nc.vector.tensor_tensor(ckt[:], ps[:, 3, 0:T * DC].rearrange("p (t n) -> p t n", t=T),
                                        over_tiles(row("bdkv"), DC), ALU.add).then_inc(ckt_ready, 1)

                def row_max(h):
                    for t in range(T):
                        n = h * T + t
                        dve.wait_ge(s_psum, H1 * T * b + n + 1)
                        nc.vector.tensor_reduce(nm[:, h, t:t + 1], ps[:, 3 + n % 2, :], X, ALU.max,
                                                negate=True).then_inc(nm_ready, 1)

                def turned(h):
                    for k in range(T):
                        n = h * T + k
                        dve.wait_ge(PT_psum, H1 * T * b + n + 1)
                        if k == 0 and h >= 1:
                            dve.wait_ge(pv_psum, H1 * b + h)
                        nc.vector.tensor_copy(PT[:, k, :], ps[:, 5 + n % 2, :]).then_inc(PT_ready, 1)

                row_max(0)
                for h in range(H1):
                    if h + 1 < H1:
                        row_max(h + 1)
                    turned(h)
                dve.wait_ge(p_ready, H1 * T * (b + 1))
                link(b, nc.vector.reciprocal(rrow[:], rowsum[:]))
                dve.wait_ge(pv_psum, H1 * (b + 1))
                for t in range(T):
                    a = (t % 2) * H1 * DC
                    i = nc.vector.tensor_tensor(
                        on[:, t], ps[:, 7 * (1 - t // 2), a:a + H1 * DC].rearrange("p (h d) -> p h d", h=H1),
                        rrow[:, :, t:t + 1].to_broadcast([P, H1, DC]), ALU.mult)
                i.then_inc(on_ready, 1)
                dve.wait_ge(mo_psum, b + 1)
                link(b, nc.vector.tensor_tensor(x[:].rearrange("p t d -> p (t d)"), ps[:, 1, :],
                                                x[:].rearrange("p t d -> p (t d)"), ALU.add))
                nc.vector.tensor_tensor(x[:], x[:], over_tiles(bOb[:], D), ALU.add).then_inc(x_ready, 1)
                dve.wait_ge(x_ready, 4 * b + 4)

            setup()
            with nc.vector.Fori(0, NB) as b:
                nc.vector.sem_clear(v_chain)
                dve.wait_ge(x_in, 16 * b + 16)
                proto_ffn(b, 0, 0, xin)
                nsa(b, 1)
                proto_ffn(b, 2, 1, x)
                moe(b, 3, 0)
                mla(b, 4)
                moe(b, 5, 1)


def lay_out(i):
    def f(name):
        return np.asarray(i[name])

    def t(a):
        return np.ascontiguousarray(a)

    wqkv = f("L0_attn_w_qkv").reshape(H0, 3, HD0, D)
    bqkv = f("L0_attn_b_qkv").reshape(H0, 3, HD0).transpose(1, 0, 2).reshape(3, D)
    buq = f("L1_attn_b_UQ").reshape(H1, DK)
    bukh = f("L1_attn_b_UK").reshape(H1, DK)
    parts = {"bv": bqkv[2], "bg": f("L0_attn_b_gate"), "bo": f("L0_attn_b_o"), "gb": f("L1_ffn_gate_b"),
             "bdkv": f("L1_attn_b_DKV"), "bO": f("L1_attn_b_O"), "bs": f("L0_attn_b_score"),
             "temp": f("L0_ffn_temp").reshape(1)}
    cols = np.zeros((P, NCOLS), np.float32)

    def put(name, a):
        cols[:a.shape[0], COL_AT[name]:COL_AT[name] + a.shape[1]] = a

    put("bq", bqkv[0][:, None])
    put("bk", bqkv[1][:, None])
    put("bvc", bqkv[2][:, None])
    put("bcomp", f("L0_attn_b_comp")[:, None])
    put("b1", f("L1_ffn_b1").reshape(E * FC, P).T)
    put("buv", f("L1_attn_b_UV").reshape(H1, DK).T)
    put("bkr", np.concatenate([f("L1_attn_b_DKV"), f("L1_attn_b_KR")])[:, None])
    put("bdq", f("L1_attn_b_DQ")[:, None])
    put("ws", f("L0_attn_w_score").T)
    wuq = np.concatenate([f("L1_attn_W_UQ").reshape(DC, H1, DK), buq[None]], 0)
    wuk = np.concatenate([f("L1_attn_W_UK").reshape(DC, H1, DK), bukh[None]], 0)
    return {
        "x": t(f("L0_attn_x")),
        "const": constants(),
        "rows": t(np.concatenate([parts[n] for n, _ in ROWS])),
        "cols": cols,
        "proto": t(f("L0_ffn_prototypes").T),
        "pB": t(f("L0_ffn_B").reshape(NPROTO * RANK, D).T),
        "pA": t(f("L0_ffn_A").transpose(0, 2, 1).reshape(PR, P, D).transpose(1, 0, 2)),
        "pbias": t(f("L0_ffn_bias")),
        "wqkv": t(wqkv.transpose(3, 1, 0, 2).reshape(D, 3, D)),
        "wgate": t(f("L0_attn_w_gate").T),
        "wo": t(f("L0_attn_w_o").T),
        "wcomp": t(f("L0_attn_w_comp").reshape(D, CBS, D).transpose(2, 1, 0)),
        "wdq": t(f("L1_attn_W_DQ")),
        "wkvr": t(np.concatenate([f("L1_attn_W_DKV"), f("L1_attn_W_KR")], 1)),
        "uq": t(wuq.transpose(2, 1, 0)),
        "uk": t(wuk.transpose(2, 1, 0)),
        "uv": t(f("L1_attn_W_UV").reshape(DC, H1, DK).transpose(2, 1, 0)),
        "wO": t(f("L1_attn_W_O").reshape(H1, DK, D).transpose(1, 0, 2)),
        "qr": t(np.concatenate([f("L1_attn_W_QR"), f("L1_attn_b_QR")[None]], 0).reshape(KQ, H1, DR)),
        "gatew": t(f("L1_ffn_gate_w").T),
        "w1": t(f("L1_ffn_w1").transpose(2, 0, 1)),
        "w2": t(f("L1_ffn_w2").reshape(E, D, FC, P).transpose(3, 0, 2, 1)),
        "b2": t(f("L1_ffn_b2")),
    }


def kernel(**inputs):
    import concourse.bacc as _bacc
    from concourse.bass_utils import run_bass_kernel_spmd as _run

    nc = _bacc.Bacc("TRN2", target_bir_lowering=False, num_devices=1)
    arrays = {f"in_{k}_dram": a for k, a in lay_out(inputs).items()}
    dram = {k[3:-5]: nc.dram_tensor(k, a.shape, mybir.dt.from_np(a.dtype), kind="ExternalInput").ap()
            for k, a in arrays.items()}
    out = nc.dram_tensor("out_0_dram", (NB, S, D), F32, kind="ExternalOutput").ap()
    build(nc, dram, out)
    r = _run(nc, [arrays], core_ids=[0])
    return r.results[0]["out_0_dram"]
```

```python
import concourse.bass as bass
from concourse import mybir
from contextlib import ExitStack
import numpy as np

F32 = mybir.dt.float32
F32R = mybir.dt.float32r
U32 = mybir.dt.uint32
ALU = mybir.AluOpType
ACT = mybir.ActivationFunctionType
X = mybir.AxisListType.X

P = 128
NB, S, D = 8, 512, 128
T = S // P
EPS = 1e-5
NPROTO, RANK = 32, 16
PR = NPROTO * RANK // P
TINY = 2.0 ** -60
H0, HD0 = 16, 8
SCALE0 = HD0 ** -0.5
WIN = 32
CBS = 32
NCMP = S // CBS
SBS, TOPK = 64, 16
NSEL = S // SBS * TOPK
WK = P + 2 * WIN
PAD = WIN + S + (P - WIN)
SELT, CMPT = 2, 1
NSEG = T + SELT + CMPT
OSEL = T * WK
OCMP = OSEL + SELT * NSEL
NSC = OCMP + NCMP
NEG = -1e30
LOWEST = -3.4028234663852886e38
H1, DK, DC, DR = 8, 128, 32, 32
SCALE1 = (DK + DR) ** -0.5
KQ = DC + 1
KK = DC + DR + 1
KS = 3 * DC + 2
E, F = 8, 512
FC = F // P

C_ID, C_MASK = 0, P
C_IOTA = C_MASK + NSC
C_PCOL = C_IOTA + NPROTO
C_VALID = C_PCOL + 1
C_DELTA = C_VALID + NSEG
C_HALF = C_DELTA + 2 * T * 2 * TOPK
C_ONES = C_HALF + 2 * TOPK
NCONST = C_ONES + P
DELTA_W = 2 * TOPK

ROWS = [("bv", D), ("bg", 3), ("bo", D), ("gb", E), ("bdkv", DC), ("bO", D), ("bs", 1), ("temp", 1)]
ROW_AT = {}
_at = 0
for _name, _n in ROWS:
    ROW_AT[_name] = _at
    _at += _n
NROWS = _at

COLS = [("bq", 1), ("bk", 1), ("bvc", 1), ("bcomp", 1), ("b1", E * FC), ("buv", H1), ("bkr", 1), ("bdq", 1), ("ws", 1),
        ("qlow", 1), ("klow", 1)]
COL_AT = {}
_at = 0
for _name, _n in COLS:
    COL_AT[_name] = _at
    _at += _n
NCOLS = _at


def constants():
    c = np.zeros((P, NCONST), np.float32)
    c[:, C_ID:C_ID + P] = np.eye(P)
    mask = np.full((P, NSC), NEG, np.float32)
    for t in range(T):
        for p in range(P):
            i = t * P + p
            for w in range(WK):
                j = t * P - WIN + w
                if 0 <= j < S and i - WIN <= j < min(S, i + WIN + 1):
                    mask[p, t * WK + w] = 0
            if t < SELT:
                for j in range(NSEL):
                    if i - WIN <= j < min(S, i + WIN + 1):
                        mask[p, OSEL + t * NSEL + j] = 0
            if t < CMPT:
                for j in range(NCMP):
                    if i - WIN <= j < min(S, i + WIN + 1):
                        mask[p, OCMP + j] = 0
    c[:, C_MASK:C_MASK + NSC] = mask
    c[:, C_IOTA:C_IOTA + NPROTO] = np.arange(NPROTO)
    c[:, C_PCOL] = np.arange(P)
    c[:, C_VALID:C_VALID + T] = 1
    for t in range(SELT):
        c[:, C_VALID + T + t] = (mask[:, OSEL + t * NSEL:OSEL + (t + 1) * NSEL] == 0).any(1)
    c[:, C_VALID + T + SELT] = (mask[:, OCMP:] == 0).any(1)
    for j in range(2 * T):
        c[j, C_DELTA + j * DELTA_W:C_DELTA + (j + 1) * DELTA_W] = 1
    c[:, C_HALF + TOPK:C_HALF + 2 * TOPK] = SBS
    c[:, C_ONES:] = 1
    return c


def segment(i):
    if i < T:
        return i * WK, WK
    if i < T + SELT:
        return OSEL + (i - T) * NSEL, NSEL
    return OCMP, NCMP


def build(nc, dram, out):
    with ExitStack() as ctx:
        def sb(name, shape, dt=F32):
            return ctx.enter_context(nc.sbuf_tensor(name, shape, dt))

        def sem(name):
            return ctx.enter_context(nc.semaphore(name))

        const = sb("const", [P, NCONST])
        rows = sb("rows", [P, NROWS])
        cols = sb("cols", [P, NCOLS])
        proto = sb("proto", [P, NPROTO])
        pB = sb("pB", [P, NPROTO * RANK])
        pA = sb("pA", [P, PR, D])
        pbias = sb("pbias", [NPROTO, D])
        wqkv = sb("wqkv", [P, 3, D])
        wcomp = sb("wcomp", [P, CBS, D])
        wgate = sb("wgate", [P, 3])
        wo = sb("wo", [P, D])
        wdq = sb("wdq", [P, 3, DC])
        wkvr = sb("wkvr", [P, DC + DR])
        qr = sb("qr", [DC + DR, H1, KQ])
        gatew = sb("gatew", [P, E])
        w1 = sb("w1", [P, E, F])
        w2 = sb("w2", [P, E, FC, D])
        b2 = sb("b2", [E, D])
        ws8 = sb("ws8", [P, 2 * T, 2 * T])
        protosq = sb("protosq", [P, NPROTO])
        p2b = sb("p2b", [P, NPROTO])
        ninvt = sb("ninvt", [P, 2])
        qk = sb("qk", [P, H1, KS])
        vo = sb("vo", [P, 2, D])
        bOb = sb("bOb", [P, D])
        xin = sb("xin", [P, T, D])
        x = sb("x", [P, T, D])
        stats = sb("stats", [P, T, 6])
        mv = sb("mv", [P, T, 2])
        var = sb("var", [P, T])
        lnv = sb("lnv", [P, T])
        rstd0 = sb("rstd0", [P, T])
        nt = sb("nt", [P, T])
        rstd = sb("rstd", [P, T])
        xn = sb("xn", [P, T, D])
        xnT = sb("xnT", [P, PAD])
        sqjunk = sb("sqjunk", [P, D])
        x2 = sb("x2", [P, T])
        d2 = sb("d2", [P, T, NPROTO])
        lnd = sb("lnd", [P, T, NPROTO])
        root = sb("root", [P, T, NPROTO])
        quo = sb("quo", [P, T, NPROTO])
        low = sb("low", [P, T])
        prob = sb("prob", [P, T, NPROTO])
        top8 = sb("top8", [P, T, 8])
        idx8 = sb("idx8", [P, T, 8], U32)
        idxf = sb("idxf", [P, T, 2])
        den = sb("den", [P, T])
        rden = sb("rden", [P, T])
        wk = sb("wk", [P, T, 2])
        wa = sb("wa", [P, T, NPROTO])
        wb = sb("wb", [P, T, NPROTO])
        wsum = sb("wsum", [P, T, NPROTO])
        wT = sb("wT", [NPROTO, S])
        hw = sb("hw", [P, 2, NPROTO * RANK])
        hwT = sb("hwT", [P, 2, PR, P])
        qT = sb("qT", [P, S])
        kvT = sb("kvT", [P, 2, PAD])
        vs = sb("vs", [P, T + 1, D])
        gz = sb("gz", [P, T, 3])
        ge = sb("ge", [P, T, 3])
        gate = sb("gate", [P, T, 3])
        sc = sb("sc", [2 * T, P])
        sc2 = sb("sc2", [2 * T, P])
        sel8 = sb("sel8", [2 * T, 2, TOPK])
        seli = sb("seli", [2 * T, 2, TOPK], U32)
        self_ = sb("self", [2 * T, 2, TOPK])
        selx = sb("selx", [2 * T, 2 * T, DELTA_W])
        onehot = sb("onehot", [P, 2, T, DELTA_W])
        xsel = sb("xsel", [P, 2, NSEL])
        skT = sb("skT", [P, NSEL])
        sv = sb("sv", [P, D])
        ckv = sb("ckv", [P, 2, NCMP])
        cv = sb("cv", [NCMP, D])
        probs0 = sb("probs0", [P, NSC])
        nm0 = sb("nm0", [P, NSEG])
        sum0 = sb("sum0", [P, NSEG])
        rs0 = sb("rs0", [P, NSEG])
        coef = sb("coef", [P, NSEG])
        pTa = sb("pTa", [P, T, P])
        pTb = sb("pTb", [2 * WIN, T, P])
        pTs = sb("pTs", [P, SELT, P])
        pTc = sb("pTc", [NCMP, P])
        combT = sb("combT", [P, T, P])
        lg = sb("lg", [P, T, E])
        pm = sb("pm", [P, 2])
        gm = sb("gm", [2, 1])
        dg = sb("dg", [2, 2])
        nm1 = sb("nm1", [P, 2])
        ek = sb("ek", [P, 2, T])
        es = sb("es", [P, 2])
        rtot = sb("rtot", [P, 2])
        gk = sb("gk", [P, 2, T])
        ga = sb("ga", [P, T, E])
        gb = sb("gb", [P, T, E])
        g = sb("g", [P, T, E])
        gT = sb("gT", [E, S])
        cqT = sb("cqT", [3 * DC, S])
        cqR = sb("cqR", [3 * DC, S], F32R)
        cqs = sb("cqs", [KS, S], F32R)
        kT = sb("kT", [P, S])
        kR = sb("kR", [KS, S], F32R)
        ks = sb("ks", [KS, 2, S], F32R)
        ckt = sb("ckt", [P, T, DC])
        nm = sb("nm", [P, H1, T])
        rowsum = sb("rowsum", [P, H1, T])
        rrow = sb("rrow", [P, H1, T])
        oT = sb("oT", [P, 2, S])

        arena = sb("arena", [P, 5 * T * S])
        taken = [0]

        def part(*shape):
            n = int(np.prod(shape))
            view = arena[:, taken[0]:taken[0] + n]
            taken[0] += n
            names = "abc"[:len(shape)]
            return view.rearrange(f"p ({' '.join(names)}) -> p {' '.join(names)}", **dict(zip(names, shape)))

        uq, uk, uv, wO, buvb = part(H1, KQ), part(H1, KQ), part(H1, DC), part(H1, D), part(H1, P)
        taken[0] = 0
        hT = part(2, FC, S)
        taken[0] = 0
        probs, PT = part(3, T, S), part(2, T, S)

        ps = ctx.enter_context(nc.psum_tensor("ps", [P, 8, S], F32))

        weights_in = sem("weights_in")
        x_in, x_out = sem("x_in"), sem("x_out")
        x_ready = sem("x_ready")
        zeroed = sem("zeroed")
        setup_v, setup_p, setup_own, setup_done = sem("setup_v"), sem("setup_p"), sem("setup_own"), sem("setup_done")
        v_chain, a_chain = sem("v_chain"), sem("a_chain")
        var_ready, rstd0_ready, xn_ready = sem("var_ready"), sem("rstd0_ready"), sem("xn_ready")
        xnT_psum, xnT_ready = sem("xnT_psum"), sem("xnT_ready")
        x2_ready, dot_psum, d2_ready, root_ready = sem("x2_ready"), sem("dot_psum"), sem("d2_ready"), sem("root_ready")
        gap_ready, prob_ready, w_ready, wT_psum, wT_ready = (sem("gap_ready"), sem("prob_ready"), sem("w_ready"),
                                                             sem("wT_psum"), sem("wT_ready"))
        h_psum, hw_ready, hwT_psum, hwT_ready, py_psum = (sem("h_psum"), sem("hw_ready"), sem("hwT_psum"),
                                                          sem("hwT_ready"), sem("py_psum"))
        qkv_psum, q_ready, kv_ready, vs_psum, vs_ready = (sem("qkv_psum"), sem("q_ready"), sem("kv_ready"),
                                                          sem("vs_psum"), sem("vs_ready"))
        gz_ready, ge_ready = sem("gz_ready"), sem("ge_ready")
        score_psum, selx_ready, sel_psum, onehot_ready = (sem("score_psum"), sem("selx_ready"), sem("sel_psum"),
                                                          sem("onehot_ready"))
        comp_psum, comp_ready, cv_psum, cv_ready = sem("comp_psum"), sem("comp_ready"), sem("cv_psum"), sem("cv_ready")
        xsel_psum, xsel_ready, skv_psum, skv_ready = (sem("xsel_psum"), sem("xsel_ready"), sem("skv_psum"),
                                                      sem("skv_ready"))
        win_psum, selcmp_psum, nm0_ready, exp0_ready = (sem("win_psum"), sem("selcmp_psum"), sem("nm0_ready"),
                                                        sem("exp0_ready"))
        probs0_ready, pT_psum, pT_ready, pTb_ready = (sem("probs0_ready"), sem("pT_psum"), sem("pT_ready"),
                                                      sem("pTb_ready"))
        comb_psum, comb_ready, o_psum = sem("comb_psum"), sem("comb_ready"), sem("o_psum")
        lg_psum, pm_ready, pm_psum, dg_ready, mx_psum, nm1_ready = (sem("lg_psum"), sem("pm_ready"), sem("pm_psum"),
                                                                    sem("dg_ready"), sem("mx_psum"), sem("nm1_ready"))
        es_ready, tot_psum, g_ready, gT_psum, gT_ready, b2_psum, b2_used = (
            sem("es_ready"), sem("tot_psum"), sem("g_ready"), sem("gT_psum"), sem("gT_ready"), sem("b2_psum"),
            sem("b2_used"))
        mh_psum, mh_ready, my_psum, my_used = sem("mh_psum"), sem("mh_ready"), sem("my_psum"), sem("my_used")
        cq_psum, cq_ready, kr_psum, kr_ready, ckt_psum, ckt_ready = (
            sem("cq_psum"), sem("cq_ready"), sem("kr_psum"), sem("kr_ready"), sem("ckt_psum"), sem("ckt_ready"))
        kh_psum, kR_ready, ks_ready, s_psum, nm_ready, p_ready, rrow_ready, pn_ready = (
            sem("kh_psum"), sem("kR_ready"), sem("ks_ready"), sem("s_psum"), sem("nm_ready"), sem("p_ready"),
            sem("rrow_ready"), sem("pn_ready"))
        PT_psum, PTv_ready, PTa_ready = sem("PT_psum"), sem("PTv_ready"), sem("PTa_ready")
        pv_psum, oT_ready, mo_psum = sem("pv_psum"), sem("oT_ready"), sem("mo_psum")

        ident = const[:, C_ID:C_ID + P]
        ones = const[:, C_ONES:C_ONES + P]
        iota = const[:, C_IOTA:C_IOTA + NPROTO]

        def row(name):
            return rows[:, ROW_AT[name]:ROW_AT[name] + dict(ROWS)[name]]

        def col(name, k=0):
            return cols[:, COL_AT[name] + k:COL_AT[name] + k + 1]

        def over_tiles(ap, n):
            return ap.unsqueeze(1).to_broadcast([P, T, n])

        loads = [(const[:], dram["const"]), (proto[:], dram["proto"]), (pB[:], dram["pB"]), (pA[:], dram["pA"]),
                 (pbias[:], dram["pbias"]), (cols[:], dram["cols"]), (wqkv[:], dram["wqkv"]), (wgate[:], dram["wgate"]),
                 (wo[:], dram["wo"]), (wdq[:], dram["wdq"]), (wkvr[:], dram["wkvr"]), (uq[:], dram["uq"]),
                 (uk[:], dram["uk"]), (uv[:], dram["uv"]), (wO[:], dram["wO"]), (qr[DC:], dram["qr"]),
                 (gatew[:], dram["gatew"]), (b2[:], dram["b2"]), (wcomp[:], dram["wcomp"]), (w1[:], dram["w1"]),
                 (w2[:], dram["w2"])]
        NLOADS = len(loads) + 1

        xr = dram["x"].rearrange("b (t p) d -> b p t d", p=P)
        outr = out.rearrange("b (t p) d -> b p t d", p=P)

        block = ctx.enter_context(nc.Block())

        @block.sync
        def _(sp):
            sp.dma_start(xin[:], xr[0]).then_inc(x_in, 16)
            sp.dma_start(rows[:], dram["rows"].partition_broadcast(P)).then_inc(weights_in, 16)
            for dst, src in loads:
                sp.dma_start(dst, src).then_inc(weights_in, 16)
            with nc.sync.Fori(0, NB - 1) as b:
                sp.wait_ge(x_ready, 4 * b + 1)
                sp.dma_start(xin[:], xr[b + 1]).then_inc(x_in, 16)

        @block.gpsimd
        def _(pool):
            nc.gpsimd.memset(xnT[:], 0.0).then_inc(zeroed, 1)
            nc.gpsimd.memset(kvT[:], 0.0).then_inc(zeroed, 1)
            nc.gpsimd.memset(ws8[:], 0.0).then_inc(zeroed, 1)
            nc.gpsimd.memset(kT[:], 0.0).then_inc(zeroed, 1)
            nc.gpsimd.memset(qk[:], 0.0).then_inc(zeroed, 1)
            pool.wait_ge(zeroed, 5)
            nc.gpsimd.memset(cqs[3 * DC:KS].bitcast(F32), 1.0).then_inc(zeroed, 1)
            pool.wait_ge(zeroed, 6)
            nc.gpsimd.memset(kT[DC + DR:KK], 1.0).then_inc(zeroed, 1)
            pool.wait_ge(zeroed, 7)
            with nc.gpsimd.Fori(0, NB) as b:
                for h in range(H1):
                    pool.wait_ge(rrow_ready, H1 * b + h + 1)
                    nc.gpsimd.tensor_tensor(probs[:, h % 3, 0, :], probs[:, h % 3, 0, :],
                                            rrow[:, h, 0:1].to_broadcast([P, S]), ALU.mult)
                    for t in range(1, T):
                        i = nc.gpsimd.tensor_scalar(probs[:, h % 3, t, :], probs[:, h % 3, t, :], rrow[:, h, t:t + 1],
                                                    1.0, ALU.mult, ALU.mult)
                    i.then_inc(pn_ready, 1)
                pool.wait_ge(my_used, 2 * E * b + 2 * E)
                pool.dma_start(outr[b], x[:]).then_inc(x_out, 16)
            pool.wait_ge(x_out, 16 * NB)

        @block.tensor
        def _(pe):
            def mm(o, lhsT, rhs, start=True, stop=True):
                return pe.matmul(o, lhsT, rhs, start=start, stop=stop)

            def turn(o, in_):
                return pe.transpose(o, in_, const[0:in_.shape[0], C_ID:C_ID + in_.shape[0]])

            def setup():
                pe.wait_ge(weights_in, 16 * NLOADS)
                pe.wait_ge(setup_v, 1)
                mm(ps[:, 0, 0:NPROTO], ones, protosq[:]).then_inc(setup_p, 1)
                for h in range(H1):
                    m = mm(ps[0:KQ, 1, h * KQ:(h + 1) * KQ], uk[:, h, :], uq[:, h, :])
                m.then_inc(setup_p, 1)
                for h in range(H1):
                    a = DC * (h % 4)
                    m = mm(ps[a:a + DC, 2, (h // 4) * D:(h // 4 + 1) * D], uv[:, h, :], wO[:, h, :])
                m.then_inc(setup_p, 1)
                pe.wait_ge(setup_v, 2)
                for h in range(H1):
                    m = mm(ps[:, 3, 0:D], buvb[:, h, :], wO[:, h, :], h == 0, h == H1 - 1)
                m.then_inc(setup_p, 1)
                pe.wait_ge(setup_done, 1)

            def transpose_xn(b, s):
                pe.wait_ge(xn_ready, 6 * b + s + 1)
                for t in range(T):
                    m = turn(ps[:, 0, t * P:(t + 1) * P], xn[:, t, :])
                m.then_inc(xnT_psum, 1)
                pe.wait_ge(xnT_ready, 6 * b + s + 1)

            def xT(t):
                return xnT[:, WIN + t * P:WIN + (t + 1) * P]

            def proto_ffn(b, s, r):
                transpose_xn(b, s)
                for t in range(T):
                    m = mm(ps[:, 1, t * NPROTO:(t + 1) * NPROTO], xT(t), proto[:])
                m.then_inc(dot_psum, 1)
                for t in range(T):
                    mm(ps[:, 2 + t, :], xT(t), pB[:]).then_inc(h_psum, 1)
                pe.wait_ge(w_ready, 2 * b + r + 1)
                for t in range(T):
                    m = turn(ps[0:NPROTO, 7, t * P:(t + 1) * P], wsum[:, t, :])
                m.then_inc(wT_psum, 1)
                for t in range(T + 1):
                    if t < T:
                        pe.wait_ge(hw_ready, 8 * b + 4 * r + t + 1)
                        if t >= 2:
                            pe.wait_ge(hwT_ready, 8 * b + 4 * r + t - 1)
                        for c in range(PR):
                            m = turn(ps[:, t % 2, c * P:(c + 1) * P], hw[:, t % 2, c * P:(c + 1) * P])
                        m.then_inc(hwT_psum, 1)
                    if t == 0:
                        pe.wait_ge(wT_ready, 2 * b + r + 1)
                    if t >= 1:
                        u = t - 1
                        pe.wait_ge(hwT_ready, 8 * b + 4 * r + u + 1)
                        o = ps[:, 6, u * P:(u + 1) * P]
                        for c in range(PR):
                            mm(o, hwT[:, u % 2, c, :], pA[:, c, :], c == 0, False)
                        m = mm(o, wT[:, u * P:(u + 1) * P], pbias[:], False, True)
                m.then_inc(py_psum, 1)

            def nsa(b, s):
                transpose_xn(b, s)
                for j in range(3):
                    mm(ps[:, 1 + j, :], wqkv[:, j, :], xnT[:, WIN:WIN + S]).then_inc(qkv_psum, 1)
                for u in range(T + 1):
                    o = ps[:, 4, u * P:(u + 1) * P] if u < T else ps[:, 5, 0:P]
                    mm(o, xnT[:, u * P:(u + 1) * P], wqkv[:, 2, :])
                for t in range(T):
                    m = mm(ps[:, 5, P + 3 * t:P + 3 * t + 3], xT(t), wgate[:])
                m.then_inc(vs_psum, 1)
                pe.wait_ge(kv_ready, 2 * b + 2)
                for j in range(2 * T):
                    a = WIN + (j % T) * P
                    m = mm(ps[0:2 * T, 6, 0:P], ws8[:, j, :], kvT[:, j // T, a:a + P], j == 0, j == 2 * T - 1)
                m.then_inc(score_psum, 1)
                for c in range(CBS):
                    m = mm(ps[:, 7, 0:2 * NCMP], wcomp[:, c, :], kvT[:, :, WIN + c:WIN + S:CBS], c == 0, c == CBS - 1)
                m.then_inc(comp_psum, 1)
                pe.wait_ge(q_ready, b + 1)
                for t in range(T):
                    m = mm(ps[:, t // 2, (t % 2) * 256:(t % 2) * 256 + WK], qT[:, t * P:(t + 1) * P],
                           kvT[:, 0, t * P:t * P + WK])
                m.then_inc(win_psum, 1)
                pe.wait_ge(comp_ready, b + 1)
                turn(ps[0:NCMP, 2, 0:P], ckv[:, 1, :]).then_inc(cv_psum, 1)
                pe.wait_ge(selx_ready, b + 1)
                mm(ps[:, 6, 0:2 * T * DELTA_W], ones[0:2 * T, :], selx[:].rearrange("p a b -> p (a b)")).then_inc(sel_psum, 1)
                pe.wait_ge(onehot_ready, b + 1)
                for t in range(T):
                    o = ps[:, 7, 0:2 * NSEL].rearrange("p (k t j) -> p k t j", k=2, t=T)[:, :, t, :]
                    m = mm(o, xn[:, t, :], onehot[:, :, t, :])
                m.then_inc(xsel_psum, 1)
                pe.wait_ge(xsel_ready, b + 1)
                mm(ps[:, 6, 0:NSEL], wqkv[:, 1, :], xsel[:, 0, :])
                mm(ps[:, 6, P:2 * P], xsel[:, 1, :], wqkv[:, 2, :]).then_inc(skv_psum, 1)
                pe.wait_ge(skv_ready, b + 1)
                for t in range(SELT):
                    mm(ps[:, 7, t * NSEL:(t + 1) * NSEL], qT[:, t * P:(t + 1) * P], skT[:])
                mm(ps[:, 7, SELT * NSEL:SELT * NSEL + NCMP], qT[:, 0:P], ckv[:, 0, :]).then_inc(selcmp_psum, 1)
                pe.wait_ge(probs0_ready, b + 1)
                pe.wait_ge(cv_ready, b + 1)
                for t in range(T):
                    m = turn(ps[:, 2, t * P:(t + 1) * P], probs0[:, t * WK:t * WK + P])
                m.then_inc(pT_psum, 1)
                for t in range(T):
                    m = turn(ps[0:2 * WIN, 3, t * P:(t + 1) * P], probs0[:, t * WK + P:(t + 1) * WK])
                m.then_inc(pT_psum, 1)
                for t in range(SELT):
                    turn(ps[:, 4, t * P:(t + 1) * P], probs0[:, OSEL + t * NSEL:OSEL + (t + 1) * NSEL])
                turn(ps[0:NCMP, 4, SELT * P:(SELT + 1) * P], probs0[:, OCMP:OCMP + NCMP]).then_inc(pT_psum, 1)
                pe.wait_ge(pT_ready, 2 * b + 2)
                pe.wait_ge(pTb_ready, b + 1)
                for t in range(T):
                    o = ps[:, 5, t * P:(t + 1) * P]
                    mm(o, vs[:, t, :], pTa[:, t, :], True, False)
                    m = mm(o, vs[0:2 * WIN, t + 1, :], pTb[:, t, :], False, t >= SELT)
                    if t < SELT:
                        m = mm(o, sv[:], pTs[:, t, :], False, t >= CMPT)
                    if t < CMPT:
                        m = mm(o, cv[:], pTc[:], False, True)
                m.then_inc(comb_psum, 1)
                pe.wait_ge(comb_ready, b + 1)
                for t in range(T):
                    m = mm(ps[:, 6, t * P:(t + 1) * P], combT[:, t, :], wo[:])
                m.then_inc(o_psum, 1)

            def moe(b, s, r):
                HN = E * FC
                transpose_xn(b, s)
                for t in range(T):
                    m = mm(ps[:, 1, t * E:(t + 1) * E], xT(t), gatew[:])
                m.then_inc(lg_psum, 1)

                def hidden(e):
                    for c in range(FC):
                        n = e * FC + c
                        if n >= 3:
                            pe.wait_ge(mh_ready, 2 * HN * b + HN * r + n - 2)
                        mm(ps[:, 2 + n % 3, :], w1[:, e, c * P:(c + 1) * P], xnT[:, WIN:WIN + S]).then_inc(mh_psum, 1)

                def down(e):
                    pe.wait_ge(mh_ready, 2 * HN * b + HN * r + (e + 1) * FC)
                    if e >= 2:
                        pe.wait_ge(my_used, 2 * E * b + E * r + e - 1)
                    for t in range(T):
                        for c in range(FC):
                            m = mm(ps[:, 6 + e % 2, t * P:(t + 1) * P], hT[:, e % 2, c, t * P:(t + 1) * P],
                                   w2[:, e, c, :], c == 0, c == FC - 1)
                    m.then_inc(my_psum, 1)

                hidden(0)
                pe.wait_ge(pm_ready, 2 * b + r + 1)
                turn(ps[0:2, 1, 0:P], pm[:]).then_inc(pm_psum, 1)
                hidden(1)
                pe.wait_ge(dg_ready, 2 * b + r + 1)
                mm(ps[:, 1, 0:2], ones[0:2, :], dg[:]).then_inc(mx_psum, 1)
                down(0)
                pe.wait_ge(es_ready, 2 * b + r + 1)
                mm(ps[:, 1, 0:2], ones, es[:]).then_inc(tot_psum, 1)
                down(1)
                hidden(2)
                pe.wait_ge(g_ready, 2 * b + r + 1)
                for t in range(T):
                    m = turn(ps[0:E, 5, t * P:(t + 1) * P], g[:, t, :])
                m.then_inc(gT_psum, 1)
                hidden(3)
                pe.wait_ge(gT_ready, 2 * b + r + 1)
                for t in range(T):
                    m = mm(ps[:, 0, t * P:(t + 1) * P], gT[:, t * P:(t + 1) * P], b2[:])
                m.then_inc(b2_psum, 1)
                down(2)
                for e in range(4, E):
                    hidden(e)
                    down(e - 1)
                down(E - 1)

            def mla(b, s):
                transpose_xn(b, s)
                mm(ps[0:3 * DC, 1, :], wdq[:].rearrange("p a b -> p (a b)"), xnT[:, WIN:WIN + S]).then_inc(cq_psum, 1)
                mm(ps[0:DC + DR, 2, :], wkvr[:], xnT[:, WIN:WIN + S]).then_inc(kr_psum, 1)
                for t in range(T):
                    m = mm(ps[:, 3, t * DC:(t + 1) * DC], xT(t), wkvr[:, 0:DC])
                m.then_inc(ckt_psum, 1)

                def keys(h):
                    if h == 0:
                        pe.wait_ge(cq_ready, b + 1)
                        pe.wait_ge(kr_ready, b + 1)
                        pe.wait_ge(ckt_ready, b + 1)
                    else:
                        pe.wait_ge(ks_ready, H1 * b + h)
                    mm(ps[0:KS, 1, :], qk[:, h, :], kT[:]).then_inc(kh_psum, 1)

                def scores(h, t):
                    n = h * T + t
                    if t == 0:
                        pe.wait_ge(ks_ready, H1 * b + h + 1)
                    if n >= 3:
                        pe.wait_ge(p_ready, H1 * T * b + n - 2)
                    mm(ps[:, 2 + n % 3, :], cqs[:, t * P:(t + 1) * P], ks[:, h % 2, :]).then_inc(s_psum, 1)

                def turn_probs(h, k):
                    if k == 0:
                        pe.wait_ge(pn_ready, H1 * b + h + 1)
                    if k == 0 and h > 0:
                        pe.wait_ge(PTv_ready, 3 * H1 * b + 3 * h)
                    if k == 1 and h > 0:
                        pe.wait_ge(PTa_ready, H1 * b + h)
                    if k >= 2:
                        pe.wait_ge(PTv_ready, 3 * H1 * b + 3 * h + k - 1)
                    for t in range(T):
                        m = turn(ps[:, 5 + k % 2, t * P:(t + 1) * P], probs[:, h % 3, t, k * P:(k + 1) * P])
                    m.then_inc(PT_psum, 1)

                def values(h, k):
                    if k == 0:
                        pe.wait_ge(PTv_ready, 3 * H1 * b + 3 * h + 3)
                        pe.wait_ge(PTa_ready, H1 * b + h + 1)
                    a = DC * (h % 4)
                    m = mm(ps[a:a + DC, 7 * (1 - h // 4), :], ckt[:, k, :], PT[:, h % 2, k, :], k == 0, k == T - 1)
                    if k == T - 1:
                        m.then_inc(pv_psum, 1)

                keys(0)
                for h in range(H1 + 3):
                    if h + 1 < H1:
                        keys(h + 1)
                    for t in range(T):
                        if h < H1:
                            scores(h, t)
                        if 2 <= h < H1 + 2:
                            turn_probs(h - 2, t)
                        if h >= 3:
                            values(h - 3, t)
                pe.wait_ge(oT_ready, 2 * b + 2)
                for t in range(T):
                    for c in range(2):
                        m = mm(ps[:, 1, t * P:(t + 1) * P], oT[:, c, t * P:(t + 1) * P], vo[:, c, :], c == 0, c == 1)
                m.then_inc(mo_psum, 1)

            setup()
            with nc.tensor.Fori(0, NB) as b:
                proto_ffn(b, 0, 0)
                nsa(b, 1)
                proto_ffn(b, 2, 1)
                moe(b, 3, 0)
                mla(b, 4)
                moe(b, 5, 1)

        @block.scalar
        def _(act):
            nc.scalar.preload_act_table_set("natural_log_exp_and_others")
            chained = [0]

            def link(b, ins):
                chained[0] += 1
                ins.then_inc(a_chain, 1)
                act.wait_ge(a_chain, chained[0])

            def transpose_xn(b, s):
                act.wait_ge(var_ready, 6 * b + s + 1)
                link(b, nc.scalar.activation(lnv[:], var[:], ACT.Ln))
                nc.scalar.activation(rstd0[:], lnv[:], ACT.Exp, scale=-0.5).then_inc(rstd0_ready, 1)
                act.wait_ge(xnT_psum, 6 * b + s + 1)
                nc.scalar.copy(xnT[:, WIN:WIN + S], ps[:, 0, :]).then_inc(xnT_ready, 1)

            def proto_ffn(b, s, r):
                transpose_xn(b, s)
                for t in range(T):
                    i = nc.scalar.activation(sqjunk[:], xn[:, t, :], ACT.Square, accum_out=x2[:, t:t + 1])
                    if t < T - 1:
                        link(b, i)
                i.then_inc(x2_ready, 1)
                act.wait_ge(d2_ready, 2 * b + r + 1)
                link(b, nc.scalar.activation(lnd[:], d2[:], ACT.Ln))
                nc.scalar.activation(root[:], lnd[:], ACT.Exp, scale=0.5).then_inc(root_ready, 1)
                act.wait_ge(gap_ready, 2 * b + r + 1)
                nc.scalar.activation(prob[:], quo[:], ACT.Exp, scale=ninvt[:, 1:2]).then_inc(prob_ready, 1)
                act.wait_ge(wT_psum, 2 * b + r + 1)
                nc.scalar.copy(wT[:], ps[0:NPROTO, 7, :]).then_inc(wT_ready, 1)
                for t in range(T):
                    act.wait_ge(hwT_psum, 8 * b + 4 * r + t + 1)
                    nc.scalar.copy(hwT[:, t % 2].rearrange("p c j -> p (c j)"), ps[:, t % 2, :]).then_inc(hwT_ready, 1)

            def nsa(b, s):
                transpose_xn(b, s)
                for j, bias in ((0, col("bk")), (1, col("bvc"))):
                    act.wait_ge(qkv_psum, 3 * b + 2 + j)
                    nc.scalar.activation(kvT[:, j, WIN:WIN + S], ps[:, 2 + j, :], ACT.Identity, bias=bias).then_inc(kv_ready, 1)
                act.wait_ge(gz_ready, b + 1)
                nc.scalar.activation(ge[:], gz[:], ACT.Exp, scale=-1.0).then_inc(ge_ready, 1)
                act.wait_ge(comp_psum, b + 1)
                nc.scalar.activation(ckv[:].rearrange("p k n -> p (k n)"), ps[:, 7, 0:2 * NCMP], ACT.Identity,
                                     bias=col("bcomp")).then_inc(comp_ready, 1)
                act.wait_ge(cv_psum, b + 1)
                nc.scalar.copy(cv[:], ps[0:NCMP, 2, 0:P]).then_inc(cv_ready, 1)
                act.wait_ge(xsel_psum, b + 1)
                nc.scalar.copy(xsel[:].rearrange("p k n -> p (k n)"), ps[:, 7, 0:2 * NSEL]).then_inc(xsel_ready, 1)
                act.wait_ge(nm0_ready, b + 1)
                for i in range(NSEG):
                    a, n = segment(i)
                    e = nc.scalar.activation(probs0[:, a:a + n], probs0[:, a:a + n], ACT.Exp, bias=nm0[:, i:i + 1],
                                             accum_out=sum0[:, i:i + 1])
                e.then_inc(exp0_ready, 1)
                act.wait_ge(pT_psum, 3 * b + 1)
                nc.scalar.copy(pTa[:].rearrange("p t q -> p (t q)"), ps[:, 2, :]).then_inc(pT_ready, 1)
                act.wait_ge(pT_psum, 3 * b + 3)
                nc.scalar.copy(pTs[:].rearrange("p t q -> p (t q)"), ps[:, 4, 0:SELT * P])
                nc.scalar.copy(pTc[:], ps[0:NCMP, 4, SELT * P:(SELT + 1) * P]).then_inc(pT_ready, 1)
                act.wait_ge(comb_psum, b + 1)
                nc.scalar.copy(combT[:].rearrange("p t q -> p (t q)"), ps[:, 5, :]).then_inc(comb_ready, 1)

            def moe(b, s, r):
                HN = E * FC
                transpose_xn(b, s)

                def hidden(e):
                    for c in range(FC):
                        n = e * FC + c
                        act.wait_ge(mh_psum, 2 * HN * b + HN * r + n + 1)
                        if c == 0 and e >= 2:
                            act.wait_ge(my_psum, 2 * E * b + E * r + e - 1)
                        nc.scalar.activation(hT[:, e % 2, c, :], ps[:, 2 + n % 3, :], ACT.Relu,
                                             bias=col("b1", n)).then_inc(mh_ready, 1)

                hidden(0)
                hidden(1)
                act.wait_ge(nm1_ready, 2 * b + r + 1)
                for k in range(2):
                    i = nc.scalar.activation(ek[:, k, :], top8[:, :, k], ACT.Exp, bias=nm1[:, k:k + 1],
                                             accum_out=es[:, k:k + 1])
                i.then_inc(es_ready, 1)
                hidden(2)
                act.wait_ge(gT_psum, 2 * b + r + 1)
                nc.scalar.copy(gT[:], ps[0:E, 5, :]).then_inc(gT_ready, 1)
                for e in range(3, E):
                    hidden(e)

            def mla(b, s):
                transpose_xn(b, s)
                act.wait_ge(kr_psum, b + 1)
                nc.scalar.activation(kT[0:DC + DR, :], ps[0:DC + DR, 2, :], ACT.Identity,
                                     bias=cols[0:DC + DR, COL_AT["bkr"]:COL_AT["bkr"] + 1]).then_inc(kr_ready, 1)

                def key_high(h):
                    act.wait_ge(kh_psum, H1 * b + h + 1)
                    if h > 0:
                        act.wait_ge(ks_ready, H1 * b + h)
                    nc.scalar.copy(kR[:], ps[0:KS, 1, :]).then_inc(kR_ready, 1)

                def soft(h):
                    for t in range(T):
                        n = h * T + t
                        act.wait_ge(nm_ready, H1 * T * b + n + 1)
                        if t == 0 and h >= 3:
                            act.wait_ge(PT_psum, H1 * T * b + (h - 2) * T)
                        nc.scalar.activation(probs[:, h % 3, t, :], ps[:, 2 + n % 3, :], ACT.Exp,
                                             bias=nm[:, h, t:t + 1], accum_out=rowsum[:, h, t:t + 1]).then_inc(p_ready, 1)

                key_high(0)
                for h in range(H1 + 2):
                    if h + 1 < H1:
                        key_high(h + 1)
                    if h < H1:
                        soft(h)
                    if h >= 2:
                        act.wait_ge(PT_psum, H1 * T * b + (h - 2) * T + T)
                        if h >= 4:
                            act.wait_ge(pv_psum, H1 * b + h - 3)
                        nc.scalar.copy(PT[:, h % 2, T - 1, :], ps[:, 5 + (T - 1) % 2, :]).then_inc(PTa_ready, 1)
                for c in range(2):
                    act.wait_ge(pv_psum, H1 * b + 4 * c + 4)
                    nc.scalar.copy(oT[:, c, :], ps[:, 7 * (1 - c), :]).then_inc(oT_ready, 1)

            with nc.scalar.Fori(0, NB) as b:
                nc.scalar.sem_clear(a_chain)
                proto_ffn(b, 0, 0)
                nsa(b, 1)
                proto_ffn(b, 2, 1)
                moe(b, 3, 0)
                mla(b, 4)
                moe(b, 5, 1)

        @block.vector
        def _(dve):
            chained = [0]

            def link(b, ins):
                chained[0] += 1
                ins.then_inc(v_chain, 1)
                dve.wait_ge(v_chain, chained[0])

            def setup():
                dve.wait_ge(weights_in, 16 * NLOADS)
                dve.wait_ge(zeroed, 7)
                done = [0]

                def then(ins):
                    done[0] += 1
                    ins.then_inc(setup_own, 1)
                    dve.wait_ge(setup_own, done[0])

                nc.vector.tensor_tensor(protosq[:], proto[:], proto[:], ALU.mult).then_inc(setup_v, 1)
                nc.vector.tensor_copy(buvb[:], cols[:, COL_AT["buv"]:COL_AT["buv"] + H1].unsqueeze(2).to_broadcast([P, H1, P])
                                      ).then_inc(setup_v, 1)
                nc.vector.tensor_copy(ws8[:].rearrange("p a b -> p (a b)")[:, ::2 * T + 1],
                                      col("ws").to_broadcast([P, 2 * T]))
                then(nc.vector.tensor_scalar(ninvt[:, 0:1], row("temp"), -1.0, None, ALU.mult))
                then(nc.vector.tensor_tensor(ninvt[:, 0:1], ninvt[:, 0:1], row("temp"), ALU.max))
                then(nc.vector.tensor_scalar(ninvt[:, 0:1], ninvt[:, 0:1], 0.1, -2.0, ALU.max, ALU.mult))
                then(nc.vector.reciprocal(ninvt[:, 1:2], ninvt[:, 0:1]))
                dve.wait_ge(setup_p, 1)
                nc.vector.tensor_copy(p2b[:], ps[:, 0, 0:NPROTO])
                dve.wait_ge(setup_p, 2)
                o = ps[0:KQ, 1, 0:H1 * KQ].rearrange("p (h k) -> p h k", h=H1)
                for dst, src in ((qk[0:DC], o[0:DC]), (qk[DC:DC + DR], qr[DC:]), (qk[DC + DR:KK], o[DC:KQ])):
                    for c in range(3):
                        nc.vector.tensor_scalar(dst[:, :, c * DC:(c + 1) * DC], src[:, :, 0:DC], SCALE1, None, ALU.mult)
                    for c in range(2):
                        nc.vector.tensor_scalar(dst[:, :, 3 * DC + c:3 * DC + c + 1], src[:, :, DC:KQ], SCALE1, None,
                                                ALU.mult)
                dve.wait_ge(setup_p, 3)
                nc.vector.tensor_copy(vo[:].rearrange("p c d -> p (c d)"), ps[:, 2, 0:2 * D])
                dve.wait_ge(setup_p, 4)
                then(nc.vector.tensor_tensor(bOb[:], ps[:, 3, 0:D], row("bO"), ALU.add))
                nc.vector.memset(nt[:], 0.0).then_inc(setup_done, 1)

            def layernorm(b, s, src):
                for t in range(T):
                    i = nc.vector.bn_stats(stats[:, t, :], src[:, t, :])
                link(b, i)
                for t in range(T):
                    i = nc.vector.bn_aggr(mv[:, t, :], stats[:, t, :])
                link(b, i)
                nc.vector.tensor_scalar(var[:], mv[:, :, 1], EPS, None, ALU.add).then_inc(var_ready, 1)
                dve.wait_ge(rstd0_ready, 6 * b + s + 1)
                link(b, nc.vector.tensor_tensor(nt[:], rstd0[:], rstd0[:], ALU.mult))
                link(b, nc.vector.tensor_tensor(nt[:], nt[:], var[:], ALU.mult))
                link(b, nc.vector.tensor_scalar(nt[:], nt[:], -0.5, 1.5, ALU.mult, ALU.add))
                link(b, nc.vector.tensor_tensor(rstd[:], nt[:], rstd0[:], ALU.mult))
                for t in range(T):
                    i = nc.vector.tensor_scalar(xn[:, t, :], src[:, t, :], mv[:, t, 0:1], rstd[:, t:t + 1],
                                                ALU.subtract, ALU.mult)
                i.then_inc(xn_ready, 1)

            def two_hot(b, first, second, total, weight, n):
                for t in range(T):
                    nc.vector.tensor_scalar(first[:, t, :], iota[:, 0:n], idxf[:, t, 0:1], weight(t, 0),
                                            ALU.is_equal, ALU.mult)
                    i = nc.vector.tensor_scalar(second[:, t, :], iota[:, 0:n], idxf[:, t, 1:2], weight(t, 1),
                                                ALU.is_equal, ALU.mult)
                link(b, i)
                return nc.vector.tensor_tensor(total[:], first[:], second[:], ALU.add)

            def proto_ffn(b, s, r, src):
                layernorm(b, s, src)
                dve.wait_ge(dot_psum, 2 * b + r + 1)
                link(b, nc.vector.scalar_tensor_tensor(
                    out=d2[:], in0=ps[:, 1, 0:T * NPROTO].rearrange("p (t n) -> p t n", t=T), scalar=-2.0,
                    in1=over_tiles(p2b[:], NPROTO), op0=ALU.mult, op1=ALU.add))
                dve.wait_ge(x2_ready, 2 * b + r + 1)
                link(b, nc.vector.tensor_tensor(d2[:], d2[:], x2[:].unsqueeze(2).to_broadcast([P, T, NPROTO]), ALU.add))
                nc.vector.tensor_scalar(d2[:], d2[:], 0.0, TINY, ALU.max, ALU.max).then_inc(d2_ready, 1)
                dve.wait_ge(root_ready, 2 * b + r + 1)
                link(b, nc.vector.reciprocal(quo[:], root[:]))
                link(b, nc.vector.tensor_tensor(quo[:], quo[:], d2[:], ALU.mult))
                link(b, nc.vector.tensor_tensor(quo[:], quo[:], root[:], ALU.add))
                link(b, nc.vector.tensor_reduce(low[:], quo[:], X, ALU.min))
                nc.vector.tensor_tensor(quo[:], quo[:], low[:].unsqueeze(2).to_broadcast([P, T, NPROTO]),
                                        ALU.subtract).then_inc(gap_ready, 1)
                dve.wait_ge(prob_ready, 2 * b + r + 1)
                nc.vector.memset(wk[:], 0.0)
                for t in range(T):
                    i = nc.vector.max(top8[:, t, :], prob[:, t, :])
                link(b, i)
                for t in range(T):
                    nc.vector.max_index(idx8[:, t, :], top8[:, t, :], prob[:, t, :])
                link(b, nc.vector.tensor_tensor(den[:], top8[:, :, 0], top8[:, :, 1], ALU.add))
                nc.vector.tensor_copy(idxf[:], idx8[:, :, 0:2])
                link(b, nc.vector.reciprocal(rden[:], den[:]))
                link(b, nc.vector.scalar_tensor_tensor(out=wk[:], in0=top8[:, :, 0:2], scalar=0.5,
                                                       in1=rden[:].unsqueeze(2).to_broadcast([P, T, 2]),
                                                       op0=ALU.mult, op1=ALU.mult))
                two_hot(b, wa, wb, wsum, lambda t, k: wk[:, t, k:k + 1], NPROTO).then_inc(w_ready, 1)
                dve.wait_ge(w_ready, 2 * b + r + 1)
                for t in range(T):
                    dve.wait_ge(h_psum, 8 * b + 4 * r + t + 1)
                    if t >= 2:
                        dve.wait_ge(hwT_psum, 8 * b + 4 * r + t - 1)
                    nc.vector.tensor_tensor(hw[:, t % 2].rearrange("p (n j) -> p n j", j=RANK),
                                            ps[:, 2 + t, :].rearrange("p (n j) -> p n j", j=RANK),
                                            wsum[:, t, :].unsqueeze(2).to_broadcast([P, NPROTO, RANK]),
                                            ALU.mult).then_inc(hw_ready, 1)
                dve.wait_ge(py_psum, 2 * b + r + 1)
                if s == 0:
                    dve.wait_ge(x_out, 16 * b)
                nc.vector.tensor_tensor(x[:].rearrange("p t d -> p (t d)"), ps[:, 6, :],
                                        src[:].rearrange("p t d -> p (t d)"), ALU.add).then_inc(x_ready, 1)
                dve.wait_ge(x_ready, 4 * b + s + 1)

            def topk(b):
                link(b, nc.vector.tensor_scalar(sc[:], ps[0:2 * T, 6, 0:P], rows[0:2 * T, ROW_AT["bs"]:ROW_AT["bs"] + 1],
                                                None, ALU.add))
                blk = [slice(h * SBS, (h + 1) * SBS) for h in range(2)]
                for h in range(2):
                    i = nc.vector.max(sel8[:, h, 0:8], sc[:, blk[h]])
                link(b, i)
                for h in range(2):
                    nc.vector.max_index(seli[:, h, 0:8], sel8[:, h, 0:8], sc[:, blk[h]])
                    i = nc.vector.match_replace(sc2[:, blk[h]], sel8[:, h, 0:8], sc[:, blk[h]], LOWEST)
                link(b, i)
                for h in range(2):
                    i = nc.vector.max(sel8[:, h, 8:16], sc2[:, blk[h]])
                link(b, i)
                for h in range(2):
                    i = nc.vector.max_index(seli[:, h, 8:16], sel8[:, h, 8:16], sc2[:, blk[h]])
                link(b, i)
                link(b, nc.vector.tensor_copy(self_[:], seli[:]))
                link(b, nc.vector.tensor_tensor(self_[:].rearrange("p a b -> p (a b)"), self_[:].rearrange("p a b -> p (a b)"),
                                                const[0:2 * T, C_HALF:C_HALF + DELTA_W], ALU.add))
                nc.vector.tensor_tensor(
                    selx[:], self_[:].rearrange("p a b -> p (a b)").unsqueeze(1).to_broadcast([2 * T, 2 * T, DELTA_W]),
                    const[0:2 * T, C_DELTA:C_DELTA + 2 * T * DELTA_W].rearrange("p (a b) -> p a b", a=2 * T),
                    ALU.mult).then_inc(selx_ready, 1)

            def nsa(b, s):
                layernorm(b, s, x)
                dve.wait_ge(qkv_psum, 3 * b + 1)
                nc.vector.tensor_scalar(qT[:], ps[:, 1, :], col("bq"), None, ALU.add).then_inc(q_ready, 1)
                dve.wait_ge(vs_psum, b + 1)
                nc.vector.tensor_tensor(vs[:, 0:T, :], ps[:, 4, :].rearrange("p (t d) -> p t d", t=T),
                                        over_tiles(row("bv"), D), ALU.add)
                nc.vector.tensor_tensor(gz[:], ps[:, 5, P:P + 3 * T].rearrange("p (t n) -> p t n", t=T),
                                        over_tiles(row("bg"), 3), ALU.add).then_inc(gz_ready, 1)
                nc.vector.tensor_tensor(vs[:, T, :], ps[:, 5, 0:P], row("bv"), ALU.add).then_inc(vs_ready, 1)
                dve.wait_ge(score_psum, b + 1)
                topk(b)
                dve.wait_ge(ge_ready, b + 1)
                link(b, nc.vector.tensor_scalar(ge[:], ge[:], 1.0, None, ALU.add))
                link(b, nc.vector.reciprocal(gate[:], ge[:]))
                dve.wait_ge(win_psum, b + 1)
                for j in range(2):
                    a = 2 * j * WK
                    i = nc.vector.scalar_tensor_tensor(
                        out=probs0[:, a:a + 2 * WK].rearrange("p (t k) -> p t k", t=2),
                        in0=ps[:, j, :].rearrange("p (t k) -> p t k", t=2)[:, :, 0:WK], scalar=SCALE0,
                        in1=const[:, C_MASK + a:C_MASK + a + 2 * WK].rearrange("p (t k) -> p t k", t=2),
                        op0=ALU.mult, op1=ALU.add)
                link(b, i)
                nc.vector.tensor_reduce(nm0[:, 0:T], probs0[:, 0:T * WK].rearrange("p (t k) -> p t k", t=T), X, ALU.max,
                                        negate=True)
                dve.wait_ge(sel_psum, b + 1)
                nc.vector.tensor_scalar(onehot[:].rearrange("p k t j -> p (k t j)"), ps[:, 6, 0:2 * T * DELTA_W],
                                        const[:, C_PCOL:C_PCOL + 1], None, ALU.is_equal).then_inc(onehot_ready, 1)
                dve.wait_ge(skv_psum, b + 1)
                nc.vector.tensor_scalar(skT[:], ps[:, 6, 0:NSEL], col("bk"), None, ALU.add)
                nc.vector.tensor_tensor(sv[:], ps[:, 6, P:2 * P], row("bv"), ALU.add).then_inc(skv_ready, 1)
                dve.wait_ge(selcmp_psum, b + 1)
                link(b, nc.vector.scalar_tensor_tensor(
                    out=probs0[:, OSEL:NSC], in0=ps[:, 7, 0:NSC - OSEL], scalar=SCALE0,
                    in1=const[:, C_MASK + OSEL:C_MASK + NSC], op0=ALU.mult, op1=ALU.add))
                nc.vector.tensor_reduce(nm0[:, T:T + SELT], probs0[:, OSEL:OCMP].rearrange("p (t k) -> p t k", t=SELT),
                                        X, ALU.max, negate=True)
                nc.vector.tensor_reduce(nm0[:, T + SELT:NSEG], probs0[:, OCMP:NSC], X, ALU.max,
                                        negate=True).then_inc(nm0_ready, 1)
                dve.wait_ge(exp0_ready, b + 1)
                link(b, nc.vector.reciprocal(rs0[:], sum0[:]))
                nc.vector.tensor_tensor(coef[:, 0:T], rs0[:, 0:T], gate[:, :, 2], ALU.mult)
                nc.vector.tensor_tensor(coef[:, T:T + SELT], rs0[:, T:T + SELT], gate[:, 0:SELT, 1], ALU.mult)
                link(b, nc.vector.tensor_tensor(coef[:, T + SELT:NSEG], rs0[:, T + SELT:NSEG], gate[:, 0:CMPT, 0], ALU.mult))
                link(b, nc.vector.tensor_tensor(coef[:], coef[:], const[:, C_VALID:C_VALID + NSEG], ALU.mult))
                for k in range(NSEG):
                    a, n = segment(k)
                    i = nc.vector.tensor_scalar(probs0[:, a:a + n], probs0[:, a:a + n], coef[:, k:k + 1], None, ALU.mult)
                i.then_inc(probs0_ready, 1)
                dve.wait_ge(pT_psum, 3 * b + 2)
                nc.vector.tensor_copy(pTb[:].rearrange("p t q -> p (t q)"), ps[0:2 * WIN, 3, :]).then_inc(pTb_ready, 1)
                dve.wait_ge(o_psum, b + 1)
                link(b, nc.vector.tensor_tensor(x[:].rearrange("p t d -> p (t d)"), ps[:, 6, :],
                                                x[:].rearrange("p t d -> p (t d)"), ALU.add))
                nc.vector.tensor_tensor(x[:], x[:], over_tiles(row("bo"), D), ALU.add).then_inc(x_ready, 1)
                dve.wait_ge(x_ready, 4 * b + 2)

            def moe(b, s, r):
                layernorm(b, s, x)
                dve.wait_ge(lg_psum, 2 * b + r + 1)
                link(b, nc.vector.tensor_tensor(lg[:], ps[:, 1, 0:T * E].rearrange("p (t e) -> p t e", t=T),
                                                over_tiles(row("gb"), E), ALU.add))
                for t in range(T):
                    i = nc.vector.max(top8[:, t, :], lg[:, t, :])
                link(b, i)
                nc.vector.tensor_reduce(pm[:], top8[:, :, 0:2].rearrange("p t k -> p k t"), X, ALU.max).then_inc(pm_ready, 1)
                for t in range(T):
                    i = nc.vector.max_index(idx8[:, t, :], top8[:, t, :], lg[:, t, :])
                link(b, i)
                nc.vector.tensor_copy(idxf[:], idx8[:, :, 0:2])
                dve.wait_ge(pm_psum, 2 * b + r + 1)
                link(b, nc.vector.tensor_reduce(gm[:], ps[0:2, 1, 0:P], X, ALU.max))
                nc.vector.tensor_scalar(dg[:], const[0:2, C_ID:C_ID + 2], gm[:], None, ALU.mult).then_inc(dg_ready, 1)
                dve.wait_ge(mx_psum, 2 * b + r + 1)
                nc.vector.tensor_scalar(nm1[:], ps[:, 1, 0:2], -1.0, None, ALU.mult).then_inc(nm1_ready, 1)
                dve.wait_ge(tot_psum, 2 * b + r + 1)
                link(b, nc.vector.reciprocal(rtot[:], ps[:, 1, 0:2]))
                link(b, nc.vector.scalar_tensor_tensor(out=gk[:], in0=ek[:], scalar=0.5,
                                                       in1=rtot[:].unsqueeze(2).to_broadcast([P, 2, T]),
                                                       op0=ALU.mult, op1=ALU.mult))
                two_hot(b, ga, gb, g, lambda t, k: gk[:, k, t:t + 1], E).then_inc(g_ready, 1)
                dve.wait_ge(g_ready, 2 * b + r + 1)
                for e in range(E):
                    dve.wait_ge(my_psum, 2 * E * b + E * r + e + 1)
                    for t in range(T):
                        i = nc.vector.scalar_tensor_tensor(
                            out=x[:, t, :], in0=ps[:, 6 + e % 2, t * P:(t + 1) * P], scalar=g[:, t, e:e + 1],
                            in1=x[:, t, :], op0=ALU.mult, op1=ALU.add)
                    i.then_inc(my_used, 1)
                    if s < 5 or e < E - 1:
                        dve.wait_ge(my_used, 2 * E * b + E * r + e + 1)
                    if e == 2:
                        dve.wait_ge(b2_psum, 2 * b + r + 1)
                        link(b, nc.vector.tensor_tensor(x[:].rearrange("p t d -> p (t d)"), ps[:, 0, :],
                                                        x[:].rearrange("p t d -> p (t d)"), ALU.add))

            def mla(b, s):
                layernorm(b, s, x)
                dve.wait_ge(cq_psum, b + 1)
                link(b, nc.vector.tensor_scalar(cqT[:], ps[0:3 * DC, 1, :], cols[0:3 * DC, COL_AT["bdq"]:COL_AT["bdq"] + 1],
                                                None, ALU.add))
                link(b, nc.vector.tensor_copy(cqR[:], cqT[:]))
                nc.vector.scalar_tensor_tensor(out=cqs[0:3 * DC], in0=cqR[:].bitcast(F32),
                                               scalar=cols[0:3 * DC, COL_AT["qlow"]:COL_AT["qlow"] + 1], in1=cqT[:],
                                               op0=ALU.mult, op1=ALU.add).then_inc(cq_ready, 1)
                dve.wait_ge(ckt_psum, b + 1)
                nc.vector.tensor_tensor(ckt[:], ps[:, 3, 0:T * DC].rearrange("p (t n) -> p t n", t=T),
                                        over_tiles(row("bdkv"), DC), ALU.add).then_inc(ckt_ready, 1)

                def key_stack(h):
                    dve.wait_ge(kR_ready, H1 * b + h + 1)
                    nc.vector.scalar_tensor_tensor(out=ks[:, h % 2, :], in0=kR[:].bitcast(F32),
                                                   scalar=cols[0:KS, COL_AT["klow"]:COL_AT["klow"] + 1],
                                                   in1=ps[0:KS, 1, :], op0=ALU.mult, op1=ALU.add).then_inc(ks_ready, 1)

                def row_max(h, t):
                    n = h * T + t
                    dve.wait_ge(s_psum, H1 * T * b + n + 1)
                    nc.vector.tensor_reduce(nm[:, h, t:t + 1], ps[:, 2 + n % 3, :], X, ALU.max,
                                            negate=True).then_inc(nm_ready, 1)

                def row_sum(h):
                    dve.wait_ge(p_ready, H1 * T * b + (h + 1) * T)
                    nc.vector.reciprocal(rrow[:, h, :], rowsum[:, h, :]).then_inc(rrow_ready, 1)

                def turned(h, k):
                    dve.wait_ge(PT_psum, H1 * T * b + h * T + k + 1)
                    if k == 0 and h >= 2:
                        dve.wait_ge(pv_psum, H1 * b + h - 1)
                    nc.vector.tensor_copy(PT[:, h % 2, k, :], ps[:, 5 + k % 2, :]).then_inc(PTv_ready, 1)

                key_stack(0)
                for h in range(H1 + 2):
                    for t in range(T):
                        if h < H1:
                            row_max(h, t)
                        if t == 0 and h + 1 < H1:
                            key_stack(h + 1)
                        if t == 0 and 1 <= h <= H1:
                            row_sum(h - 1)
                        if t < T - 1 and h >= 2:
                            turned(h - 2, t)
                dve.wait_ge(mo_psum, b + 1)
                link(b, nc.vector.tensor_tensor(x[:].rearrange("p t d -> p (t d)"), ps[:, 1, :],
                                                x[:].rearrange("p t d -> p (t d)"), ALU.add))
                nc.vector.tensor_tensor(x[:], x[:], over_tiles(bOb[:], D), ALU.add).then_inc(x_ready, 1)
                dve.wait_ge(x_ready, 4 * b + 4)

            setup()
            with nc.vector.Fori(0, NB) as b:
                nc.vector.sem_clear(v_chain)
                dve.wait_ge(x_in, 16 * b + 16)
                proto_ffn(b, 0, 0, xin)
                nsa(b, 1)
                proto_ffn(b, 2, 1, x)
                moe(b, 3, 0)
                mla(b, 4)
                moe(b, 5, 1)


def lay_out(i):
    def f(name):
        return np.asarray(i[name])

    def t(a):
        return np.ascontiguousarray(a)

    wqkv = f("L0_attn_w_qkv").reshape(H0, 3, HD0, D)
    bqkv = f("L0_attn_b_qkv").reshape(H0, 3, HD0).transpose(1, 0, 2).reshape(3, D)
    buq = f("L1_attn_b_UQ").reshape(H1, DK)
    bukh = f("L1_attn_b_UK").reshape(H1, DK)
    parts = {"bv": bqkv[2], "bg": f("L0_attn_b_gate"), "bo": f("L0_attn_b_o"), "gb": f("L1_ffn_gate_b"),
             "bdkv": f("L1_attn_b_DKV"), "bO": f("L1_attn_b_O"), "bs": f("L0_attn_b_score"),
             "temp": f("L0_ffn_temp").reshape(1)}
    cols = np.zeros((P, NCOLS), np.float32)

    def put(name, a):
        cols[:a.shape[0], COL_AT[name]:COL_AT[name] + a.shape[1]] = a

    put("bq", bqkv[0][:, None])
    put("bk", bqkv[1][:, None])
    put("bvc", bqkv[2][:, None])
    put("bcomp", f("L0_attn_b_comp")[:, None])
    put("b1", f("L1_ffn_b1").reshape(E * FC, P).T)
    put("buv", f("L1_attn_b_UV").reshape(H1, DK).T)
    put("bkr", np.concatenate([f("L1_attn_b_DKV"), f("L1_attn_b_KR")])[:, None])
    put("bdq", np.concatenate([f("L1_attn_b_DQ")] * 3)[:, None])
    cols[DC:2 * DC, COL_AT["qlow"]] = -1
    cols[2 * DC:3 * DC, COL_AT["klow"]] = -1
    cols[KS - 1, COL_AT["klow"]] = -1
    put("ws", f("L0_attn_w_score").T)
    wuq = np.concatenate([f("L1_attn_W_UQ").reshape(DC, H1, DK), buq[None]], 0)
    wuk = np.concatenate([f("L1_attn_W_UK").reshape(DC, H1, DK), bukh[None]], 0)
    return {
        "x": t(f("L0_attn_x")),
        "const": constants(),
        "rows": t(np.concatenate([parts[n] for n, _ in ROWS])),
        "cols": cols,
        "proto": t(f("L0_ffn_prototypes").T),
        "pB": t(f("L0_ffn_B").reshape(NPROTO * RANK, D).T),
        "pA": t(f("L0_ffn_A").transpose(0, 2, 1).reshape(PR, P, D).transpose(1, 0, 2)),
        "pbias": t(f("L0_ffn_bias")),
        "wqkv": t(wqkv.transpose(3, 1, 0, 2).reshape(D, 3, D)),
        "wgate": t(f("L0_attn_w_gate").T),
        "wo": t(f("L0_attn_w_o").T),
        "wcomp": t(f("L0_attn_w_comp").reshape(D, CBS, D).transpose(2, 1, 0)),
        "wdq": t(np.stack([f("L1_attn_W_DQ")] * 3, 1)),
        "wkvr": t(np.concatenate([f("L1_attn_W_DKV"), f("L1_attn_W_KR")], 1)),
        "uq": t(wuq.transpose(2, 1, 0)),
        "uk": t(wuk.transpose(2, 1, 0)),
        "uv": t(f("L1_attn_W_UV").reshape(DC, H1, DK).transpose(2, 1, 0)),
        "wO": t(f("L1_attn_W_O").reshape(H1, DK, D).transpose(1, 0, 2)),
        "qr": t(np.concatenate([f("L1_attn_W_QR"), f("L1_attn_b_QR")[None]], 0).reshape(KQ, H1, DR).transpose(2, 1, 0)),
        "gatew": t(f("L1_ffn_gate_w").T),
        "w1": t(f("L1_ffn_w1").transpose(2, 0, 1)),
        "w2": t(f("L1_ffn_w2").reshape(E, D, FC, P).transpose(3, 0, 2, 1)),
        "b2": t(f("L1_ffn_b2")),
    }


def kernel(**inputs):
    import concourse.bacc as _bacc
    from concourse.bass_utils import run_bass_kernel_spmd as _run

    nc = _bacc.Bacc("TRN2", target_bir_lowering=False, num_devices=1)
    arrays = {f"in_{k}_dram": a for k, a in lay_out(inputs).items()}
    dram = {k[3:-5]: nc.dram_tensor(k, a.shape, mybir.dt.from_np(a.dtype), kind="ExternalInput").ap()
            for k, a in arrays.items()}
    out = nc.dram_tensor("out_0_dram", (NB, S, D), F32, kind="ExternalOutput").ap()
    build(nc, dram, out)
    r = _run(nc, [arrays], core_ids=[0])
    return r.results[0]["out_0_dram"]
```

```python
import concourse.bass as bass
from concourse import mybir
from contextlib import ExitStack
import numpy as np

F32 = mybir.dt.float32
F32R = mybir.dt.float32r
U32 = mybir.dt.uint32
ALU = mybir.AluOpType
ACT = mybir.ActivationFunctionType
X = mybir.AxisListType.X

P = 128
NB, S, D = 8, 512, 128
T = S // P
EPS = 1e-5
NPROTO, RANK = 32, 16
PR = NPROTO * RANK // P
TINY = 2.0 ** -60
H0, HD0 = 16, 8
SCALE0 = HD0 ** -0.5
WIN = 32
CBS = 32
NCMP = S // CBS
SBS, TOPK = 64, 16
NSEL = S // SBS * TOPK
WK = P + 2 * WIN
PAD = WIN + S + (P - WIN)
SELT, CMPT = 2, 1
NSEG = T + SELT + CMPT
OSEL = T * WK
OCMP = OSEL + SELT * NSEL
NSC = OCMP + NCMP
NEG = -1e30
LOWEST = -3.4028234663852886e38
H1, DK, DC, DR = 8, 128, 32, 32
SCALE1 = (DK + DR) ** -0.5
KQ = DC + 1
KK = DC + DR + 1
KS = 3 * DC + 2
E, F = 8, 512
FC = F // P

GS = 2 * E

LIGHT_STEPS = 9 + 19 + 17 + 8
PACE = [(0, 0), (3, 2), (14, 7), (22, 12), (28, 17), (38, 22), (50, 26), (62, 31), (72, 36), (77, 41), (86, 47), (96, 53)]
NSA_AT = 9
SETUP_AT = 34


def light_due(k):
    return min(int(np.interp(k + 1, *zip(*PACE))), LIGHT_STEPS)


def gated_expert(u):
    if u == 5:
        return 0
    if u >= 6 and u % 2 == 0:
        return u // 2 - 2
    return None


def spread_expert(u):
    if u in (5, 6):
        return u - 5
    if u >= 7 and u % 2 == 1:
        e = (u - 3) // 2
        return e if e < E else None
    return None

C_ID, C_MASK = 0, P
C_IOTA = C_MASK + NSC
C_PCOL = C_IOTA + NPROTO
C_VALID = C_PCOL + 1
C_DELTA = C_VALID + NSEG
C_HALF = C_DELTA + 2 * T * 2 * TOPK
C_ONES = C_HALF + 2 * TOPK
NCONST = C_ONES + P
DELTA_W = 2 * TOPK

ROWS = [("bv", D), ("bg", 3), ("bo", D), ("gb", E), ("bdkv", DC), ("bO", D), ("bs", 1), ("temp", 1)]
ROW_AT = {}
_at = 0
for _name, _n in ROWS:
    ROW_AT[_name] = _at
    _at += _n
NROWS = _at

COLS = [("bq", 1), ("bk", 1), ("bvc", 1), ("bcomp", 1), ("b1", E * FC), ("buv", H1), ("bkr", 1), ("bdq", 1), ("ws", 1),
        ("qlow", 1), ("klow", 1)]
COL_AT = {}
_at = 0
for _name, _n in COLS:
    COL_AT[_name] = _at
    _at += _n
NCOLS = _at


def constants():
    c = np.zeros((P, NCONST), np.float32)
    c[:, C_ID:C_ID + P] = np.eye(P)
    mask = np.full((P, NSC), NEG, np.float32)
    for t in range(T):
        for p in range(P):
            i = t * P + p
            for w in range(WK):
                j = t * P - WIN + w
                if 0 <= j < S and i - WIN <= j < min(S, i + WIN + 1):
                    mask[p, t * WK + w] = 0
            if t < SELT:
                for j in range(NSEL):
                    if i - WIN <= j < min(S, i + WIN + 1):
                        mask[p, OSEL + t * NSEL + j] = 0
            if t < CMPT:
                for j in range(NCMP):
                    if i - WIN <= j < min(S, i + WIN + 1):
                        mask[p, OCMP + j] = 0
    c[:, C_MASK:C_MASK + NSC] = mask
    c[:, C_IOTA:C_IOTA + NPROTO] = np.arange(NPROTO)
    c[:, C_PCOL] = np.arange(P)
    c[:, C_VALID:C_VALID + T] = 1
    for t in range(SELT):
        c[:, C_VALID + T + t] = (mask[:, OSEL + t * NSEL:OSEL + (t + 1) * NSEL] == 0).any(1)
    c[:, C_VALID + T + SELT] = (mask[:, OCMP:] == 0).any(1)
    for j in range(2 * T):
        c[j, C_DELTA + j * DELTA_W:C_DELTA + (j + 1) * DELTA_W] = 1
    c[:, C_HALF + TOPK:C_HALF + 2 * TOPK] = SBS
    c[:, C_ONES:] = 1
    return c


def segment(i):
    if i < T:
        return i * WK, WK
    if i < T + SELT:
        return OSEL + (i - T) * NSEL, NSEL
    return OCMP, NCMP


def build(nc, dram, out):
    with ExitStack() as ctx:
        def sb(name, shape, dt=F32):
            return ctx.enter_context(nc.sbuf_tensor(name, shape, dt))

        def sem(name):
            return ctx.enter_context(nc.semaphore(name))

        const = sb("const", [P, NCONST])
        rows = sb("rows", [P, NROWS])
        cols = sb("cols", [P, NCOLS])
        proto = sb("proto", [P, NPROTO])
        pB = sb("pB", [P, NPROTO * RANK])
        pA = sb("pA", [P, PR, D])
        pbias = sb("pbias", [NPROTO, D])
        wqkv = sb("wqkv", [P, 3, D])
        wcomp = sb("wcomp", [P, CBS, D])
        wgate = sb("wgate", [P, 3])
        wo = sb("wo", [P, D])
        wdq = sb("wdq", [P, 3, DC])
        wkvr = sb("wkvr", [P, DC + DR])
        gatew = sb("gatew", [P, E])
        b2 = sb("b2", [GS, D])
        b2h, b2l = sb("b2h", [GS, D], F32R), sb("b2l", [GS, D], F32R)
        w1h, w1l = sb("w1h", [P, E, F], F32R), sb("w1l", [P, E, F], F32R)
        w2h, w2l = sb("w2h", [P, E, FC, D], F32R), sb("w2l", [P, E, FC, D], F32R)
        ws8 = sb("ws8", [P, 2 * T, 2 * T])
        protosq = sb("protosq", [P, NPROTO])
        p2b = sb("p2b", [P, NPROTO])
        ninvt = sb("ninvt", [P, 2])
        qk = sb("qk", [P, H1, KS])
        vo = sb("vo", [P, 2, D])
        bOb = sb("bOb", [P, D])
        gsel = sb("gsel", [GS, E], F32R)

        class Lane:
            def __init__(self, name):
                self.stats = sb(name + "stats", [P, T, 6])
                self.mv = sb(name + "mv", [P, T, 2])
                self.var = sb(name + "var", [P, T])
                self.lnv = sb(name + "lnv", [P, T])
                self.rstd0 = sb(name + "rstd0", [P, T])
                self.nt = sb(name + "nt", [P, T])
                self.rstd = sb(name + "rstd", [P, T])
                self.xn = sb(name + "xn", [P, T, D])
                self.top8 = sb(name + "top8", [P, T, 8])
                self.idx8 = sb(name + "idx8", [P, T, 8], U32)
                self.idxf = sb(name + "idxf", [P, T, 2])
                self.var_ready, self.rstd0_ready = sem(name + "var_ready"), sem(name + "rstd0_ready")
                self.xn_ready, self.xnT_psum = sem(name + "xn_ready"), sem(name + "xnT_psum")
                self.xnT_ready = sem(name + "xnT_ready")

        light, heavy = Lane("light_"), Lane("heavy_")
        light.xnT = sb("light_xnT", [P, PAD])
        heavy.xnT = sb("heavy_xnT", [P, S])
        light.bank, heavy.bank = 6, 0
        xin = sb("xin", [P, T, D])
        xl = sb("xl", [P, T, D])
        xh = sb("xh", [P, T, D])
        xout = sb("xout", [P, T, D])

        def arena(name, size):
            whole = sb(name, [P, size])
            taken = [0]

            def part(*shape, start=None):
                if start is not None:
                    taken[0] = start
                n = int(np.prod(shape))
                assert taken[0] + n <= size, (name, taken, n)
                view = whole[:, taken[0]:taken[0] + n]
                taken[0] += n
                names = "abc"[:len(shape)]
                return view.rearrange(f"p ({' '.join(names)}) -> p {' '.join(names)}", **dict(zip(names, shape)))
            return part, lambda: taken[0]

        part, here = arena("light_arena", 5720)
        x2, d2, lnd, root = part(T), part(T, NPROTO), part(T, NPROTO), part(T, NPROTO)
        quo, low, prob = part(T, NPROTO), part(T), part(T, NPROTO)
        den, rden, wk = part(T), part(T), part(T, 2)
        wa, wb, wsum = part(T, NPROTO), part(T, NPROTO), part(T, NPROTO)
        sqjunk, wT = part(D), part(S)[0:NPROTO]
        hw, hwT = part(2, NPROTO * RANK), part(2, PR, P)
        vs = part(T + 1, D, start=0)
        gz, ge, gate = part(T, 3), part(T, 3), part(T, 3)
        sc, sc2 = part(P)[0:2 * T], part(P)[0:2 * T]
        sel8, self_ = part(2, TOPK)[0:2 * T], part(2, TOPK)[0:2 * T]
        selx = part(2 * T, DELTA_W)[0:2 * T]
        onehot_at = here()
        onehot, xsel = part(2, T, DELTA_W), part(2, NSEL)
        pTa = combT = part(T, P, start=onehot_at)
        skT, sv, ckv = part(NSEL), part(D), part(2, NCMP)
        cv, probs0 = part(D)[0:NCMP], part(NSC)
        nm0, sum0, rs0, coef = part(NSEG), part(NSEG), part(NSEG), part(NSEG)
        pTb = part(T, P)[0:2 * WIN]
        pTs, pTc, qT = part(SELT, P), part(P)[0:NCMP], part(S)
        seli = sb("seli", [2 * T, 2, TOPK], U32)
        kvT = sb("kvT", [P, 2, PAD])

        with ExitStack() as start_only:
            w1 = start_only.enter_context(nc.sbuf_tensor("w1", [P, E, F], F32))
            w2 = start_only.enter_context(nc.sbuf_tensor("w2", [P, E, FC, D], F32))
            uq = start_only.enter_context(nc.sbuf_tensor("uq", [P, H1, KQ], F32))
            uk = start_only.enter_context(nc.sbuf_tensor("uk", [P, H1, KQ], F32))
            uv = start_only.enter_context(nc.sbuf_tensor("uv", [P, H1, DC], F32))
            wO = start_only.enter_context(nc.sbuf_tensor("wO", [P, H1, D], F32))
            qr = start_only.enter_context(nc.sbuf_tensor("qr", [P, H1, KQ], F32))
        with ExitStack() as mla_only:
            probs = mla_only.enter_context(nc.sbuf_tensor("probs", [P, 3, T, S], F32))
            PT = mla_only.enter_context(nc.sbuf_tensor("PT", [P, 2, T, S], F32))
            oT0 = mla_only.enter_context(nc.sbuf_tensor("oT0", [P, S], F32))
        hf = sb("hf", [P, 2, S])
        accT, gbs, prod = sb("accT", [P, S]), sb("gbs", [P, S]), sb("prod", [P, S])
        hh, hl = sb("hh", [P, 2, FC, S], F32R), sb("hl", [P, 2, FC, S], F32R)
        oT = oT0, sb("oT1", [P, S])
        xTh, xTl = sb("xTh", [P, S], F32R), sb("xTl", [P, S], F32R)
        lg = sb("lg", [P, T, E])
        pm, gm, dg, nm1 = sb("pm", [P, 2]), sb("gm", [2, 1]), sb("dg", [2, 2]), sb("nm1", [P, 2])
        ek, es, rtot, gk = sb("ek", [P, 2, T]), sb("es", [P, 2]), sb("rtot", [P, 2]), sb("gk", [P, 2, T])
        ga, gb, g = sb("ga", [P, T, E]), sb("gb", [P, T, E]), sb("g", [P, T, E])
        gR = sb("gR", [P, T, E], F32R)
        gs = sb("gs", [P, T, GS])
        gTr = sb("gTr", [GS, S], F32R)
        cqT, cqs = PT[0:3 * DC, 0, 0, :], sb("cqs", [KS, S], F32R)
        kT = sb("kT", [P, S])
        kR, ks = xTh[0:KS], sb("ks", [KS, 2, S], F32R)
        cqR = xTl[0:3 * DC]
        ckt = sb("ckt", [P, T, DC])
        nm, rowsum, rrow = sb("nm", [P, H1, T]), sb("rowsum", [P, H1, T]), sb("rrow", [P, H1, T])

        ps = ctx.enter_context(nc.psum_tensor("ps", [P, 8, S], F32))
        A, B = 6, 7

        first_in, nsa_in, heavy_in = sem("first_in"), sem("nsa_in"), sem("heavy_in")
        x_in, x_out = sem("x_in"), sem("x_out")
        xl_ready = sem("xl_ready")
        xh_copied = sem("xh_copied")
        xh_ready = sem("xh_ready")
        xout_ready = sem("xout_ready")
        bo_ready, bO_ready = sem("bo_ready"), sem("bO_ready")
        zeroed = sem("zeroed")
        setup_v, setup_p, setup_own, setup_done = sem("setup_v"), sem("setup_p"), sem("setup_own"), sem("setup_done")
        high_ready, low_ready = sem("high_ready"), sem("low_ready")
        v_chain, a_chain = sem("v_chain"), sem("a_chain")
        x2_ready, dot_psum, d2_ready, root_ready = sem("x2_ready"), sem("dot_psum"), sem("d2_ready"), sem("root_ready")
        gap_ready, prob_ready, w_ready, wT_psum, wT_ready = (sem("gap_ready"), sem("prob_ready"), sem("w_ready"),
                                                             sem("wT_psum"), sem("wT_ready"))
        h_psum, hw_ready, hwT_psum, hwT_ready, py_psum = (sem("h_psum"), sem("hw_ready"), sem("hwT_psum"),
                                                          sem("hwT_ready"), sem("py_psum"))
        q_psum, q_ready, kv_psum, kv_ready = sem("q_psum"), sem("q_ready"), sem("kv_psum"), sem("kv_ready")
        gz_psum, gz_ready, ge_ready, vs_psum, vs_ready = (sem("gz_psum"), sem("gz_ready"), sem("ge_ready"),
                                                          sem("vs_psum"), sem("vs_ready"))
        score_psum, selx_ready, sel_psum, onehot_ready = (sem("score_psum"), sem("selx_ready"), sem("sel_psum"),
                                                          sem("onehot_ready"))
        comp_psum, comp_ready, cv_psum, cv_ready = sem("comp_psum"), sem("comp_ready"), sem("cv_psum"), sem("cv_ready")
        xsel_psum, xsel_ready, skv_psum, skv_ready = (sem("xsel_psum"), sem("xsel_ready"), sem("skv_psum"),
                                                      sem("skv_ready"))
        win_psum, win_ready, selcmp_psum, nm0_ready, exp0_ready = (
            sem("win_psum"), sem("win_ready"), sem("selcmp_psum"), sem("nm0_ready"), sem("exp0_ready"))
        probs0_ready, pTa_psum, pTa_ready, pTb_psum, pTb_ready, pTs_psum, pTs_ready = (
            sem("probs0_ready"), sem("pTa_psum"), sem("pTa_ready"), sem("pTb_psum"), sem("pTb_ready"),
            sem("pTs_psum"), sem("pTs_ready"))
        comb_psum, comb_ready, o_psum = sem("comb_psum"), sem("comb_ready"), sem("o_psum")
        xTh_ready, xTl_ready = sem("xTh_ready"), sem("xTl_ready")
        lg_psum, pm_ready, pm_psum, dg_ready, mx_psum, nm1_ready = (sem("lg_psum"), sem("pm_ready"), sem("pm_psum"),
                                                                    sem("dg_ready"), sem("mx_psum"), sem("nm1_ready"))
        es_ready, tot_psum, gs_ready, gT_psum, gT_ready, b2_psum = (
            sem("es_ready"), sem("tot_psum"), sem("gs_ready"), sem("gT_psum"), sem("gT_ready"), sem("b2_psum"))
        mh_psum, mh_ready, hl_ready = sem("mh_psum"), sem("mh_ready"), sem("hl_ready")
        my_psum, my_used, gb_psum, gb_ready, acc_ready, acc_psum = (
            sem("my_psum"), sem("my_used"), sem("gb_psum"), sem("gb_ready"), sem("acc_ready"), sem("acc_psum"))
        cq_psum, cq_ready, kr_psum, kr_ready, ckt_psum, ckt_ready = (
            sem("cq_psum"), sem("cq_ready"), sem("kr_psum"), sem("kr_ready"), sem("ckt_psum"), sem("ckt_ready"))
        kh_psum, kR_ready, ks_ready, s_psum, nm_ready, p_ready, rrow_ready, pn_ready = (
            sem("kh_psum"), sem("kR_ready"), sem("ks_ready"), sem("s_psum"), sem("nm_ready"), sem("p_ready"),
            sem("rrow_ready"), sem("pn_ready"))
        PT_psum, PTv_ready, PTa_ready = sem("PT_psum"), sem("PTv_ready"), sem("PTa_ready")
        pv_psum, oT_ready, mo_psum = sem("pv_psum"), sem("oT_ready"), sem("mo_psum")

        ident = const[:, C_ID:C_ID + P]
        ones = const[:, C_ONES:C_ONES + P]
        iota = const[:, C_IOTA:C_IOTA + NPROTO]

        def row(name):
            return rows[:, ROW_AT[name]:ROW_AT[name] + dict(ROWS)[name]]

        def col(name, k=0):
            return cols[:, COL_AT[name] + k:COL_AT[name] + k + 1]

        def over_tiles(ap, n):
            return ap.unsqueeze(1).to_broadcast([P, T, n])

        def flat(ap):
            return ap.rearrange("p a b -> p (a b)")

        def both_lanes(heavy_steps, light_steps):
            taken = 0
            for k, _ in enumerate(heavy_steps):
                if taken < light_due(k):
                    next(light_steps)
                    taken += 1
            for _ in light_steps:
                pass

        first_loads = [(const[:], dram["const"]), (proto[:], dram["proto"]), (pB[:], dram["pB"]), (cols[:], dram["cols"]),
                       (pA[:], dram["pA"]), (pbias[:], dram["pbias"])]
        nsa_loads = [(wqkv[:], dram["wqkv"]), (wgate[:], dram["wgate"]), (wcomp[:], dram["wcomp"]), (wo[:], dram["wo"])]
        heavy_loads = [(wdq[:], dram["wdq"]), (wkvr[:], dram["wkvr"]), (gatew[:], dram["gatew"]), (b2[:], dram["b2"]),
                       (uq[:], dram["uq"]), (uk[:], dram["uk"]), (qr[DC:DC + DR], dram["qr"]), (uv[:], dram["uv"]),
                       (wO[:], dram["wO"]), (w1[:], dram["w1"]), (w2[:], dram["w2"])]
        HN = E * FC

        xr = dram["x"].rearrange("b (t p) d -> b p t d", p=P)
        outr = out.rearrange("b (t p) d -> b p t d", p=P)

        block = ctx.enter_context(nc.Block())

        @block.sync
        def _(sp):
            sp.dma_start(xin[:], xr[0]).then_inc(x_in, 16)
            sp.dma_start(rows[:], dram["rows"].partition_broadcast(P)).then_inc(first_in, 16)
            for arrived, loads in ((first_in, first_loads), (nsa_in, nsa_loads), (heavy_in, heavy_loads)):
                for dst, src in loads:
                    sp.dma_start(dst, src).then_inc(arrived, 16)
            sp.wait_ge(xl_ready, 1)
            sp.dma_start(xin[:], xr[1]).then_inc(x_in, 16)
            with nc.sync.Fori(0, NB - 2) as b:
                sp.wait_ge(xl_ready, 3 * b + 4)
                sp.dma_start(xin[:], xr[b + 2]).then_inc(x_in, 16)
                sp.wait_ge(xout_ready, b + 1)
                sp.dma_start(outr[b], xout[:]).then_inc(x_out, 16)
            sp.wait_ge(xl_ready, 3 * (NB - 2) + 4)
            sp.dma_start(xin[:], xr[0]).then_inc(x_in, 16)
            for b in (NB - 2, NB - 1):
                sp.wait_ge(xout_ready, b + 1)
                sp.dma_start(outr[b], xout[:]).then_inc(x_out, 16)
            sp.wait_ge(x_out, 16 * NB + 16)

        @block.gpsimd
        def _(pool):
            nc.gpsimd.memset(xout[:], 0.0).then_inc(x_out, 16)
            nc.gpsimd.memset(light.xnT[:], 0.0).then_inc(zeroed, 1)
            nc.gpsimd.memset(kvT[:], 0.0).then_inc(zeroed, 1)
            nc.gpsimd.memset(ws8[:], 0.0).then_inc(zeroed, 1)
            nc.gpsimd.memset(kT[:], 0.0).then_inc(zeroed, 1)
            nc.gpsimd.memset(qk[:], 0.0).then_inc(zeroed, 1)
            pool.wait_ge(zeroed, 5)
            nc.gpsimd.memset(cqs[3 * DC:KS].bitcast(F32), 1.0).then_inc(zeroed, 1)
            pool.wait_ge(zeroed, 6)
            nc.gpsimd.memset(kT[DC + DR:KK], 1.0).then_inc(zeroed, 1)
            pool.wait_ge(zeroed, 7)

            def moe(b, r):
                for e in range(E):
                    for c in range(FC):
                        pool.wait_ge(mh_ready, 2 * HN * b + HN * r + e * FC + c + 1)
                        nc.gpsimd.tensor_tensor(hl[:, e % 2, c, :], hf[:, c % 2, :], hh[:, e % 2, c, :].bitcast(F32),
                                                ALU.subtract).then_inc(hl_ready, 1)

            def mla(b):
                for h in range(H1):
                    pool.wait_ge(rrow_ready, H1 * b + h + 1)
                    nc.gpsimd.tensor_tensor(probs[:, h % 3, 0, :], probs[:, h % 3, 0, :],
                                            rrow[:, h, 0:1].to_broadcast([P, S]), ALU.mult)
                    for t in range(1, T):
                        i = nc.gpsimd.tensor_scalar(probs[:, h % 3, t, :], probs[:, h % 3, t, :], rrow[:, h, t:t + 1],
                                                    1.0, ALU.mult, ALU.mult)
                    i.then_inc(pn_ready, 1)

            def nsa_bias(b):
                pool.wait_ge(light.xn_ready, T * (3 * b + 2))
                nc.gpsimd.tensor_tensor(xl[:], xl[:], over_tiles(row("bo"), D), ALU.add).then_inc(bo_ready, 1)

            def mla_bias(b):
                pool.wait_ge(heavy.xn_ready, T * (3 * b + 2))
                nc.gpsimd.tensor_tensor(xh[:], xh[:], over_tiles(bOb[:], D), ALU.add).then_inc(bO_ready, 1)

            def take_over(b):
                pool.wait_ge(xl_ready, 3 * b + 3)
                pool.wait_ge(x_out, 16 * b + 16)
                nc.gpsimd.tensor_tensor(xh[:], xl[:], over_tiles(ones, D), ALU.mult).then_inc(xh_copied, 1)

            nsa_bias(0)
            pool.wait_ge(low_ready, 2)
            with nc.gpsimd.Fori(0, NB - 1) as b:
                take_over(b)
                moe(b, 0)
                nsa_bias(b + 1)
                mla_bias(b)
                mla(b)
                moe(b, 1)
            take_over(NB - 1)
            moe(NB - 1, 0)
            mla_bias(NB - 1)
            mla(NB - 1)
            moe(NB - 1, 1)

        @block.tensor
        def _(pe):
            def mm(o, lhsT, rhs, start=True, stop=True):
                return pe.matmul(o, lhsT, rhs, start=start, stop=stop)

            def turn(o, in_):
                return pe.transpose(o, in_, const[0:in_.shape[0], C_ID:C_ID + in_.shape[0]])

            def light_setup():
                pe.wait_ge(first_in, 16 * (len(first_loads) + 1))
                pe.wait_ge(setup_v, 1)
                mm(ps[:, 0, 0:NPROTO], ones, protosq[:]).then_inc(setup_p, 1)

            def heavy_setup():
                pe.wait_ge(heavy_in, 16 * len(heavy_loads))
                pe.wait_ge(setup_done, 1)
                for h in range(H1):
                    m = mm(ps[0:KQ, 1, h * KQ:(h + 1) * KQ], uk[:, h, :], uq[:, h, :])
                m.then_inc(setup_p, 1)
                for h in range(H1):
                    a = DC * (h % 4)
                    m = mm(ps[a:a + DC, 2, (h // 4) * D:(h // 4 + 1) * D], uv[:, h, :], wO[:, h, :])
                m.then_inc(setup_p, 1)
                for h in range(H1):
                    m = mm(ps[:, 3, 0:D], col("buv", h).to_broadcast([P, P]), wO[:, h, :], h == 0, h == H1 - 1)
                m.then_inc(setup_p, 1)

            def layernorm(lane, n):
                yield
                yield
                for t in range(T):
                    pe.wait_ge(lane.xn_ready, T * n + t + 1)
                    m = turn(ps[:, lane.bank, t * P:(t + 1) * P], lane.xn[:, t, :])
                m.then_inc(lane.xnT_psum, 1)
                yield

            def xT(t):
                return light.xnT[:, WIN + t * P:WIN + (t + 1) * P]

            def proto_route(b, r):
                n = 2 * b + r
                s = 2 * r
                yield from layernorm(light, 3 * b + s)
                pe.wait_ge(light.xnT_ready, 3 * b + s + 1)
                for t in range(T):
                    m = mm(ps[:, B, t * NPROTO:(t + 1) * NPROTO], xT(t), proto[:])
                m.then_inc(dot_psum, 1)
                yield
                mm(ps[:, A, :], xT(0), pB[:]).then_inc(h_psum, 1)
                yield
                yield
                yield
                pe.wait_ge(w_ready, n + 1)
                for t in range(T):
                    m = turn(ps[0:NPROTO, B, t * P:(t + 1) * P], wsum[:, t, :])
                m.then_inc(wT_psum, 1)
                yield

            def proto_experts(b, r):
                n = 2 * b + r
                for t in range(T):
                    pe.wait_ge(hw_ready, T * n + t + 1)
                    for c in range(PR):
                        m = turn(ps[:, A, c * P:(c + 1) * P], hw[:, t % 2, c * P:(c + 1) * P])
                    m.then_inc(hwT_psum, 1)
                    yield
                    if t == 0:
                        pe.wait_ge(wT_ready, n + 1)
                    pe.wait_ge(hwT_ready, T * n + t + 1)
                    if t + 1 < T:
                        mm(ps[:, A, :], xT(t + 1), pB[:]).then_inc(h_psum, 1)
                    o = ps[:, B, t * P:(t + 1) * P]
                    for c in range(PR):
                        mm(o, hwT[:, t % 2, c, :], pA[:, c, :], c == 0, False)
                    m = mm(o, wT[:, t * P:(t + 1) * P], pbias[:], False, True)
                    if t == T - 1:
                        m.then_inc(py_psum, 1)
                    yield
                yield

            def nsa(b):
                yield from layernorm(light, 3 * b + 1)
                pe.wait_ge(light.xnT_ready, 3 * b + 2)
                mm(ps[:, A, :], wqkv[:, 0, :], light.xnT[:, WIN:WIN + S]).then_inc(q_psum, 1)
                mm(ps[:, B, :], wqkv[:, 1, :], light.xnT[:, WIN:WIN + S]).then_inc(kv_psum, 1)
                yield
                pe.wait_ge(q_ready, b + 1)
                mm(ps[:, A, :], wqkv[:, 2, :], light.xnT[:, WIN:WIN + S]).then_inc(kv_psum, 1)
                pe.wait_ge(kv_ready, 2 * b + 1)
                mm(ps[:, B, 0:P], light.xnT[:, T * P:(T + 1) * P], wqkv[:, 2, :])
                for t in range(T):
                    m = mm(ps[:, B, P + 3 * t:P + 3 * t + 3], xT(t), wgate[:])
                m.then_inc(gz_psum, 1)
                yield
                pe.wait_ge(kv_ready, 2 * b + 2)
                for j in range(2 * T):
                    a = WIN + (j % T) * P
                    m = mm(ps[0:2 * T, A, 0:P], ws8[:, j, :], kvT[:, j // T, a:a + P], j == 0, j == 2 * T - 1)
                m.then_inc(score_psum, 1)
                pe.wait_ge(gz_ready, b + 1)
                for u in range(T):
                    m = mm(ps[:, B, u * P:(u + 1) * P], light.xnT[:, u * P:(u + 1) * P], wqkv[:, 2, :])
                m.then_inc(vs_psum, 1)
                yield
                pe.wait_ge(vs_ready, b + 1)
                for half in range(2):
                    for c in range(half * CBS // 2, (half + 1) * CBS // 2):
                        m = mm(ps[:, B, 0:2 * NCMP], wcomp[:, c, :], kvT[:, :, WIN + c:WIN + S:CBS], c == 0, c == CBS - 1)
                    if half == 1:
                        m.then_inc(comp_psum, 1)
                    yield
                pe.wait_ge(selx_ready, b + 1)
                for t in range(2):
                    m = mm(ps[:, A, t * 256:t * 256 + WK], qT[:, t * P:(t + 1) * P], kvT[:, 0, t * P:t * P + WK])
                m.then_inc(win_psum, 1)
                pe.wait_ge(comp_ready, b + 1)
                turn(ps[0:NCMP, B, 0:P], ckv[:, 1, :]).then_inc(cv_psum, 1)
                yield
                pe.wait_ge(cv_ready, b + 1)
                mm(ps[:, B, 0:2 * T * DELTA_W], ones[0:2 * T, :], flat(selx)).then_inc(sel_psum, 1)
                pe.wait_ge(win_ready, 2 * b + 1)
                for t in range(2, T):
                    m = mm(ps[:, A, (t - 2) * 256:(t - 2) * 256 + WK], qT[:, t * P:(t + 1) * P],
                           kvT[:, 0, t * P:t * P + WK])
                m.then_inc(win_psum, 1)
                yield
                pe.wait_ge(onehot_ready, b + 1)
                for t in range(T):
                    o = ps[:, B, 0:2 * NSEL].rearrange("p (k t j) -> p k t j", k=2, t=T)[:, :, t, :]
                    m = mm(o, light.xn[:, t, :], onehot[:, :, t, :])
                m.then_inc(xsel_psum, 1)
                yield
                pe.wait_ge(xsel_ready, b + 1)
                pe.wait_ge(win_ready, 2 * b + 2)
                mm(ps[:, A, 0:NSEL], wqkv[:, 1, :], xsel[:, 0, :])
                mm(ps[:, A, P:2 * P], xsel[:, 1, :], wqkv[:, 2, :]).then_inc(skv_psum, 1)
                yield
                pe.wait_ge(skv_ready, b + 1)
                for t in range(SELT):
                    mm(ps[:, B, t * NSEL:(t + 1) * NSEL], qT[:, t * P:(t + 1) * P], skT[:])
                mm(ps[:, B, SELT * NSEL:SELT * NSEL + NCMP], qT[:, 0:P], ckv[:, 0, :]).then_inc(selcmp_psum, 1)
                yield
                yield
                yield
                pe.wait_ge(probs0_ready, b + 1)
                for t in range(T):
                    m = turn(ps[:, A, t * P:(t + 1) * P], probs0[:, t * WK:t * WK + P])
                m.then_inc(pTa_psum, 1)
                for t in range(T):
                    m = turn(ps[0:2 * WIN, B, t * P:(t + 1) * P], probs0[:, t * WK + P:(t + 1) * WK])
                m.then_inc(pTb_psum, 1)
                yield
                pe.wait_ge(pTa_ready, b + 1)
                for t in range(SELT):
                    turn(ps[:, A, t * P:(t + 1) * P], probs0[:, OSEL + t * NSEL:OSEL + (t + 1) * NSEL])
                turn(ps[0:NCMP, A, SELT * P:(SELT + 1) * P], probs0[:, OCMP:OCMP + NCMP]).then_inc(pTs_psum, 1)
                yield
                pe.wait_ge(pTb_ready, b + 1)
                pe.wait_ge(pTs_ready, b + 1)
                for t in range(T):
                    o = ps[:, B, t * P:(t + 1) * P]
                    mm(o, vs[:, t, :], pTa[:, t, :], True, False)
                    m = mm(o, vs[0:2 * WIN, t + 1, :], pTb[:, t, :], False, t >= SELT)
                    if t < SELT:
                        m = mm(o, sv[:], pTs[:, t, :], False, t >= CMPT)
                    if t < CMPT:
                        m = mm(o, cv[:], pTc[:], False, True)
                m.then_inc(comb_psum, 1)
                yield
                pe.wait_ge(comb_ready, b + 1)
                for t in range(T):
                    m = mm(ps[:, A, t * P:(t + 1) * P], combT[:, t, :], wo[:])
                m.then_inc(o_psum, 1)
                yield

            def moe(b, r):
                n = 2 * b + r
                yield from layernorm(heavy, 3 * b + 2 * r)

                def split_mm(o, high, low, rhigh, rlow, start, stop, wait_low=False):
                    mm(o, high, rhigh, start, False)
                    mm(o, low, rhigh, False, False)
                    if wait_low:
                        pe.wait_ge(xTl_ready, n + 1)
                    return mm(o, high, rlow, False, stop)

                def hidden(e, c):
                    k = e * FC + c
                    if k >= 2:
                        pe.wait_ge(mh_ready, HN * n + k - 1)
                    w = slice(c * P, (c + 1) * P)
                    split_mm(ps[:, 1 + k % 2, :], w1h[:, e, w], w1l[:, e, w], xTh[:], xTl[:], True, True,
                             k == 0).then_inc(mh_psum, 1)

                def down(e, c):
                    pe.wait_ge(hl_ready, HN * n + FC * e + c + 1)
                    if c == 0 and e >= 2:
                        pe.wait_ge(my_used, E * n + e - 1)
                    m = split_mm(ps[:, 3 + e % 2, :], w2h[:, e, c, :], w2l[:, e, c, :], hh[:, e % 2, c, :],
                                 hl[:, e % 2, c, :], c == 0, c == FC - 1)
                    if c == FC - 1:
                        m.then_inc(my_psum, 1)

                def route(u):
                    if u == 0:
                        pe.wait_ge(heavy.xnT_ready, 3 * b + 2 * r + 1)
                        for t in range(T):
                            m = mm(ps[:, 0, t * E:(t + 1) * E], heavy.xnT[:, t * P:(t + 1) * P], gatew[:])
                        m.then_inc(lg_psum, 1)
                    elif u == 1:
                        pe.wait_ge(pm_ready, n + 1)
                        turn(ps[0:2, 0, 0:P], pm[:]).then_inc(pm_psum, 1)
                    elif u == 2:
                        pe.wait_ge(dg_ready, n + 1)
                        mm(ps[:, 0, 0:2], ones[0:2, :], dg[:]).then_inc(mx_psum, 1)
                    elif u == 3:
                        pe.wait_ge(es_ready, n + 1)
                        mm(ps[:, 0, 0:2], ones, es[:]).then_inc(tot_psum, 1)
                    elif u == 4:
                        pe.wait_ge(gs_ready, n + 1)
                        for t in range(T):
                            m = turn(ps[0:GS, 0, t * P:(t + 1) * P], gs[:, t, :])
                        m.then_inc(gT_psum, 1)
                    elif u == 5:
                        pe.wait_ge(gT_ready, n + 1)
                        mm(ps[:, 0, :], b2h[:], gTr[:], True, False)
                        mm(ps[:, 0, :], b2l[:], gTr[:], False, True).then_inc(b2_psum, 1)

                def spread_gate(e):
                    if e > 0:
                        pe.wait_ge(gb_ready, E * n + e)
                    mm(ps[:, 5, :], gsel[:, e:e + 1].to_broadcast([GS, P]), gTr[:]).then_inc(gb_psum, 1)

                for u in range(2 * E + 3):
                    e, half = u // 2, u % 2
                    if u == 0:
                        pe.wait_ge(xTh_ready, n + 1)
                        route(0)
                    for c in (2 * half, 2 * half + 1):
                        if e < E:
                            hidden(e, c)
                        if 1 <= e <= E:
                            down(e - 1, c)
                    if u > 0:
                        route(u)
                    if spread_expert(u) is not None:
                        spread_gate(spread_expert(u))
                    yield
                pe.wait_ge(acc_ready, n + 1)
                for t in range(T):
                    m = turn(ps[:, 0, t * P:(t + 1) * P], accT[:, t * P:(t + 1) * P])
                m.then_inc(acc_psum, 1)
                yield

            def mla(b):
                yield from layernorm(heavy, 3 * b + 1)
                pe.wait_ge(heavy.xnT_ready, 3 * b + 2)
                mm(ps[0:DC + DR, 2, :], wkvr[:], heavy.xnT[:]).then_inc(kr_psum, 1)
                mm(ps[0:3 * DC, 1, :], flat(wdq), heavy.xnT[:]).then_inc(cq_psum, 1)
                for t in range(T):
                    m = mm(ps[:, 3, t * DC:(t + 1) * DC], heavy.xnT[:, t * P:(t + 1) * P], wkvr[:, 0:DC])
                m.then_inc(ckt_psum, 1)
                yield

                def keys(h):
                    if h == 0:
                        pe.wait_ge(kr_ready, b + 1)
                    else:
                        pe.wait_ge(ks_ready, H1 * b + h)
                    mm(ps[0:KS, 0, :], qk[:, h, :], kT[:]).then_inc(kh_psum, 1)

                def scores(h, t):
                    n = h * T + t
                    if n == 0:
                        pe.wait_ge(cq_ready, b + 1)
                    if t == 0:
                        pe.wait_ge(ks_ready, H1 * b + h + 1)
                    if n >= 2:
                        pe.wait_ge(p_ready, H1 * T * b + n - 1)
                    mm(ps[:, 1 + n % 2, :], cqs[:, t * P:(t + 1) * P], ks[:, h % 2, :]).then_inc(s_psum, 1)

                def turn_probs(h, k):
                    if k == 0:
                        pe.wait_ge(pn_ready, H1 * b + h + 1)
                    if h * T + k == 0:
                        pe.wait_ge(ckt_ready, b + 1)
                    if h * T + k >= 2:
                        pe.wait_ge((PTv_ready, PTa_ready)[k % 2], 2 * H1 * b + 2 * h + k // 2)
                    for t in range(T):
                        m = turn(ps[:, 3 + k % 2, t * P:(t + 1) * P], probs[:, h % 3, t, k * P:(k + 1) * P])
                    m.then_inc(PT_psum, 1)

                def values(h, k):
                    if k == 0:
                        pe.wait_ge(PTv_ready, 2 * H1 * b + 2 * h + 2)
                        pe.wait_ge(PTa_ready, 2 * H1 * b + 2 * h + 2)
                        if h == 4:
                            pe.wait_ge(oT_ready, 2 * b + 1)
                    a = DC * (h % 4)
                    m = mm(ps[a:a + DC, 5, :], ckt[:, k, :], PT[:, h % 2, k, :], k == 0, k == T - 1)
                    if k == T - 1:
                        m.then_inc(pv_psum, 1)

                keys(0)
                yield
                for h in range(H1 + 3):
                    for t in range(T):
                        if 2 <= h < H1 + 2:
                            turn_probs(h - 2, t)
                        if t == 0 and h + 1 < H1:
                            keys(h + 1)
                        if h < H1:
                            scores(h, t)
                        if h >= 3:
                            values(h - 3, t)
                        yield
                pe.wait_ge(oT_ready, 2 * b + 2)
                for t in range(T):
                    for c in range(2):
                        m = mm(ps[:, 0, t * P:(t + 1) * P], oT[c][:, t * P:(t + 1) * P], vo[:, c, :], c == 0, c == 1)
                m.then_inc(mo_psum, 1)
                yield

            def light_lane(b):
                yield from proto_experts(b, 0)
                yield from nsa(b)
                yield from proto_route(b, 1)
                yield from proto_experts(b, 1)
                yield from proto_route(b + 1, 0)

            def heavy_lane(b):
                yield from moe(b, 0)
                yield from mla(b)
                yield from moe(b, 1)

            light_setup()
            for _ in proto_route(0, 0):
                pass
            for k, _ in enumerate(light_lane(0)):
                if k == NSA_AT - 1:
                    pe.wait_ge(nsa_in, 16 * len(nsa_loads))
                if k == SETUP_AT:
                    heavy_setup()
            pe.wait_ge(low_ready, 2)
            with nc.tensor.Fori(0, NB - 1) as b:
                both_lanes(heavy_lane(b), light_lane(b + 1))
            for _ in heavy_lane(NB - 1):
                pass

        @block.scalar
        def _(act):
            nc.scalar.preload_act_table_set("natural_log_exp_and_others")
            chained = [0]

            def link(ins):
                chained[0] += 1
                ins.then_inc(a_chain, 1)
                act.wait_ge(a_chain, chained[0])

            def layernorm(lane, n):
                act.wait_ge(lane.var_ready, n + 1)
                link(nc.scalar.activation(lane.lnv[:], lane.var[:], ACT.Ln))
                nc.scalar.activation(lane.rstd0[:], lane.lnv[:], ACT.Exp, scale=-0.5).then_inc(lane.rstd0_ready, 1)
                yield
                yield
                act.wait_ge(lane.xnT_psum, n + 1)
                to = lane.xnT[:, WIN:WIN + S] if lane is light else lane.xnT[:]
                nc.scalar.copy(to, ps[:, lane.bank, :]).then_inc(lane.xnT_ready, 1)

            def proto_route(b, r):
                n = 2 * b + r
                yield from layernorm(light, 3 * b + 2 * r)
                for t in range(T):
                    i = nc.scalar.activation(sqjunk[:], light.xn[:, t, :], ACT.Square, accum_out=x2[:, t:t + 1])
                    if t < T - 1:
                        link(i)
                i.then_inc(x2_ready, 1)
                yield
                act.wait_ge(d2_ready, n + 1)
                link(nc.scalar.activation(lnd[:], d2[:], ACT.Ln))
                nc.scalar.activation(root[:], lnd[:], ACT.Exp, scale=0.5).then_inc(root_ready, 1)
                yield
                act.wait_ge(gap_ready, n + 1)
                nc.scalar.activation(prob[:], quo[:], ACT.Exp, scale=ninvt[:, 1:2]).then_inc(prob_ready, 1)
                yield
                yield
                yield
                act.wait_ge(wT_psum, n + 1)
                nc.scalar.copy(wT, ps[0:NPROTO, B, :]).then_inc(wT_ready, 1)
                yield

            def proto_experts(b, r):
                n = 2 * b + r
                for t in range(T):
                    act.wait_ge(hwT_psum, T * n + t + 1)
                    nc.scalar.copy(flat(hwT[:, t % 2]), ps[:, A, :]).then_inc(hwT_ready, 1)
                    yield
                    yield
                yield

            def nsa(b):
                yield from layernorm(light, 3 * b + 1)
                yield
                act.wait_ge(kv_psum, 2 * b + 1)
                nc.scalar.activation(kvT[:, 0, WIN:WIN + S], ps[:, B, :], ACT.Identity, bias=col("bk")).then_inc(kv_ready, 1)
                yield
                act.wait_ge(kv_psum, 2 * b + 2)
                nc.scalar.activation(kvT[:, 1, WIN:WIN + S], ps[:, A, :], ACT.Identity, bias=col("bvc")).then_inc(kv_ready, 1)
                act.wait_ge(gz_ready, b + 1)
                nc.scalar.activation(ge[:], gz[:], ACT.Exp, scale=-1.0).then_inc(ge_ready, 1)
                yield
                yield
                yield
                act.wait_ge(comp_psum, b + 1)
                nc.scalar.activation(flat(ckv), ps[:, B, 0:2 * NCMP], ACT.Identity, bias=col("bcomp")).then_inc(comp_ready, 1)
                yield
                act.wait_ge(cv_psum, b + 1)
                nc.scalar.copy(cv, ps[0:NCMP, B, 0:P]).then_inc(cv_ready, 1)
                yield
                yield
                act.wait_ge(xsel_psum, b + 1)
                nc.scalar.copy(flat(xsel), ps[:, B, 0:2 * NSEL]).then_inc(xsel_ready, 1)
                yield
                yield
                yield
                act.wait_ge(nm0_ready, b + 1)
                for i in range(NSEG):
                    a, n = segment(i)
                    e = nc.scalar.activation(probs0[:, a:a + n], probs0[:, a:a + n], ACT.Exp, bias=nm0[:, i:i + 1],
                                             accum_out=sum0[:, i:i + 1])
                e.then_inc(exp0_ready, 1)
                yield
                yield
                act.wait_ge(pTa_psum, b + 1)
                nc.scalar.copy(flat(pTa), ps[:, A, :]).then_inc(pTa_ready, 1)
                yield
                act.wait_ge(pTs_psum, b + 1)
                nc.scalar.copy(flat(pTs), ps[:, A, 0:SELT * P])
                nc.scalar.copy(pTc, ps[0:NCMP, A, SELT * P:(SELT + 1) * P]).then_inc(pTs_ready, 1)
                yield
                act.wait_ge(comb_psum, b + 1)
                nc.scalar.copy(flat(combT), ps[:, B, :]).then_inc(comb_ready, 1)
                yield
                yield

            def moe(b, r):
                n = 2 * b + r
                yield from layernorm(heavy, 3 * b + 2 * r)
                nc.scalar.copy(xTh[:], ps[:, 0, :]).then_inc(xTh_ready, 1)
                yield

                def hidden(e, c):
                    k = e * FC + c
                    act.wait_ge(mh_psum, HN * n + k + 1)
                    if c == 0 and e >= 2:
                        act.wait_ge(my_psum, E * n + e - 1)
                    if k >= 2:
                        act.wait_ge(hl_ready, HN * n + k - 1)
                    nc.scalar.activation(hf[:, c % 2, :], ps[:, 1 + k % 2, :], ACT.Relu, bias=col("b1", k))
                    nc.scalar.activation(hh[:, e % 2, c, :], ps[:, 1 + k % 2, :], ACT.Relu,
                                         bias=col("b1", k)).then_inc(mh_ready, 1)

                for u in range(2 * E + 3):
                    e, half = u // 2, u % 2
                    if e < E:
                        hidden(e, 2 * half)
                        hidden(e, 2 * half + 1)
                    if u == 2:
                        act.wait_ge(nm1_ready, n + 1)
                        for k in range(2):
                            i = nc.scalar.activation(ek[:, k, :], heavy.top8[:, :, k], ACT.Exp, bias=nm1[:, k:k + 1],
                                                     accum_out=es[:, k:k + 1])
                        i.then_inc(es_ready, 1)
                    if u == 4:
                        act.wait_ge(gT_psum, n + 1)
                        nc.scalar.copy(gTr[:], ps[0:GS, 0, :]).then_inc(gT_ready, 1)
                    g_e = spread_expert(u)
                    if g_e is not None:
                        act.wait_ge(gb_psum, E * n + g_e + 1)
                        if g_e > 0:
                            act.wait_ge(my_used, E * n + g_e)
                        nc.scalar.copy(gbs[:], ps[:, 5, :]).then_inc(gb_ready, 1)
                    yield
                yield

            def mla(b):
                yield from layernorm(heavy, 3 * b + 1)
                yield
                act.wait_ge(kr_psum, b + 1)
                nc.scalar.activation(kT[0:DC + DR, :], ps[0:DC + DR, 2, :], ACT.Identity,
                                     bias=cols[0:DC + DR, COL_AT["bkr"]:COL_AT["bkr"] + 1]).then_inc(kr_ready, 1)
                yield

                def key_high(h):
                    act.wait_ge(kh_psum, H1 * b + h + 1)
                    if h > 0:
                        act.wait_ge(ks_ready, H1 * b + h)
                    nc.scalar.copy(kR, ps[0:KS, 0, :]).then_inc(kR_ready, 1)

                def soft(h, t):
                    n = h * T + t
                    act.wait_ge(nm_ready, H1 * T * b + n + 1)
                    if t == 0 and h >= 3:
                        act.wait_ge(PT_psum, H1 * T * b + (h - 2) * T)
                    nc.scalar.activation(probs[:, h % 3, t, :], ps[:, 1 + n % 2, :], ACT.Exp,
                                         bias=nm[:, h, t:t + 1], accum_out=rowsum[:, h, t:t + 1]).then_inc(p_ready, 1)

                key_high(0)
                yield
                for h in range(H1 + 3):
                    for t in range(T):
                        if t % 2 == 1 and 2 <= h < H1 + 2:
                            act.wait_ge(PT_psum, H1 * T * b + (h - 2) * T + t + 1)
                            if t == 1 and h >= 4:
                                act.wait_ge(pv_psum, H1 * b + h - 3)
                            nc.scalar.copy(PT[:, h % 2, t, :], ps[:, 4, :]).then_inc(PTa_ready, 1)
                        if t == 0 and h + 1 < H1:
                            key_high(h + 1)
                        if h < H1:
                            soft(h, t)
                        if t == T - 1 and h in (6, 10):
                            act.wait_ge(pv_psum, H1 * b + h - 2)
                            nc.scalar.copy(oT[(h - 6) // 4][:], ps[:, 5, :]).then_inc(oT_ready, 1)
                        yield
                yield

            def light_lane(b):
                yield from proto_experts(b, 0)
                yield from nsa(b)
                yield from proto_route(b, 1)
                yield from proto_experts(b, 1)
                yield from proto_route(b + 1, 0)

            def heavy_lane(b):
                yield from moe(b, 0)
                yield from mla(b)
                yield from moe(b, 1)

            for _ in proto_route(0, 0):
                pass
            for k, _ in enumerate(light_lane(0)):
                if k == SETUP_AT:
                    act.wait_ge(heavy_in, 16 * len(heavy_loads))
                    nc.scalar.copy(w1h[:], w1[:]).then_inc(high_ready, 1)
                    nc.scalar.copy(w2h[:], w2[:]).then_inc(high_ready, 1)
            with nc.scalar.Fori(0, NB - 1) as b:
                nc.scalar.sem_clear(a_chain)
                chained[0] = 0
                both_lanes(heavy_lane(b), light_lane(b + 1))
            nc.scalar.sem_clear(a_chain)
            chained[0] = 0
            for _ in heavy_lane(NB - 1):
                pass

        @block.vector
        def _(dve):
            chained = [0]

            def link(ins):
                chained[0] += 1
                ins.then_inc(v_chain, 1)
                dve.wait_ge(v_chain, chained[0])

            def light_setup():
                done = [0]

                def then(ins):
                    done[0] += 1
                    ins.then_inc(setup_own, 1)
                    dve.wait_ge(setup_own, done[0])

                dve.wait_ge(first_in, 16 * (len(first_loads) + 1))
                nc.vector.tensor_tensor(protosq[:], proto[:], proto[:], ALU.mult).then_inc(setup_v, 1)
                dve.wait_ge(zeroed, 7)
                nc.vector.tensor_copy(ws8[:].rearrange("p a b -> p (a b)")[:, ::2 * T + 1],
                                      col("ws").to_broadcast([P, 2 * T]))
                then(nc.vector.tensor_scalar(ninvt[:, 0:1], row("temp"), -1.0, None, ALU.mult))
                then(nc.vector.tensor_tensor(ninvt[:, 0:1], ninvt[:, 0:1], row("temp"), ALU.max))
                then(nc.vector.tensor_scalar(ninvt[:, 0:1], ninvt[:, 0:1], 0.1, -2.0, ALU.max, ALU.mult))
                then(nc.vector.reciprocal(ninvt[:, 1:2], ninvt[:, 0:1]))
                dve.wait_ge(setup_p, 1)
                then(nc.vector.tensor_copy(p2b[:], ps[:, 0, 0:NPROTO]))
                nc.vector.memset(light.nt[:], 0.0).then_inc(setup_done, 1)

            def heavy_setup():
                dve.wait_ge(heavy_in, 16 * len(heavy_loads))
                dve.wait_ge(setup_p, 2)
                o = ps[0:KQ, 1, 0:H1 * KQ].rearrange("p (h k) -> p h k", h=H1)
                for dst, src in ((qk[0:DC], o[0:DC]), (qk[DC:DC + DR], qr[DC:DC + DR]), (qk[DC + DR:KK], o[DC:KQ])):
                    for c in range(3):
                        nc.vector.tensor_scalar(dst[:, :, c * DC:(c + 1) * DC], src[:, :, 0:DC], SCALE1, None, ALU.mult)
                    for c in range(2):
                        nc.vector.tensor_scalar(dst[:, :, 3 * DC + c:3 * DC + c + 1], src[:, :, DC:KQ], SCALE1, None,
                                                ALU.mult)
                nc.vector.tensor_tensor(gsel[:], ident[0:GS, 0:E], ident[0:GS, GS - E:GS], ALU.add)
                link(nc.vector.tensor_copy(b2h[:], b2[:]))
                nc.vector.tensor_tensor(b2l[:], b2[:], b2h[:].bitcast(F32), ALU.subtract)
                dve.wait_ge(setup_p, 3)
                nc.vector.tensor_copy(flat(vo), ps[:, 2, 0:2 * D])
                dve.wait_ge(setup_p, 4)
                nc.vector.tensor_tensor(bOb[:], ps[:, 3, 0:D], row("bO"), ALU.add)
                dve.wait_ge(high_ready, 1)
                nc.vector.tensor_tensor(w1l[:], w1[:], w1h[:].bitcast(F32), ALU.subtract).then_inc(low_ready, 1)
                dve.wait_ge(high_ready, 2)
                nc.vector.tensor_tensor(w2l[:], w2[:], w2h[:].bitcast(F32), ALU.subtract).then_inc(low_ready, 1)

            def layernorm(lane, n, src):
                for t in range(T):
                    i = nc.vector.bn_stats(lane.stats[:, t, :], src[:, t, :])
                link(i)
                for t in range(T):
                    i = nc.vector.bn_aggr(lane.mv[:, t, :], lane.stats[:, t, :])
                link(i)
                nc.vector.tensor_scalar(lane.var[:], lane.mv[:, :, 1], EPS, None, ALU.add).then_inc(lane.var_ready, 1)
                yield
                nt, rstd0 = lane.nt, lane.rstd0
                dve.wait_ge(lane.rstd0_ready, n + 1)
                link(nc.vector.scalar_tensor_tensor(out=nt[:], in0=rstd0[:], scalar=-0.5, in1=rstd0[:],
                                                    op0=ALU.mult, op1=ALU.mult))
                link(nc.vector.tensor_tensor(nt[:], nt[:], lane.var[:], ALU.mult))
                link(nc.vector.scalar_tensor_tensor(out=lane.rstd[:], in0=nt[:], scalar=1.5, in1=rstd0[:],
                                                    op0=ALU.add, op1=ALU.mult))
                for t in range(T):
                    nc.vector.tensor_scalar(lane.xn[:, t, :], src[:, t, :], lane.mv[:, t, 0:1], lane.rstd[:, t:t + 1],
                                            ALU.subtract, ALU.mult).then_inc(lane.xn_ready, 1)
                yield

            def two_hot(lane, first, second, weight, n):
                for t in range(T):
                    nc.vector.tensor_scalar(first[:, t, :], iota[:, 0:n], lane.idxf[:, t, 0:1], weight(t, 0),
                                            ALU.is_equal, ALU.mult)
                    i = nc.vector.tensor_scalar(second[:, t, :], iota[:, 0:n], lane.idxf[:, t, 1:2], weight(t, 1),
                                                ALU.is_equal, ALU.mult)
                link(i)

            def weigh_hidden(n, t):
                dve.wait_ge(h_psum, T * n + t + 1)
                nc.vector.tensor_tensor(hw[:, t % 2].rearrange("p (n j) -> p n j", j=RANK),
                                        ps[:, A, :].rearrange("p (n j) -> p n j", j=RANK),
                                        wsum[:, t, :].unsqueeze(2).to_broadcast([P, NPROTO, RANK]),
                                        ALU.mult).then_inc(hw_ready, 1)

            def proto_route(b, r):
                n = 2 * b + r
                if r == 0:
                    dve.wait_ge(x_in, 16 * b + 16)
                else:
                    dve.wait_ge(xl_ready, 3 * b + 2)
                yield from layernorm(light, 3 * b + 2 * r, (xin, xl)[r])
                yield
                dve.wait_ge(dot_psum, n + 1)
                link(nc.vector.scalar_tensor_tensor(
                    out=d2, in0=ps[:, B, 0:T * NPROTO].rearrange("p (t n) -> p t n", t=T), scalar=-2.0,
                    in1=over_tiles(p2b[:], NPROTO), op0=ALU.mult, op1=ALU.add))
                dve.wait_ge(x2_ready, n + 1)
                link(nc.vector.tensor_tensor(d2, d2, x2.unsqueeze(2).to_broadcast([P, T, NPROTO]), ALU.add))
                nc.vector.tensor_scalar(d2, d2, 0.0, TINY, ALU.max, ALU.max).then_inc(d2_ready, 1)
                yield
                dve.wait_ge(root_ready, n + 1)
                link(nc.vector.reciprocal(quo, root))
                link(nc.vector.tensor_tensor(quo, quo, d2, ALU.mult))
                link(nc.vector.tensor_tensor(quo, quo, root, ALU.add))
                link(nc.vector.tensor_reduce(low, quo, X, ALU.min))
                nc.vector.tensor_tensor(quo, quo, low.unsqueeze(2).to_broadcast([P, T, NPROTO]),
                                        ALU.subtract).then_inc(gap_ready, 1)
                yield
                dve.wait_ge(prob_ready, n + 1)
                nc.vector.memset(wk, 0.0)
                top8, idx8, idxf = light.top8, light.idx8, light.idxf
                for t in range(T):
                    i = nc.vector.max(top8[:, t, :], prob[:, t, :])
                link(i)
                for t in range(T):
                    nc.vector.max_index(idx8[:, t, :], top8[:, t, :], prob[:, t, :])
                link(nc.vector.tensor_tensor(den, top8[:, :, 0], top8[:, :, 1], ALU.add))
                nc.vector.tensor_copy(idxf[:], idx8[:, :, 0:2])
                link(nc.vector.reciprocal(rden, den))
                link(nc.vector.scalar_tensor_tensor(out=wk, in0=top8[:, :, 0:2], scalar=0.5,
                                                    in1=rden.unsqueeze(2).to_broadcast([P, T, 2]),
                                                    op0=ALU.mult, op1=ALU.mult))
                yield
                two_hot(light, wa, wb, lambda t, k: wk[:, t, k:k + 1], NPROTO)
                nc.vector.tensor_tensor(wsum, wa, wb, ALU.add).then_inc(w_ready, 1)
                yield
                dve.wait_ge(w_ready, n + 1)
                weigh_hidden(n, 0)
                yield

            def proto_experts(b, r, first=False):
                n = 2 * b + r
                yield
                for t in range(1, T):
                    weigh_hidden(n, t)
                    yield
                    yield
                yield
                dve.wait_ge(py_psum, n + 1)
                if r == 0 and not first:
                    dve.wait_ge(xh_copied, b)
                    dve.wait_ge(heavy.xn_ready, T * (3 * (b - 1) + 1))
                nc.vector.tensor_tensor(flat(xl), ps[:, B, :], flat((xin, xl)[r]), ALU.add).then_inc(xl_ready, 1)
                yield

            def topk():
                link(nc.vector.tensor_scalar(sc, ps[0:2 * T, A, 0:P], rows[0:2 * T, ROW_AT["bs"]:ROW_AT["bs"] + 1],
                                             None, ALU.add))
                blk = [slice(h * SBS, (h + 1) * SBS) for h in range(2)]
                for h in range(2):
                    i = nc.vector.max(sel8[:, h, 0:8], sc[:, blk[h]])
                link(i)
                yield
                for h in range(2):
                    nc.vector.max_index(seli[:, h, 0:8], sel8[:, h, 0:8], sc[:, blk[h]])
                    i = nc.vector.match_replace(sc2[:, blk[h]], sel8[:, h, 0:8], sc[:, blk[h]], LOWEST)
                link(i)
                for h in range(2):
                    i = nc.vector.max(sel8[:, h, 8:16], sc2[:, blk[h]])
                link(i)
                yield
                for h in range(2):
                    i = nc.vector.max_index(seli[:, h, 8:16], sel8[:, h, 8:16], sc2[:, blk[h]])
                link(i)
                link(nc.vector.tensor_copy(self_, seli[:]))
                link(nc.vector.tensor_tensor(flat(self_), flat(self_), const[0:2 * T, C_HALF:C_HALF + DELTA_W], ALU.add))
                nc.vector.tensor_tensor(
                    selx, flat(self_).unsqueeze(1).to_broadcast([2 * T, 2 * T, DELTA_W]),
                    const[0:2 * T, C_DELTA:C_DELTA + 2 * T * DELTA_W].rearrange("p (a b) -> p a b", a=2 * T),
                    ALU.mult).then_inc(selx_ready, 1)

            def nsa(b):
                dve.wait_ge(xl_ready, 3 * b + 1)
                yield from layernorm(light, 3 * b + 1, xl)
                yield
                dve.wait_ge(q_psum, b + 1)
                nc.vector.tensor_scalar(qT, ps[:, A, :], col("bq"), None, ALU.add).then_inc(q_ready, 1)
                yield
                dve.wait_ge(gz_psum, b + 1)
                nc.vector.tensor_tensor(vs[:, T, :], ps[:, B, 0:P], row("bv"), ALU.add)
                nc.vector.tensor_tensor(gz, ps[:, B, P:P + 3 * T].rearrange("p (t n) -> p t n", t=T),
                                        over_tiles(row("bg"), 3), ALU.add).then_inc(gz_ready, 1)
                yield
                dve.wait_ge(vs_psum, b + 1)
                nc.vector.tensor_tensor(vs[:, 0:T, :], ps[:, B, :].rearrange("p (t d) -> p t d", t=T),
                                        over_tiles(row("bv"), D), ALU.add).then_inc(vs_ready, 1)
                dve.wait_ge(score_psum, b + 1)
                yield from topk()
                dve.wait_ge(ge_ready, b + 1)
                link(nc.vector.tensor_scalar(ge, ge, 1.0, None, ALU.add))
                link(nc.vector.reciprocal(gate, ge))
                yield
                for j in range(2):
                    a = 2 * j * WK
                    dve.wait_ge(win_psum, 2 * b + j + 1)
                    i = nc.vector.scalar_tensor_tensor(
                        out=probs0[:, a:a + 2 * WK].rearrange("p (t k) -> p t k", t=2),
                        in0=ps[:, A, :].rearrange("p (t k) -> p t k", t=2)[:, :, 0:WK], scalar=SCALE0,
                        in1=const[:, C_MASK + a:C_MASK + a + 2 * WK].rearrange("p (t k) -> p t k", t=2),
                        op0=ALU.mult, op1=ALU.add).then_inc(win_ready, 1)
                    if j == 0:
                        yield
                dve.wait_ge(sel_psum, b + 1)
                nc.vector.tensor_scalar(onehot.rearrange("p k t j -> p (k t j)"), ps[:, B, 0:2 * T * DELTA_W],
                                        const[:, C_PCOL:C_PCOL + 1], None, ALU.is_equal).then_inc(onehot_ready, 1)
                yield
                dve.wait_ge(win_ready, 2 * b + 2)
                nc.vector.tensor_reduce(nm0[:, 0:T], probs0[:, 0:T * WK].rearrange("p (t k) -> p t k", t=T), X, ALU.max,
                                        negate=True)
                yield
                dve.wait_ge(skv_psum, b + 1)
                nc.vector.tensor_scalar(skT, ps[:, A, 0:NSEL], col("bk"), None, ALU.add)
                nc.vector.tensor_tensor(sv, ps[:, A, P:2 * P], row("bv"), ALU.add).then_inc(skv_ready, 1)
                yield
                dve.wait_ge(selcmp_psum, b + 1)
                link(nc.vector.scalar_tensor_tensor(
                    out=probs0[:, OSEL:NSC], in0=ps[:, B, 0:NSC - OSEL], scalar=SCALE0,
                    in1=const[:, C_MASK + OSEL:C_MASK + NSC], op0=ALU.mult, op1=ALU.add))
                nc.vector.tensor_reduce(nm0[:, T:T + SELT], probs0[:, OSEL:OCMP].rearrange("p (t k) -> p t k", t=SELT),
                                        X, ALU.max, negate=True)
                nc.vector.tensor_reduce(nm0[:, T + SELT:NSEG], probs0[:, OCMP:NSC], X, ALU.max,
                                        negate=True).then_inc(nm0_ready, 1)
                yield
                yield
                dve.wait_ge(exp0_ready, b + 1)
                link(nc.vector.reciprocal(rs0, sum0))
                nc.vector.tensor_tensor(coef[:, 0:T], rs0[:, 0:T], gate[:, :, 2], ALU.mult)
                nc.vector.tensor_tensor(coef[:, T:T + SELT], rs0[:, T:T + SELT], gate[:, 0:SELT, 1], ALU.mult)
                link(nc.vector.tensor_tensor(coef[:, T + SELT:NSEG], rs0[:, T + SELT:NSEG], gate[:, 0:CMPT, 0], ALU.mult))
                link(nc.vector.tensor_tensor(coef, coef, const[:, C_VALID:C_VALID + NSEG], ALU.mult))
                for k in range(NSEG):
                    a, n = segment(k)
                    i = nc.vector.tensor_scalar(probs0[:, a:a + n], probs0[:, a:a + n], coef[:, k:k + 1], None, ALU.mult)
                i.then_inc(probs0_ready, 1)
                yield
                dve.wait_ge(pTb_psum, b + 1)
                nc.vector.tensor_copy(flat(pTb), ps[0:2 * WIN, B, :]).then_inc(pTb_ready, 1)
                yield
                yield
                yield
                dve.wait_ge(o_psum, b + 1)
                dve.wait_ge(bo_ready, b + 1)
                nc.vector.tensor_tensor(flat(xl), ps[:, A, :], flat(xl), ALU.add).then_inc(xl_ready, 1)
                yield

            def moe(b, r):
                n = 2 * b + r
                if r == 0:
                    dve.wait_ge(xl_ready, 3 * b + 3)
                else:
                    dve.wait_ge(xh_ready, 2 * b + 2)
                yield from layernorm(heavy, 3 * b + 2 * r, (xl, xh)[r])
                dve.wait_ge(xTh_ready, n + 1)
                nc.vector.tensor_tensor(xTl[:], heavy.xnT[:], xTh[:].bitcast(F32), ALU.subtract).then_inc(xTl_ready, 1)
                yield
                top8, idx8, idxf = heavy.top8, heavy.idx8, heavy.idxf

                def route(u):
                    if u == 0:
                        dve.wait_ge(lg_psum, n + 1)
                        link(nc.vector.tensor_tensor(lg[:], ps[:, 0, 0:T * E].rearrange("p (t e) -> p t e", t=T),
                                                     over_tiles(row("gb"), E), ALU.add))
                        for t in range(T):
                            i = nc.vector.max(top8[:, t, :], lg[:, t, :])
                        link(i)
                        nc.vector.tensor_reduce(pm[:], top8[:, :, 0:2].rearrange("p t k -> p k t"), X,
                                                ALU.max).then_inc(pm_ready, 1)
                        for t in range(T):
                            i = nc.vector.max_index(idx8[:, t, :], top8[:, t, :], lg[:, t, :])
                        link(i)
                        nc.vector.tensor_copy(idxf[:], idx8[:, :, 0:2])
                    elif u == 1:
                        dve.wait_ge(pm_psum, n + 1)
                        link(nc.vector.tensor_reduce(gm[:], ps[0:2, 0, 0:P], X, ALU.max))
                        nc.vector.tensor_scalar(dg[:], const[0:2, C_ID:C_ID + 2], gm[:], None, ALU.mult).then_inc(dg_ready, 1)
                    elif u == 2:
                        dve.wait_ge(mx_psum, n + 1)
                        nc.vector.tensor_scalar(nm1[:], ps[:, 0, 0:2], -1.0, None, ALU.mult).then_inc(nm1_ready, 1)
                    elif u == 3:
                        dve.wait_ge(tot_psum, n + 1)
                        link(nc.vector.reciprocal(rtot[:], ps[:, 0, 0:2]))
                        link(nc.vector.scalar_tensor_tensor(out=gk[:], in0=ek[:], scalar=0.5,
                                                            in1=rtot[:].unsqueeze(2).to_broadcast([P, 2, T]),
                                                            op0=ALU.mult, op1=ALU.mult))
                        two_hot(heavy, ga, gb, lambda t, k: gk[:, k, t:t + 1], E)
                        link(nc.vector.tensor_tensor(g[:], ga[:], gb[:], ALU.add))
                        link(nc.vector.tensor_copy(gR[:], g[:]))
                        nc.vector.tensor_copy(gs[:, :, 0:E], gR[:].bitcast(F32))
                        nc.vector.tensor_tensor(gs[:, :, GS - E:GS], g[:], gR[:].bitcast(F32),
                                                ALU.subtract).then_inc(gs_ready, 1)
                    elif u == 5:
                        dve.wait_ge(b2_psum, n + 1)
                        link(nc.vector.tensor_copy(accT[:], ps[:, 0, :]))

                for u in range(2 * E + 3):
                    route(u)
                    g_e = gated_expert(u)
                    if g_e is not None:
                        dve.wait_ge(gb_ready, E * n + g_e + 1)
                        dve.wait_ge(my_psum, E * n + g_e + 1)
                        i = nc.vector.tensor_tensor(prod[:], ps[:, 3 + g_e % 2, :], gbs[:], ALU.mult)
                        i.then_inc(my_used, 1)
                        dve.wait_ge(my_used, E * n + g_e + 1)
                        i = nc.vector.tensor_tensor(accT[:], accT[:], prod[:], ALU.add)
                        if g_e < E - 1:
                            link(i)
                        else:
                            i.then_inc(acc_ready, 1)
                    yield
                dve.wait_ge(acc_psum, n + 1)
                if r == 0:
                    dve.wait_ge(xh_copied, b + 1)
                    nc.vector.tensor_tensor(flat(xh), ps[:, 0, :], flat(xh), ALU.add).then_inc(xh_ready, 1)
                else:
                    dve.wait_ge(x_out, 16 * b + 16)
                    nc.vector.tensor_tensor(flat(xout), ps[:, 0, :], flat(xh), ALU.add).then_inc(xout_ready, 1)
                yield

            def mla(b):
                dve.wait_ge(xh_ready, 2 * b + 1)
                yield from layernorm(heavy, 3 * b + 1, xh)
                yield
                dve.wait_ge(cq_psum, b + 1)
                link(nc.vector.tensor_scalar(cqT, ps[0:3 * DC, 1, :], cols[0:3 * DC, COL_AT["bdq"]:COL_AT["bdq"] + 1],
                                             None, ALU.add))
                link(nc.vector.tensor_copy(cqR, cqT))
                nc.vector.scalar_tensor_tensor(out=cqs[0:3 * DC], in0=cqR.bitcast(F32),
                                               scalar=cols[0:3 * DC, COL_AT["qlow"]:COL_AT["qlow"] + 1], in1=cqT,
                                               op0=ALU.mult, op1=ALU.add).then_inc(cq_ready, 1)
                dve.wait_ge(ckt_psum, b + 1)
                nc.vector.tensor_tensor(ckt[:], ps[:, 3, 0:T * DC].rearrange("p (t n) -> p t n", t=T),
                                        over_tiles(row("bdkv"), DC), ALU.add).then_inc(ckt_ready, 1)
                yield

                def key_stack(h):
                    dve.wait_ge(kR_ready, H1 * b + h + 1)
                    nc.vector.scalar_tensor_tensor(out=ks[:, h % 2, :], in0=kR.bitcast(F32),
                                                   scalar=cols[0:KS, COL_AT["klow"]:COL_AT["klow"] + 1],
                                                   in1=ps[0:KS, 0, :], op0=ALU.mult, op1=ALU.add).then_inc(ks_ready, 1)

                def row_max(h, t):
                    n = h * T + t
                    dve.wait_ge(s_psum, H1 * T * b + n + 1)
                    nc.vector.tensor_reduce(nm[:, h, t:t + 1], ps[:, 1 + n % 2, :], X, ALU.max,
                                            negate=True).then_inc(nm_ready, 1)

                def row_sum(h):
                    dve.wait_ge(p_ready, H1 * T * b + (h + 1) * T)
                    nc.vector.reciprocal(rrow[:, h, :], rowsum[:, h, :]).then_inc(rrow_ready, 1)

                def turned(h, k):
                    dve.wait_ge(PT_psum, H1 * T * b + h * T + k + 1)
                    if k == 0 and h >= 2:
                        dve.wait_ge(pv_psum, H1 * b + h - 1)
                    nc.vector.tensor_copy(PT[:, h % 2, k, :], ps[:, 3, :]).then_inc(PTv_ready, 1)

                key_stack(0)
                yield
                for h in range(H1 + 3):
                    for t in range(T):
                        if t == 0 and 1 <= h <= H1:
                            row_sum(h - 1)
                        if t % 2 == 0 and 2 <= h < H1 + 2:
                            turned(h - 2, t)
                        if h < H1:
                            row_max(h, t)
                        if t == 0 and h + 1 < H1:
                            key_stack(h + 1)
                        yield
                dve.wait_ge(mo_psum, b + 1)
                dve.wait_ge(bO_ready, b + 1)
                nc.vector.tensor_tensor(flat(xh), ps[:, 0, :], flat(xh), ALU.add).then_inc(xh_ready, 1)
                yield

            def light_lane(b, first=False):
                yield from proto_experts(b, 0, first)
                yield from nsa(b)
                yield from proto_route(b, 1)
                yield from proto_experts(b, 1)
                yield from proto_route(b + 1, 0)

            def heavy_lane(b):
                yield from moe(b, 0)
                yield from mla(b)
                yield from moe(b, 1)

            light_setup()
            for _ in proto_route(0, 0):
                pass
            for k, _ in enumerate(light_lane(0, first=True)):
                if k == SETUP_AT:
                    heavy_setup()
            with nc.vector.Fori(0, NB - 1) as b:
                nc.vector.sem_clear(v_chain)
                chained[0] = 0
                both_lanes(heavy_lane(b), light_lane(b + 1))
            nc.vector.sem_clear(v_chain)
            chained[0] = 0
            for _ in heavy_lane(NB - 1):
                pass


def lay_out(i):
    def f(name):
        return np.asarray(i[name])

    def t(a):
        return np.ascontiguousarray(a)

    wqkv = f("L0_attn_w_qkv").reshape(H0, 3, HD0, D)
    bqkv = f("L0_attn_b_qkv").reshape(H0, 3, HD0).transpose(1, 0, 2).reshape(3, D)
    buq = f("L1_attn_b_UQ").reshape(H1, DK)
    bukh = f("L1_attn_b_UK").reshape(H1, DK)
    parts = {"bv": bqkv[2], "bg": f("L0_attn_b_gate"), "bo": f("L0_attn_b_o"), "gb": f("L1_ffn_gate_b"),
             "bdkv": f("L1_attn_b_DKV"), "bO": f("L1_attn_b_O"), "bs": f("L0_attn_b_score"),
             "temp": f("L0_ffn_temp").reshape(1)}
    cols = np.zeros((P, NCOLS), np.float32)

    def put(name, a):
        cols[:a.shape[0], COL_AT[name]:COL_AT[name] + a.shape[1]] = a

    put("bq", bqkv[0][:, None])
    put("bk", bqkv[1][:, None])
    put("bvc", bqkv[2][:, None])
    put("bcomp", f("L0_attn_b_comp")[:, None])
    put("b1", f("L1_ffn_b1").reshape(E * FC, P).T)
    put("buv", f("L1_attn_b_UV").reshape(H1, DK).T)
    put("bkr", np.concatenate([f("L1_attn_b_DKV"), f("L1_attn_b_KR")])[:, None])
    put("bdq", np.concatenate([f("L1_attn_b_DQ")] * 3)[:, None])
    cols[DC:2 * DC, COL_AT["qlow"]] = -1
    cols[2 * DC:3 * DC, COL_AT["klow"]] = -1
    cols[KS - 1, COL_AT["klow"]] = -1
    put("ws", f("L0_attn_w_score").T)
    b2 = np.zeros((GS, D), np.float32)
    b2[0:E] = b2[GS - E:GS] = f("L1_ffn_b2")
    wuq = np.concatenate([f("L1_attn_W_UQ").reshape(DC, H1, DK), buq[None]], 0)
    wuk = np.concatenate([f("L1_attn_W_UK").reshape(DC, H1, DK), bukh[None]], 0)
    return {
        "x": t(f("L0_attn_x")),
        "const": constants(),
        "rows": t(np.concatenate([parts[n] for n, _ in ROWS])),
        "cols": cols,
        "proto": t(f("L0_ffn_prototypes").T),
        "pB": t(f("L0_ffn_B").reshape(NPROTO * RANK, D).T),
        "pA": t(f("L0_ffn_A").transpose(0, 2, 1).reshape(PR, P, D).transpose(1, 0, 2)),
        "pbias": t(f("L0_ffn_bias")),
        "wqkv": t(wqkv.transpose(3, 1, 0, 2).reshape(D, 3, D)),
        "wgate": t(f("L0_attn_w_gate").T),
        "wo": t(f("L0_attn_w_o").T),
        "wcomp": t(f("L0_attn_w_comp").reshape(D, CBS, D).transpose(2, 1, 0)),
        "wdq": t(np.stack([f("L1_attn_W_DQ")] * 3, 1)),
        "wkvr": t(np.concatenate([f("L1_attn_W_DKV"), f("L1_attn_W_KR")], 1)),
        "uq": t(wuq.transpose(2, 1, 0)),
        "uk": t(wuk.transpose(2, 1, 0)),
        "uv": t(f("L1_attn_W_UV").reshape(DC, H1, DK).transpose(2, 1, 0)),
        "wO": t(f("L1_attn_W_O").reshape(H1, DK, D).transpose(1, 0, 2)),
        "qr": t(np.concatenate([f("L1_attn_W_QR"), f("L1_attn_b_QR")[None]], 0).reshape(KQ, H1, DR).transpose(2, 1, 0)),
        "gatew": t(f("L1_ffn_gate_w").T),
        "w1": t(f("L1_ffn_w1").transpose(2, 0, 1)),
        "w2": t(f("L1_ffn_w2").reshape(E, D, FC, P).transpose(3, 0, 2, 1)),
        "b2": b2,
    }


def kernel(**inputs):
    import concourse.bacc as _bacc
    from concourse.bass_utils import run_bass_kernel_spmd as _run

    nc = _bacc.Bacc("TRN2", target_bir_lowering=False, num_devices=1)
    arrays = {f"in_{k}_dram": a for k, a in lay_out(inputs).items()}
    dram = {k[3:-5]: nc.dram_tensor(k, a.shape, mybir.dt.from_np(a.dtype), kind="ExternalInput").ap()
            for k, a in arrays.items()}
    out = nc.dram_tensor("out_0_dram", (NB, S, D), F32, kind="ExternalOutput").ap()
    build(nc, dram, out)
    r = _run(nc, [arrays], core_ids=[0])
    return r.results[0]["out_0_dram"]
```
